# Optimizing a Trainium2 kernel written in Bass

```python
import numpy as np
import jax
import jax.numpy as jnp

def _softmax(x, axis=-1):
    return jax.nn.softmax(x, axis=axis)

def _gelu(x):
    return jax.nn.gelu(x, approximate=True)

def _silu(x):
    return jax.nn.silu(x)

def _sigmoid(x):
    return jax.nn.sigmoid(x)

def _layernorm(x, axis=-1, eps=1e-05):
    m = jnp.mean(x, axis=axis, keepdims=True)
    v = jnp.var(x, axis=axis, keepdims=True)
    return (x - m) / jnp.sqrt(v + eps)

def _scatter_add(tgt, idx, src, axis=0):
    return tgt.at[idx].add(src)

def _segment_sum(src, seg, n):
    return jax.ops.segment_sum(src, seg, n)
kernel_name = 'mk_adaln_d2_jaxref_r4_a1eb0f'

def setup_inputs(seed: int=0):
    np.random.seed(seed)
    _w = jnp.asarray

    def _L0_attn_setup():
        import math
        import jax, jax.numpy as jnp
        import numpy as np
        B, T, C = (2, 512, 256)
        HEADS = 16
        HD = C // HEADS

        def _rope_tables(seq_len, dim):
            pos = jnp.arange(seq_len, dtype=jnp.float32)
            freqs = 1.0 / 10000.0 ** (jnp.arange(0, dim, 2, dtype=jnp.float32) / dim)
            ang = pos[:, None] * freqs[None, :]
            return (jnp.sin(ang)[None, :, None, :], jnp.cos(ang)[None, :, None, :])

        def _apply_rope(t, sin, cos, dim):
            t1, t2 = (t[..., :dim // 2], t[..., dim // 2:])
            return jnp.concatenate([t1 * cos + t2 * sin, t1 * sin - t2 * cos], axis=-1)
        key = jax.random.key(seed)
        ks = jax.random.split(key, 5)
        s = 0.02
        return {'x': jax.random.normal(ks[0], (B, T, C), jnp.float32), 'Wq': jax.random.normal(ks[1], (C, C), jnp.float32) * s, 'bq': jnp.zeros((C,), jnp.float32), 'Wk': jax.random.normal(ks[2], (C, HD), jnp.float32) * s, 'bk': jnp.zeros((HD,), jnp.float32), 'Wv': jax.random.normal(ks[3], (C, HD), jnp.float32) * s, 'bv': jnp.zeros((HD,), jnp.float32), 'Wo': jax.random.normal(ks[4], (C, C), jnp.float32) * s, 'bo': jnp.zeros((C,), jnp.float32)}
    _L0_attn_in = _L0_attn_setup()

    def _L0_ffn_setup():
        import jax, jax.numpy as jnp
        import numpy as np
        K = 64
        key = jax.random.key(seed)
        ks = jax.random.split(key, 9)
        B, S, D, O, E = (8, 512, 256, 256, 16)

        def xavier(k_, shape):
            fan_in, fan_out = (shape[-2], shape[-1])
            lim = (6.0 / (fan_in + fan_out)) ** 0.5
            return jax.random.uniform(k_, shape, jnp.float32, -lim, lim)
        return {'x': jax.random.normal(ks[0], (B, S, D), jnp.float32), 'Wg': xavier(ks[1], (D, E)), 'bg': jnp.zeros((E,), jnp.float32), 'w1': xavier(ks[2], (E, D, O)), 'b1': xavier(ks[3], (E, 1)), 'w2': xavier(ks[4], (E, O, O)), 'b2': xavier(ks[5], (E, 1)), 'w3': xavier(ks[6], (E, O, O)), 'b3': xavier(ks[7], (E, 1))}
    _L0_ffn_in = _L0_ffn_setup()
    _L0_c = _w((lambda *s: np.random.randn(*s).astype(np.float32) * 0.05)(8, 256))
    _L0_wmod = _w((lambda *s: np.random.randn(*s).astype(np.float32) * 0.05)(256, 6 * 256) * 256 ** (-0.5))

    def _L1_attn_setup():
        import jax, jax.numpy as jnp
        import numpy as np
        B, L, E, H = (1, 1024, 256, 16)
        D = E // H
        EPS = 1e-06
        key = jax.random.key(seed)
        k1, k2, k3 = jax.random.split(key, 3)
        x = jax.random.normal(k1, (B, L, E), dtype=jnp.float32)
        qkv_w = jax.random.normal(k2, (E, 3 * E), dtype=jnp.float32) / np.sqrt(E)
        qkv_b = jnp.zeros((3 * E,), dtype=jnp.float32)
        out_w = jax.random.normal(k3, (E, E), dtype=jnp.float32) / np.sqrt(E)
        out_b = jnp.zeros((E,), dtype=jnp.float32)
        return {'x': x, 'qkv_w': qkv_w, 'qkv_b': qkv_b, 'out_w': out_w, 'out_b': out_b}
    _L1_attn_in = _L1_attn_setup()

    def _L1_ffn_setup():
        import jax, jax.numpy as jnp
        import numpy as np
        B, S, DIM = (4, 1024, 256)
        BASE_COUPLING = 0.1
        NUM_CYCLES = 3

        def _gelu(x):
            return jax.nn.gelu(x, approximate=False)

        def _coupling_net(h, w1, b1, w2, b2, w3, b3, w4, b4):
            h = _gelu(h @ w1 + b1)
            h = _gelu(h @ w2 + b2)
            h = _gelu(h @ w3 + b3)
            return jax.nn.sigmoid(h @ w4 + b4)

        def _global_net(h, w1, b1, w2, b2, w3, b3):
            h = _gelu(h @ w1 + b1)
            h = _gelu(h @ w2 + b2)
            return jax.nn.sigmoid(h @ w3 + b3)

        def _twist(x):
            o_r, o_i, p_r, p_i = jnp.split(x, 4, axis=-1)
            return jnp.concatenate([p_r, -p_i, -o_r, o_i], axis=-1)
        key = jax.random.key(seed)
        ks = jax.random.split(key, 9)
        d = DIM

        def w(k, fan_in, fan_out):
            return jax.random.normal(k, (fan_in, fan_out), dtype=jnp.float32) / np.sqrt(fan_in).astype(np.float32)
        inp = {'x': jax.random.normal(ks[0], (B, S, d), dtype=jnp.float32)}
        cn_dims = [(d, d), (d, d // 2), (d // 2, d // 4), (d // 4, 1)]
        for i, (a, b) in enumerate(cn_dims):
            inp[f'cn_w{i + 1}'] = w(ks[1 + i], a, b)
            inp[f'cn_b{i + 1}'] = jnp.zeros((b,), dtype=jnp.float32)
        gc_dims = [(d, d // 2), (d // 2, d // 4), (d // 4, 1)]
        for i, (a, b) in enumerate(gc_dims):
            inp[f'gc_w{i + 1}'] = w(ks[5 + i], a, b)
            inp[f'gc_b{i + 1}'] = jnp.zeros((b,), dtype=jnp.float32)
        inp['adaptive_range'] = jnp.full((1,), 0.2, dtype=jnp.float32)
        return inp
    _L1_ffn_in = _L1_ffn_setup()
    _L1_c = _w((lambda *s: np.random.randn(*s).astype(np.float32) * 0.05)(8, 256))
    _L1_wmod = _w((lambda *s: np.random.randn(*s).astype(np.float32) * 0.05)(256, 6 * 256) * 256 ** (-0.5))
    _d = {'L0_attn_x': _L0_attn_in['x'], 'L0_attn_Wq': _L0_attn_in['Wq'], 'L0_attn_bq': _L0_attn_in['bq'], 'L0_attn_Wk': _L0_attn_in['Wk'], 'L0_attn_bk': _L0_attn_in['bk'], 'L0_attn_Wv': _L0_attn_in['Wv'], 'L0_attn_bv': _L0_attn_in['bv'], 'L0_attn_Wo': _L0_attn_in['Wo'], 'L0_attn_bo': _L0_attn_in['bo'], 'L0_ffn_Wg': _L0_ffn_in['Wg'], 'L0_ffn_bg': _L0_ffn_in['bg'], 'L0_ffn_w1': _L0_ffn_in['w1'], 'L0_ffn_b1': _L0_ffn_in['b1'], 'L0_ffn_w2': _L0_ffn_in['w2'], 'L0_ffn_b2': _L0_ffn_in['b2'], 'L0_ffn_w3': _L0_ffn_in['w3'], 'L0_ffn_b3': _L0_ffn_in['b3'], 'L0_c': _L0_c, 'L0_wmod': _L0_wmod, 'L1_attn_qkv_w': _L1_attn_in['qkv_w'], 'L1_attn_qkv_b': _L1_attn_in['qkv_b'], 'L1_attn_out_w': _L1_attn_in['out_w'], 'L1_attn_out_b': _L1_attn_in['out_b'], 'L1_ffn_cn_w1': _L1_ffn_in['cn_w1'], 'L1_ffn_cn_b1': _L1_ffn_in['cn_b1'], 'L1_ffn_cn_w2': _L1_ffn_in['cn_w2'], 'L1_ffn_cn_b2': _L1_ffn_in['cn_b2'], 'L1_ffn_cn_w3': _L1_ffn_in['cn_w3'], 'L1_ffn_cn_b3': _L1_ffn_in['cn_b3'], 'L1_ffn_cn_w4': _L1_ffn_in['cn_w4'], 'L1_ffn_cn_b4': _L1_ffn_in['cn_b4'], 'L1_ffn_gc_w1': _L1_ffn_in['gc_w1'], 'L1_ffn_gc_b1': _L1_ffn_in['gc_b1'], 'L1_ffn_gc_w2': _L1_ffn_in['gc_w2'], 'L1_ffn_gc_b2': _L1_ffn_in['gc_b2'], 'L1_ffn_gc_w3': _L1_ffn_in['gc_w3'], 'L1_ffn_gc_b3': _L1_ffn_in['gc_b3'], 'L1_ffn_adaptive_range': _L1_ffn_in['adaptive_range'], 'L1_c': _L1_c, 'L1_wmod': _L1_wmod}
    _x0 = _d['L0_attn_x']
    _d['L0_attn_x'] = jax.random.normal(jax.random.fold_in(jax.random.key(seed), 1), (8, 512, 256), dtype=_x0.dtype)
    del _x0
    return _d

def reference(L0_attn_x, L0_attn_Wq, L0_attn_bq, L0_attn_Wk, L0_attn_bk, L0_attn_Wv, L0_attn_bv, L0_attn_Wo, L0_attn_bo, L0_ffn_Wg, L0_ffn_bg, L0_ffn_w1, L0_ffn_b1, L0_ffn_w2, L0_ffn_b2, L0_ffn_w3, L0_ffn_b3, L0_c, L0_wmod, L1_attn_qkv_w, L1_attn_qkv_b, L1_attn_out_w, L1_attn_out_b, L1_ffn_cn_w1, L1_ffn_cn_b1, L1_ffn_cn_w2, L1_ffn_cn_b2, L1_ffn_cn_w3, L1_ffn_cn_b3, L1_ffn_cn_w4, L1_ffn_cn_b4, L1_ffn_gc_w1, L1_ffn_gc_b1, L1_ffn_gc_w2, L1_ffn_gc_b2, L1_ffn_gc_w3, L1_ffn_gc_b3, L1_ffn_adaptive_range, L1_c, L1_wmod):

    def _L0_attn_ref(x, Wq, bq, Wk, bk, Wv, bv, Wo, bo):
        import math
        import jax, jax.numpy as jnp
        import numpy as np
        B, T, C = (2, 512, 256)
        HEADS = 16
        HD = C // HEADS

        def _rope_tables(seq_len, dim):
            pos = jnp.arange(seq_len, dtype=jnp.float32)
            freqs = 1.0 / 10000.0 ** (jnp.arange(0, dim, 2, dtype=jnp.float32) / dim)
            ang = pos[:, None] * freqs[None, :]
            return (jnp.sin(ang)[None, :, None, :], jnp.cos(ang)[None, :, None, :])

        def _apply_rope(t, sin, cos, dim):
            t1, t2 = (t[..., :dim // 2], t[..., dim // 2:])
            return jnp.concatenate([t1 * cos + t2 * sin, t1 * sin - t2 * cos], axis=-1)
        Bx, Tx, Cx = x.shape
        q = (x @ Wq + bq).reshape(Bx, Tx, HEADS, HD)
        k = (x @ Wk + bk)[:, :, None, :]
        v = (x @ Wv + bv)[:, :, None, :]
        sin, cos = _rope_tables(Tx, HD)
        q = _apply_rope(q, sin, cos, HD)
        k = _apply_rope(k, sin, cos, HD)
        att = jnp.einsum('bthd,bThd->bhtT', q, k) / math.sqrt(HD)
        causal = jnp.triu(jnp.ones((Tx, Tx), bool), 1)
        att = jnp.where(causal, -jnp.inf, att)
        att = jax.nn.softmax(att, axis=-1)
        out = jnp.einsum('bhtT,bThd->bthd', att, v).reshape(Bx, Tx, Cx)
        return out @ Wo + bo

    def _L0_ffn_ref(x, Wg, bg, w1, b1, w2, b2, w3, b3):
        import jax, jax.numpy as jnp
        import numpy as np
        K = 64
        B, S, D = x.shape
        E, _, O = w1.shape
        logits = jnp.einsum('bsd,de->bse', x, Wg) + bg
        probs = jax.nn.softmax(logits, axis=-2)
        pv = jnp.transpose(probs, (0, 2, 1))
        vals, idx = jax.lax.top_k(pv, K)
        bidx = jnp.arange(B)[:, None, None]
        tok = x[bidx, idx]
        b1b = b1[None, :, None, :]
        b2b = b2[None, :, None, :]
        b3b = b3[None, :, None, :]
        h = jax.nn.relu(jnp.einsum('bekd,edo->beko', tok, w1) + b1b)
        h = jax.nn.relu(jnp.einsum('bekd,edo->beko', h, w2) + b2b)
        h = jnp.einsum('bekd,edo->beko', h, w3) + b3b
        out = h * vals[..., None]
        outputs = jnp.zeros((B, S, O), x.dtype).at[bidx, idx].add(out)
        return outputs

    def _L1_attn_ref(x, qkv_w, qkv_b, out_w, out_b):
        import jax, jax.numpy as jnp
        import numpy as np
        B, L, E, H = (1, 1024, 256, 16)
        D = E // H
        EPS = 1e-06
        b, l, e = x.shape
        qkv = x @ qkv_w + qkv_b
        q, k, v = jnp.split(qkv, 3, axis=-1)
        q = q.reshape(b, l, H, D).transpose(0, 2, 1, 3)
        k = k.reshape(b, l, H, D).transpose(0, 2, 1, 3)
        v = v.reshape(b, l, H, D).transpose(0, 2, 1, 3)
        q_prime = jax.nn.elu(q) + 1.0
        k_prime = jax.nn.elu(k) + 1.0
        kv_prod = jnp.einsum('bhld,bhle->bhlde', k_prime, v)
        kv_cumsum = jnp.cumsum(kv_prod, axis=2)
        context = jnp.einsum('bhld,bhlde->bhle', q_prime, kv_cumsum)
        k_cumsum = jnp.cumsum(k_prime, axis=2)
        norm = jnp.einsum('bhld,bhld->bhl', q_prime, k_cumsum)
        output = context / (norm[..., None] + EPS)
        output = output.transpose(0, 2, 1, 3).reshape(b, l, e)
        return output @ out_w + out_b

    def _L1_ffn_ref(x, cn_w1, cn_b1, cn_w2, cn_b2, cn_w3, cn_b3, cn_w4, cn_b4, gc_w1, gc_b1, gc_w2, gc_b2, gc_w3, gc_b3, adaptive_range):
        import jax, jax.numpy as jnp
        import numpy as np
        B, S, DIM = (4, 1024, 256)
        BASE_COUPLING = 0.1
        NUM_CYCLES = 3

        def _gelu(x):
            return jax.nn.gelu(x, approximate=False)

        def _coupling_net(h, w1, b1, w2, b2, w3, b3, w4, b4):
            h = _gelu(h @ w1 + b1)
            h = _gelu(h @ w2 + b2)
            h = _gelu(h @ w3 + b3)
            return jax.nn.sigmoid(h @ w4 + b4)

        def _global_net(h, w1, b1, w2, b2, w3, b3):
            h = _gelu(h @ w1 + b1)
            h = _gelu(h @ w2 + b2)
            return jax.nn.sigmoid(h @ w3 + b3)

        def _twist(x):
            o_r, o_i, p_r, p_i = jnp.split(x, 4, axis=-1)
            return jnp.concatenate([p_r, -p_i, -o_r, o_i], axis=-1)
        global_context = x.mean(axis=1, keepdims=True)
        gf = _global_net(global_context, gc_w1, gc_b1, gc_w2, gc_b2, gc_w3, gc_b3)
        out = x
        for _ in range(NUM_CYCLES):
            tf = _coupling_net(out, cn_w1, cn_b1, cn_w2, cn_b2, cn_w3, cn_b3, cn_w4, cn_b4)
            combined = 0.7 * gf + 0.3 * tf
            coupling = BASE_COUPLING + adaptive_range * (combined - 0.5) * 2.0
            out = out + coupling * _twist(out)
        return out
    x = L0_attn_x
    mod = (_silu(L0_c) @ L0_wmod).reshape(L0_c.shape[0], 6, 1, -1)
    sa, ca, ga, sb, cb, gb = (mod[:, 0], mod[:, 1], mod[:, 2], mod[:, 3], mod[:, 4], mod[:, 5])
    ga = (2 * (ga >= 0) - 1) * jnp.maximum(jnp.abs(ga), 0.25)
    gb = (2 * (gb >= 0) - 1) * jnp.maximum(jnp.abs(gb), 0.25)
    h = _layernorm(x, axis=-1) * (1 + ca) + sa
    x = x + ga * _L0_attn_ref(h, L0_attn_Wq, L0_attn_bq, L0_attn_Wk, L0_attn_bk, L0_attn_Wv, L0_attn_bv, L0_attn_Wo, L0_attn_bo)
    h = _layernorm(x, axis=-1) * (1 + cb) + sb
    x = x + gb * _L0_ffn_ref(h, L0_ffn_Wg, L0_ffn_bg, L0_ffn_w1, L0_ffn_b1, L0_ffn_w2, L0_ffn_b2, L0_ffn_w3, L0_ffn_b3)
    mod = (_silu(L1_c) @ L1_wmod).reshape(L1_c.shape[0], 6, 1, -1)
    sa, ca, ga, sb, cb, gb = (mod[:, 0], mod[:, 1], mod[:, 2], mod[:, 3], mod[:, 4], mod[:, 5])
    ga = (2 * (ga >= 0) - 1) * jnp.maximum(jnp.abs(ga), 0.25)
    gb = (2 * (gb >= 0) - 1) * jnp.maximum(jnp.abs(gb), 0.25)
    h = _layernorm(x, axis=-1) * (1 + ca) + sa
    x = x + ga * _L1_attn_ref(h, L1_attn_qkv_w, L1_attn_qkv_b, L1_attn_out_w, L1_attn_out_b)
    h = _layernorm(x, axis=-1) * (1 + cb) + sb
    x = x + gb * _L1_ffn_ref(h, L1_ffn_cn_w1, L1_ffn_cn_b1, L1_ffn_cn_w2, L1_ffn_cn_b2, L1_ffn_cn_w3, L1_ffn_cn_b3, L1_ffn_cn_w4, L1_ffn_cn_b4, L1_ffn_gc_w1, L1_ffn_gc_b1, L1_ffn_gc_w2, L1_ffn_gc_b2, L1_ffn_gc_w3, L1_ffn_gc_b3, L1_ffn_adaptive_range)
    return x

_drawn_inputs = setup_inputs


def setup_inputs(seed=0):
    import zlib

    import numpy as np

    out = dict(_drawn_inputs(seed))
    spreads = {'L0_attn_bq': (0.0, 0.8),
     'L0_attn_bk': (0.0, 0.8),
     'L0_attn_bv': (0.0, 0.8),
     'L0_attn_bo': (0.0, 0.327),
     'L0_ffn_bg': (0.0, 2.0),
     'L1_attn_qkv_b': (0.0, 0.8),
     'L1_attn_out_b': (0.0, 2.0),
     'L1_ffn_cn_b1': (0.0, 2.0),
     'L1_ffn_cn_b2': (0.0, 2.0),
     'L1_ffn_cn_b3': (0.0, 2.0),
     'L1_ffn_gc_b1': (0.0, 2.0),
     'L1_ffn_gc_b2': (0.0, 0.8)}
    factors = {'L0_attn_Wq': 8.0,
     'L0_attn_Wk': 8.0,
     'L0_attn_Wv': 8.0,
     'L0_attn_Wo': 5.451,
     'L0_ffn_Wg': 8.0,
     'L0_ffn_w1': 8.0,
     'L0_ffn_b1': 8.0,
     'L0_ffn_w2': 8.0,
     'L0_ffn_b2': 8.0,
     'L0_ffn_w3': 8.0,
     'L0_ffn_b3': 54.802,
     'L1_ffn_cn_w1': 64.0,
     'L1_ffn_cn_w2': 64.0,
     'L1_ffn_cn_w3': 64.0,
     'L1_ffn_cn_w4': 64.0,
     'L1_ffn_gc_w1': 8.0,
     'L1_ffn_gc_w2': 64.0,
     'L1_ffn_gc_w3': 39.095,
     'L1_attn_qkv_w': 7.854,
     'L1_attn_out_w': 7.251}
    for name, (base, spread) in spreads.items():
        noise = np.random.default_rng([zlib.crc32(name.encode()), seed]).standard_normal(out[name].shape)
        drawn = base * np.exp(spread * noise) if base else spread * noise
        out[name] = jnp.asarray(drawn.astype(out[name].dtype))
    for name, factor in factors.items():
        out[name] = (out[name] * factor).astype(out[name].dtype)
    return out
```

```python
from contextlib import ExitStack

import numpy as np
import concourse.bass as bass
from concourse import mybir

F32 = mybir.dt.float32
BF16 = mybir.dt.bfloat16
U32 = mybir.dt.uint32
ALU = mybir.AluOpType
ACT = mybir.ActivationFunctionType
AX_X = mybir.AxisListType.X

P = 128
B, T, C = 8, 512, 256
NT = T // P
KC = C // P
H, HD = 16, 16
E, TOPK = 16, 64
EPS = 1e-5
NEG = -1e30
HG = 4
CAUSAL0 = 0
C_IDENT, C_NEGS, C_NEGT, C_KEEP, C_BD, C_SEQ, C_SGN, C_PARITY, C_ROPE = 0, 128, 256, 384, 512, 768, 769, 770, 772
C_END = C_ROPE + NT * 2 * HD


def shape_constants():
    c = np.zeros((P, C_END), np.float32)
    i = np.arange(P)
    c[:, C_IDENT:C_IDENT + P] = np.eye(P)
    c[:, C_NEGS:C_NEGS + P] = np.where(i[None, :] > i[:, None], NEG, 0)
    c[:, C_NEGT:C_NEGT + P] = np.where(i[None, :] < i[:, None], NEG, 0)
    c[:, C_KEEP:C_KEEP + P] = (i[None, :] >= i[:, None])
    col = np.arange(256)
    c[:, C_BD:C_BD + 256] = (i[:, None] // HD == col[None, :] // 32) & (col[None, :] % 32 <= HD)
    c[:, C_SEQ] = (i // E) * T
    c[:, C_SGN] = np.where(i < P // 2, 1, -1)
    c[:, C_PARITY] = i // HD % 2 == 0
    c[:, C_PARITY + 1] = i // HD % 2 == 1
    pos = np.arange(T, dtype=np.float32)
    freqs = (np.float32(1.0) / np.float32(10000.0) ** (np.arange(0, HD, 2, dtype=np.float32) / np.float32(HD)))
    ang = (pos[:, None] * freqs[None, :].astype(np.float32)).astype(np.float32)
    sin, cos = np.sin(ang), np.cos(ang)
    rope = np.concatenate([cos, -cos, sin, sin], axis=1).reshape(NT, P, 2 * HD)
    c[:, C_ROPE:] = rope.transpose(1, 0, 2).reshape(P, -1)
    return c


class Seq:

    def __init__(self, it, s):
        self.it, self.s, self.n = it, s, it * 2 + s

    def next(self):
        return Seq(self.it, 1) if self.s == 0 else Seq(self.it + 1, 0)


class Signal:

    def __init__(self, sem, per):
        self.sem, self.per = sem, per

    def done(self, q, n):
        return q.n * self.per + 2 * self.per + n

    def before(self, q, n, back=1):
        return q.n * self.per + (2 - back) * self.per + n


def settle(eng, passed):
    eng.sem_inc(passed, 1)


class Chain:

    def __init__(self, eng, signal, passed):
        self.eng, self.counter, self.passed, self.q, self.n = eng, signal, passed, None, 0

    def start(self, q):
        self.q, self.n = q, 0

    def link(self, ins):
        self.n += 1
        ins.then_inc(self.counter.sem, 1)
        self.eng.wait_ge(self.counter.sem, self.counter.done(self.q, self.n))
        settle(self.eng, self.passed)

    def end(self):
        assert self.n == self.counter.per, (self.n, self.counter.per)


S_HEADS = [4, 2, 1, 1]


def prologue_order():
    order = [("ln",), ("hT", 0), ("hT", 1)] + [("qkv", i) for i in range(NT)] + [("kT",)]
    for i in range(NT):
        order += [("qT", i, 0), ("qT", i, 1)]
    return order


def mix(a, b, start=0.0, end=1.0):
    out, n = [], 0
    for k, s in enumerate(a):
        out.append(s)
        while n < len(b) and len(a) * (start + (end - start) * (n + 1) / (len(b) + 1)) <= k + 1:
            out.append(b[n])
            n += 1
    return out + b[n:]


def scores_order(i):
    return [("S", i, u) for u in range(H // S_HEADS[i])]


def probs_order(i):
    steps = []
    for j in range(i + 1):
        steps += [("ST", i, j, g) for g in range(HG)]
        if j:
            steps.append(("PV", i, j - 1))
    return steps + [("PV", i, i)]


def tail_order(i):
    return [("oE", i), ("oT", i), ("oC", i), ("pr", i), ("h2T", i)]


def attention_order():
    order = scores_order(0) + [("mT", 0)] + scores_order(1) + [("mT", 1)]
    order += mix(scores_order(2), probs_order(0)) + [("mT", 2)]
    order += mix(mix(scores_order(3), probs_order(1)), tail_order(0)) + [("mT", 3)]
    order += mix(probs_order(2), tail_order(1)) + mix(probs_order(3), tail_order(2))
    return order + tail_order(3) + [("lg",)]


def index_of(order, kinds):
    steps = [s for s in order if s[0] in kinds]
    return {s: n for n, s in enumerate(steps)}, len(steps)


def setup_phase(nc, m):
    with ExitStack() as ctx:
        def sb(name, shape, dt=F32):
            return ctx.enter_context(nc.sbuf_tensor(name, shape, dt))

        def sem(name):
            return ctx.enter_context(nc.semaphore(name))

        cT = sb("cT", [P, 2, KC, B])
        wmod = sb("wmod", [P, 2, KC, 6 * C])
        eneg = sb("eneg", [P, 2, KC, B])
        silu = sb("silu", [P, 2, KC, B])
        rows = sb("rows", [B, 2, 6 * C])
        rtmp = sb("rtmp", [B, 2, 2, 2, C])
        ctmp = sb("ctmp", [P, 2, 2, 2, KC, B])
        ps_row = m.psum[:, 0:6, :]
        ps_col = m.psum[:, 6, 0:2 * 12 * B]
        loaded = sem("setup_loaded")
        exp_done = sem("setup_exp_done")
        silu_ready = sem("silu_ready")
        rows_ready = sem("mod_rows_psum")
        cols_ready = sem("mod_cols_psum")
        chain = sem("setup_vector_steps")
        rows_final = sem("mod_rows_final")
        stored = sem("mod_rows_stored")

        with nc.Block() as block:
            @block.sync
            def _(sp):
                sp.dma_start(m.const[:], m.d["const"]).then_inc(loaded, 16)
                sp.dma_start(cT[:], m.d["cT"]).then_inc(loaded, 16)
                sp.dma_start(wmod[:], m.d["wmod"]).then_inc(loaded, 16)
                sp.wait_ge(rows_final, 1)
                sp.dma_start(m.mod_rows.rearrange("l b n -> b l n"), rows[:]).then_inc(stored, 16)
                sp.wait_ge(stored, 16)

            @block.gpsimd
            def _(pool):
                for signal in m.primed:
                    pool.sem_inc(signal.sem, 2 * signal.per)

            @block.scalar
            def _(act):
                act.wait_ge(loaded, 48)
                act.activation(eneg[:], cT[:], ACT.Exp, scale=-1.0).then_inc(exp_done, 1)

            @block.tensor
            def _(pe):
                pe.wait_ge(silu_ready, 1)
                for l in range(2):
                    for n in range(3):
                        for k in range(KC):
                            last = pe.matmul(ps_row[0:B, 3 * l + n, :], silu[:, l, k, :],
                                             wmod[:, l, k, n * 512:(n + 1) * 512],
                                             start=k == 0, stop=k == KC - 1)
                last.then_inc(rows_ready, 1)
                for l in range(2):
                    for j in range(12):
                        for k in range(KC):
                            last = pe.matmul(ps_col[:, (12 * l + j) * B:(12 * l + j + 1) * B],
                                             wmod[:, l, k, j * P:(j + 1) * P], silu[:, l, k, :],
                                             start=k == 0, stop=k == KC - 1)
                last.then_inc(cols_ready, 1)

            @block.vector
            def _(dve):
                count = [0]

                def link(ins):
                    count[0] += 1
                    ins.then_inc(chain, 1)
                    dve.wait_ge(chain, count[0])

                link(dve.memset(m.mhalf[:], -0.5))
                link(dve.memset(m.k6T[6 * HD:6 * HD + 3], 1.0))
                link(dve.memset(m.v32[:], 0.0))
                link(dve.memset(m.v32[:, :, :, HD:HD + 1], 1.0))
                dve.wait_ge(loaded, 48)
                link(dve.tensor_copy(m.ident_bf[:], m.const[:, C_IDENT:C_IDENT + P]))
                link(dve.tensor_copy(m.negs_bf[:], m.const[:, C_NEGS:C_NEGS + P]))
                link(dve.tensor_copy(m.negt_bf[:], m.const[:, C_NEGT:C_NEGT + P]))
                dve.wait_ge(exp_done, 1)
                link(dve.tensor_scalar(eneg[:], eneg[:], 1.0, None, ALU.add))
                link(dve.reciprocal(eneg[:], eneg[:]))
                dve.tensor_tensor(silu[:], cT[:], eneg[:], ALU.mult).then_inc(silu_ready, 1)
                dve.wait_ge(rows_ready, 1)
                link(dve.tensor_copy(rows[:].rearrange("b l n -> b (l n)"),
                                     ps_row[0:B].rearrange("b n f -> b (n f)")))
                dve.wait_ge(cols_ready, 1)
                link(dve.tensor_copy(m.modT[:].rearrange("p l j b -> p (l j b)"), ps_col))

                def finish(scale_of, gate_of, tmp):
                    link(dve.tensor_scalar(scale_of, scale_of, 1.0, None, ALU.add))
                    a, s = tmp
                    link(dve.scalar_tensor_tensor(out=a, in0=gate_of, scalar=-1.0, in1=gate_of,
                                                  op0=ALU.mult, op1=ALU.max))
                    link(dve.tensor_scalar(a, a, 0.25, None, ALU.max))
                    link(dve.tensor_scalar(s, gate_of, 0.0, 2.0, ALU.is_ge, ALU.mult))
                    link(dve.scalar_tensor_tensor(out=gate_of, in0=s, scalar=-1.0, in1=a,
                                                  op0=ALU.add, op1=ALU.mult))

                rv = rows[:].rearrange("b l (g v f) -> b l g v f", g=2, v=3)
                cv = m.modT[:].rearrange("p l (g v k) b -> p l g v k b", g=2, v=3)
                for l in range(2):
                    finish(rv[:, l, :, 1, :], rv[:, l, :, 2, :], (rtmp[:, 0, l], rtmp[:, 1, l]))
                    finish(cv[:, l, :, 1], cv[:, l, :, 2], (ctmp[:, 0, l], ctmp[:, 1, l]))
                dve.sem_inc(rows_final, 1)


ATT_ACT = ("mT", "oC", "h2T", "lg")
ATT_DVE = ("oT", "pr")
PRO_ACT = ("hT", "kT", "qT")
PRO_DVE = ("qkv",)


class AttentionSignals:

    def __init__(self, new):
        n = lambda order, kinds: index_of(order, kinds)[1]
        pro, att = prologue_order(), attention_order()
        self.stats = new("att_stats", NT)
        self.moments = new("att_moments", NT)
        self.cols = new("att_mod_cols", 1)
        self.pool_pro = new("att_pool_prologue_steps", 2 + 3 + 3 + 3 * NT)
        self.pool_att = new("att_pool_steps", 3 * NT + 4 * NT)
        self.dve_pro = new("att_vector_prologue_steps", 5 * NT)
        self.dve_att = new("att_vector_steps", 2 * NT)
        self.xn = new("att_xn_ready", NT)
        self.gated = new("att_gated_ready", 1)
        self.rope = new("att_rope_ready", NT)
        self.split = new("att_split_ready", NT)
        self.q6 = new("att_q6_ready", NT)
        self.pa_fill = new("att_prologue_act_bank_filled", n(pro, PRO_ACT))
        self.pa_drain = new("att_prologue_act_bank_drained", n(pro, PRO_ACT))
        self.pd_fill = new("att_prologue_vector_bank_filled", n(pro, PRO_DVE))
        self.pd_drain = new("att_prologue_vector_bank_drained", n(pro, PRO_DVE))
        self.aa_fill = new("att_act_bank_filled", n(att, ATT_ACT))
        self.aa_drain = new("att_act_bank_drained", n(att, ATT_ACT))
        self.ad_fill = new("att_vector_bank_filled", n(att, ATT_DVE))
        self.ad_drain = new("att_vector_bank_drained", n(att, ATT_DVE))
        self.s_fill = new("att_scores_filled", n(att, ("S",)))
        self.s_max = new("att_scores_maxed", n(att, ("S",)))
        self.msp = new("att_max_split", NT)
        self.t_fill = new("att_scoresT_filled", n(att, ("ST",)))
        self.probs = new("att_probs_ready", n(att, ("ST",)))
        self.pv = new("att_pv_done", n(att, ("PV",)))
        self.o_out = new("att_out_copied", NT)
        self.moments2 = new("att_moments2", NT)
        self.h2 = new("att_h2_ready", NT)
        self.x1_store = new("att_x1_stored", 16 * NT)
        self.h2_store = new("att_h2_stored", 16 * NT)
        self.lg_store = new("att_logits_stored", 16)


def attention_phase(nc, m):
    pro, att = prologue_order(), attention_order()
    merged = mix([(s, False) for s in att], [(s, True) for s in pro], 0.0, 0.85)
    pa_use, _ = index_of(pro, PRO_ACT)
    aa_use, n_aa = index_of(att, ATT_ACT)
    pd_use, _ = index_of(pro, PRO_DVE)
    ad_use, _ = index_of(att, ATT_DVE)
    s_use, n_s = index_of(att, ("S",))
    t_use, n_t = index_of(att, ("ST",))
    pv_use, n_pv = index_of(att, ("PV",))
    SR, TR, PR = 2, 3, 8
    assert n_s % SR == 0 and n_t % PR == 0
    g = m.att
    with ExitStack() as ctx:
        def sb(name, shape, dt=F32):
            return ctx.enter_context(nc.sbuf_tensor(name, shape, dt))

        def sem(name):
            return ctx.enter_context(nc.semaphore(name))

        k6T, v32, mhalf = m.k6T, m.v32, m.mhalf
        wqkv = sb("wqkv", [P, KC, C + 2 * HD])
        wo = sb("wo", [P, KC, C])
        wg = sb("wg", [P, KC, E])
        bqkv = sb("bqkv", [P, C + 2 * HD])
        bo = sb("bo", [P, C])
        bg = sb("bg", [E, 1])
        x_in = sb("x_in", [P, 2, NT, C])
        rowb = sb("rowb", [P, 2, 3, C])
        cols = sb("cols", [P, 4])
        gwo = sb("gwo", [P, 2, KC, C])
        gbo = sb("gbo", [P, C])
        bst = sb("bst", [P, NT, 6])
        mv = sb("mv", [P, NT, 2])
        rstd = sb("rstd", [P, NT])
        vtmp = sb("vtmp", [P, NT])
        xn = sb("xn", [P, NT, C])
        hT = sb("hT", [P, KC, T])
        qkv = sb("qkv", [P, NT, C + 2 * HD])
        ra = sb("ra", [P, NT, H + 1, HD])
        rb = sb("rb", [P, NT, H + 1, HD])
        q6 = sb("q6", [P, NT, H, 6 * HD], BF16)
        qp = sb("qp", [P, NT, 3, H + 1, HD], BF16)
        k6 = sb("k6", [P, NT, 6 * HD], BF16)
        q6T = sb("q6T", [6 * HD + 3, 2, H, T], BF16)
        nmax = sb("nmax", [P, NT, H])
        mres = sb("mres", [P, NT, H])
        msp = sb("msp", [P, NT, 3, H], BF16)
        mT = sb("mT", [3 * H, NT, P], BF16)
        pT = sb("pT", [P, PR, 4, P])
        oS = sb("oS", [P, 2, 4, P])
        linv = sb("linv", [P, NT, H])
        oN = sb("oN", [P, 2, C])
        oNT = sb("oNT", [P, 2, KC, P])
        x1 = sb("x1", [P, NT, C])
        bst2 = sb("bst2", [P, NT, 6])
        mv2 = sb("mv2", [P, NT, 2])
        rstd2 = sb("rstd2", [P, NT])
        vtmp2 = sb("vtmp2", [P, NT])
        h2 = sb("h2", [P, NT, C])
        h2T = sb("h2T", [P, KC, T])
        lg = sb("lg", [E, T])
        ps_s = m.psum[:, 0:SR, :]
        ps_t = m.psum[:, SR:SR + TR, :]
        ps_o = m.psum[:, 5, :]
        ps_act = m.psum[:, 6, :]
        ps_dve = m.psum[:, 7, :]
        ident = m.const[:, C_IDENT:C_IDENT + P]
        w_loaded = sem("att_weights_loaded")
        in_loaded = [sem(f"att_inputs_loaded{s}") for s in range(2)]
        m_placed = [sem(f"att_max_rows_placed{i}") for i in range(NT)]

        def program(eng, step, enter=lambda q: None):
            def one(q, last=False):
                enter(q)
                for s, following in merged:
                    if not following:
                        step(q, s)
                    elif not last:
                        step(q.next(), s)

            for s in pro:
                step(Seq(0, 0), s)
            with eng.Fori(0, B // 2 - 1) as it:
                one(Seq(it, 0))
                one(Seq(it, 1))
            one(Seq(B // 2 - 1, 0))
            one(Seq(B // 2 - 1, 1), last=True)

        with nc.Block() as block:
            @block.sync
            def _(sp):
                for dst, src in ((wqkv, m.d["wqkv"]), (wo, m.d["wo"]), (wg, m.d["wg"]), (bqkv, m.d["bqkv"]),
                                 (bo, m.d["bo"]), (bg, m.d["bg"])):
                    sp.dma_start(dst[:], src).then_inc(w_loaded, 16)

                def step(q, s):
                    if s[0] == "ln":
                        sp.wait_ge(g.ad_drain.sem, g.ad_drain.before(q, g.ad_drain.per, 2))
                        sp.wait_ge(g.h2.sem, g.h2.before(q, NT, 2))
                        sp.dma_start(x_in[:, q.s], m.d["x"][bass.ds(q.n * NT, NT)].rearrange("i p c -> p i c")).then_inc(in_loaded[q.s], 16)
                        for n, r in enumerate((2, 4, 3)):
                            sp.dma_start(rowb[:, q.s, n, :], m.mod_rows[0, bass.ds(q.n, 1), r * C:(r + 1) * C].to_broadcast([P, C])).then_inc(in_loaded[q.s], 16)
                    if s[0] == "mT":
                        i = s[1]
                        sp.wait_ge(g.aa_drain.sem, g.aa_drain.done(q, aa_use[s] + 1))
                        sp.dma_start(q6T[6 * HD:6 * HD + 3, q.s, :, i * P:(i + 1) * P],
                                     mT[:, i, :]).then_inc(m_placed[i], 16)
                    if s[0] == "h2T":
                        i = s[1]
                        sp.wait_ge(g.h2.sem, g.h2.done(q, i + 1))
                        sp.dma_start(m.x1_d[bass.ds(q.n * NT + i, 1)].rearrange("i p c -> p (i c)"), x1[:, i, :]).then_inc(g.x1_store.sem, 16)
                        sp.dma_start(m.h2_d[bass.ds(q.n * NT + i, 1)].rearrange("i p c -> p (i c)"), h2[:, i, :]).then_inc(g.h2_store.sem, 16)
                    if s[0] == "lg":
                        sp.wait_ge(g.aa_drain.sem, g.aa_drain.done(q, aa_use[s] + 1))
                        sp.dma_start(m.lg_d[bass.ds(q.n, 1)].rearrange("b e t -> (b e) t"), lg[:]).then_inc(g.lg_store.sem, 16)

                program(sp, step)
                end = Seq(B // 2 - 1, 1)
                for store in (g.x1_store, g.h2_store, g.lg_store):
                    sp.wait_ge(store.sem, store.done(end, store.per))

            @block.gpsimd
            def _(pool):
                pro_chain, att_chain = Chain(pool, g.pool_pro, m.passed), Chain(pool, g.pool_att, m.passed)

                def step(q, s):
                    if s[0] == "ln":
                        pro_chain.start(q)
                        link = pro_chain.link
                        pool.wait_ge(g.moments.sem, g.moments.done(q, NT))
                        settle(pool, m.passed)
                        pool.wait_ge(g.pa_drain.sem, g.pa_drain.before(q, g.pa_drain.per))
                        settle(pool, m.passed)
                        link(pool.tensor_scalar(vtmp[:], mv[:, :, 1], EPS, None, ALU.add))
                        link(pool.tensor_tensor(rstd[:], vtmp[:], mhalf[:], ALU.pow))
                        for i in range(NT):
                            pool.tensor_scalar(xn[:, i, :], x_in[:, q.s, i, :], mv[:, i, 0:1], rstd[:, i:i + 1],
                                               ALU.subtract, ALU.mult).then_inc(g.xn.sem, 1)
                        link(pool.tensor_tensor(gbo[:], bo[:], rowb[:, q.s, 0, :], ALU.mult))
                        for k in range(KC):
                            link(pool.tensor_tensor(gwo[:, q.s, k, :], wo[:, k, :], rowb[:, q.s, 0, :], ALU.mult))
                        pool.wait_ge(g.xn.sem, g.xn.done(q, NT))
                        settle(pool, m.passed)
                        for i in range(NT):
                            ins = pool.tensor_tensor(x_in[:, q.s, i, :], x_in[:, q.s, i, :], gbo[:], ALU.add)
                            if i < NT - 1:
                                link(ins)
                            else:
                                ins.then_inc(g.gated.sem, 1)
                                pool.wait_ge(g.gated.sem, g.gated.done(q, 1))
                                settle(pool, m.passed)
                    if s[0] == "qkv":
                        i = s[1]
                        link = pro_chain.link
                        pool.wait_ge(g.pd_drain.sem, g.pd_drain.done(q, pd_use[s] + 1))
                        settle(pool, m.passed)
                        pool.wait_ge(g.split.sem, g.split.before(q, NT))
                        settle(pool, m.passed)
                        tab = m.const[:, C_ROPE + i * 2 * HD:C_ROPE + (i + 1) * 2 * HD]
                        src = qkv[:, i, 0:C + HD].rearrange("p (h d) -> p h d", d=HD)
                        hh = HD // 2
                        pool.tensor_tensor(ra[:, i], src, tab[:, 0:HD].unsqueeze(1).to_broadcast([P, H + 1, HD]), ALU.mult)
                        for half in range(2):
                            a, c = half * hh, (1 - half) * hh
                            link(pool.tensor_tensor(rb[:, i, :, a:a + hh], src[:, :, c:c + hh],
                                                    tab[:, HD + a:HD + a + hh].unsqueeze(1).to_broadcast([P, H + 1, hh]), ALU.mult))
                        link(pool.tensor_copy(v32[:, q.s, i, 0:HD], qkv[:, i, C + HD:C + 2 * HD]))
                        pool.tensor_tensor(ra[:, i], ra[:, i], rb[:, i], ALU.add).then_inc(g.rope.sem, 1)
                        pool.wait_ge(g.rope.sem, g.rope.done(q, i + 1))
                        settle(pool, m.passed)
                        if i == NT - 1:
                            pro_chain.end()
                    if s[0] == "qT" and s[2] == 0:
                        i = s[1]
                        pool.wait_ge(g.split.sem, g.split.done(q, i + 1))
                        settle(pool, m.passed)
                        pool.wait_ge(g.pa_drain.sem, g.pa_drain.before(q, g.pa_drain.per))
                        settle(pool, m.passed)
                        pool.tensor_copy(q6[:, i, :, 0:3 * HD].rearrange("p h (r d) -> p h r d", r=3),
                                         qp[:, i, 0, 0:H].unsqueeze(2).to_broadcast([P, H, 3, HD]))
                        pool.tensor_copy(q6[:, i, :, 3 * HD:5 * HD].rearrange("p h (r d) -> p h r d", r=2),
                                         qp[:, i, 1, 0:H].unsqueeze(2).to_broadcast([P, H, 2, HD]))
                        pool.tensor_copy(q6[:, i, :, 5 * HD:6 * HD], qp[:, i, 2, 0:H]).then_inc(g.q6.sem, 1)
                    if s[0] == "mT":
                        i = s[1]
                        if i == 0:
                            att_chain.start(q)
                        link = att_chain.link
                        pool.wait_ge(g.s_max.sem, g.s_max.done(q, s_use[("S", i, H // S_HEADS[i] - 1)] + 1))
                        settle(pool, m.passed)
                        pool.wait_ge(g.aa_drain.sem, g.aa_drain.before(q, n_aa))
                        settle(pool, m.passed)
                        link(pool.tensor_copy(msp[:, i, 0, :], nmax[:, i, :]))
                        link(pool.tensor_tensor(mres[:, i, :], nmax[:, i, :], msp[:, i, 0, :], ALU.subtract))
                        link(pool.tensor_copy(msp[:, i, 1, :], mres[:, i, :]))
                        pool.tensor_tensor(msp[:, i, 2, :], mres[:, i, :], msp[:, i, 1, :], ALU.subtract).then_inc(g.msp.sem, 1)
                        pool.wait_ge(g.msp.sem, g.msp.done(q, i + 1))
                        settle(pool, m.passed)
                    if s[0] == "pr":
                        i = s[1]
                        link = att_chain.link
                        pool.wait_ge(g.moments2.sem, g.moments2.done(q, i + 1))
                        settle(pool, m.passed)
                        pool.wait_ge(g.aa_drain.sem, g.aa_drain.before(q, n_aa))
                        settle(pool, m.passed)
                        pool.wait_ge(g.h2_store.sem, g.h2_store.before(q, 16 * NT))
                        settle(pool, m.passed)
                        link(pool.tensor_scalar(vtmp2[:, i:i + 1], mv2[:, i, 1:2], EPS, None, ALU.add))
                        link(pool.tensor_tensor(rstd2[:, i:i + 1], vtmp2[:, i:i + 1], mhalf[:, 0:1], ALU.pow))
                        link(pool.tensor_scalar(h2[:, i, :], x1[:, i, :], mv2[:, i, 0:1], rstd2[:, i:i + 1],
                                                ALU.subtract, ALU.mult))
                        link(pool.tensor_tensor(h2[:, i, :], h2[:, i, :], rowb[:, q.s, 1, :], ALU.mult))
                        pool.tensor_tensor(h2[:, i, :], h2[:, i, :], rowb[:, q.s, 2, :], ALU.add).then_inc(g.h2.sem, 1)
                        if i == NT - 1:
                            att_chain.end()

                def with_inputs(q, s):
                    if s[0] == "ln":
                        pool.wait_ge(in_loaded[q.s], q.it * 64 + 64)
                        settle(pool, m.passed)
                    step(q, s)

                pool.wait_ge(w_loaded, 6 * 16)
                program(pool, with_inputs)

            @block.vector
            def _(dve):
                pro_chain, att_chain = Chain(dve, g.dve_pro, m.passed), Chain(dve, g.dve_att, m.passed)

                def step(q, s):
                    if s[0] == "ln":
                        pro_chain.start(q)
                        dve.wait_ge(in_loaded[q.s], q.it * 64 + 64)
                        dve.wait_ge(g.pa_drain.sem, g.pa_drain.before(q, pa_use[("hT", 1)] + 1))
                        dve.tensor_copy(cols[:].unsqueeze(2), m.modT[:, 0, 0:4, bass.ds(q.n, 1)]).then_inc(g.cols.sem, 1)
                        for i in range(NT):
                            dve.bn_stats(bst[:, i, :], x_in[:, q.s, i, :]).then_inc(g.stats.sem, 1)
                        dve.wait_ge(g.stats.sem, g.stats.done(q, NT))
                        dve.wait_ge(g.xn.sem, g.xn.before(q, NT))
                        settle(dve, m.passed)
                        for i in range(NT):
                            dve.bn_aggr(mv[:, i, :], bst[:, i, :]).then_inc(g.moments.sem, 1)
                    if s[0] == "qkv":
                        i = s[1]
                        dve.wait_ge(g.pd_fill.sem, g.pd_fill.done(q, pd_use[s] + 1))
                        dve.wait_ge(g.rope.sem, g.rope.before(q, NT))
                        dve.tensor_tensor(qkv[:, i, :], ps_dve[:, 0:C + 2 * HD], bqkv[:], ALU.add).then_inc(g.pd_drain.sem, 1)
                    if s[0] == "kT":
                        link = pro_chain.link
                        dve.wait_ge(g.q6.sem, g.q6.before(q, NT))
                        dve.wait_ge(g.pa_drain.sem, g.pa_drain.before(q, g.pa_drain.per))
                        for i in range(NT):
                            dve.wait_ge(g.rope.sem, g.rope.done(q, i + 1))
                            link(dve.tensor_copy(qp[:, i, 0], ra[:, i]))
                            link(dve.tensor_tensor(ra[:, i], ra[:, i], qp[:, i, 0], ALU.subtract))
                            link(dve.tensor_copy(qp[:, i, 1], ra[:, i]))
                            link(dve.tensor_tensor(qp[:, i, 2], ra[:, i], qp[:, i, 1], ALU.subtract))
                            dve.tensor_copy(k6[:, i, 0:3 * HD].rearrange("p (r d) -> p r d", d=HD), qp[:, i, :, H, :])
                            dve.tensor_copy(k6[:, i, 3 * HD:5 * HD].rearrange("p (r d) -> p r d", d=HD), qp[:, i, 0:2, H, :])
                            link(dve.tensor_copy(k6[:, i, 5 * HD:6 * HD], qp[:, i, 0, H, :]))
                            dve.sem_inc(g.split.sem, 1)
                        pro_chain.end()
                    if s[0] == "S":
                        _, i, u = s
                        nh, n = S_HEADS[i], s_use[s]
                        dve.wait_ge(g.s_fill.sem, g.s_fill.done(q, n + 1))
                        if u == 0:
                            dve.wait_ge(g.msp.sem, g.msp.before(q, i + 1))
                        dve.tensor_reduce(nmax[:, i, u * nh:(u + 1) * nh],
                                          ps_s[:, n % SR, 0:nh * (i + 1) * P].rearrange("p (h k) -> p h k", h=nh),
                                          AX_X, ALU.max, negate=True).then_inc(g.s_max.sem, 1)
                    if s[0] == "oT":
                        i = s[1]
                        if i == 0:
                            att_chain.start(q)
                        dve.wait_ge(g.ad_fill.sem, g.ad_fill.done(q, ad_use[s] + 1))
                        src = ps_dve.rearrange("p (l g d) -> p g l d", l=4, g=HG)
                        lv = linv[:, i, :].rearrange("p (g l) -> p g l", g=HG)
                        att_chain.link(dve.reciprocal(lv, src[:, :, :, HD]))
                        if i >= 2:
                            dve.wait_ge(g.aa_drain.sem, g.aa_drain.done(q, aa_use[("oC", i - 2)] + 1))
                        dve.tensor_tensor(oN[:, i % 2, :].rearrange("p (g l d) -> p g l d", g=HG, l=4),
                                          src[:, :, :, 0:HD], lv.unsqueeze(3).to_broadcast([P, HG, 4, HD]),
                                          ALU.mult).then_inc(g.ad_drain.sem, 1)
                    if s[0] == "pr":
                        i = s[1]
                        dve.wait_ge(g.ad_fill.sem, g.ad_fill.done(q, ad_use[s] + 1))
                        dve.wait_ge(g.gated.sem, g.gated.done(q, 1))
                        dve.wait_ge(g.x1_store.sem, g.x1_store.before(q, 16 * NT))
                        dve.wait_ge(g.h2.sem, g.h2.before(q, NT))
                        dve.tensor_tensor(x1[:, i, :], ps_dve[:, 0:C], x_in[:, q.s, i, :], ALU.add).then_inc(g.ad_drain.sem, 1)
                        dve.wait_ge(g.ad_drain.sem, g.ad_drain.done(q, ad_use[s] + 1))
                        att_chain.link(dve.bn_stats(bst2[:, i, :], x1[:, i, :]))
                        dve.bn_aggr(mv2[:, i, :], bst2[:, i, :]).then_inc(g.moments2.sem, 1)
                        if i == NT - 1:
                            att_chain.end()

                dve.wait_ge(w_loaded, 6 * 16)
                program(dve, step)

            @block.scalar
            def _(act):
                def step(q, s):
                    if s[0] == "hT":
                        k = s[1]
                        act.wait_ge(g.pa_fill.sem, g.pa_fill.done(q, pa_use[s] + 1))
                        act.wait_ge(g.cols.sem, g.cols.done(q, 1))
                        act.wait_ge(g.pd_drain.sem, g.pd_drain.before(q, NT))
                        act.activation(hT[:, k, :], ps_act, ACT.Identity, bias=cols[:, k:k + 1],
                                       scale=cols[:, KC + k:KC + k + 1]).then_inc(g.pa_drain.sem, 1)
                    if s[0] == "kT":
                        act.wait_ge(g.pa_fill.sem, g.pa_fill.done(q, pa_use[s] + 1))
                        act.activation(k6T[0:6 * HD, q.s, :], ps_act[0:6 * HD].bitcast(BF16)[:, 0:T],
                                       ACT.Copy).then_inc(g.pa_drain.sem, 1)
                    if s[0] == "qT":
                        _, i, half = s
                        act.wait_ge(g.pa_fill.sem, g.pa_fill.done(q, pa_use[s] + 1))
                        act.activation(q6T[0:6 * HD, q.s, half * 8:half * 8 + 8, i * P:(i + 1) * P],
                                       ps_act[0:6 * HD].bitcast(BF16).rearrange("p (h t) -> p h t", h=8),
                                       ACT.Copy).then_inc(g.pa_drain.sem, 1)
                    if s[0] == "mT":
                        i = s[1]
                        act.wait_ge(g.aa_fill.sem, g.aa_fill.done(q, aa_use[s] + 1))
                        act.activation(mT[:, i, :], ps_act[0:3 * H].bitcast(BF16)[:, 0:P],
                                       ACT.Copy).then_inc(g.aa_drain.sem, 1)
                    if s[0] == "ST":
                        n = t_use[s]
                        act.wait_ge(g.t_fill.sem, g.t_fill.done(q, n + 1))
                        prev = (n - PR) // HG
                        if n >= PR:
                            act.wait_ge(g.pv.sem, g.pv.done(q, prev + 1))
                        else:
                            act.wait_ge(g.pv.sem, g.pv.before(q, n_pv + prev + 1))
                        act.activation(pT[:, n % PR].rearrange("p h t -> p (h t)"), ps_t[:, n % TR, :], ACT.Exp,
                                       scale=HD ** -0.5).then_inc(g.probs.sem, 1)
                    if s[0] == "oE":
                        i = s[1]
                        act.wait_ge(g.pv.sem, g.pv.done(q, pv_use[("PV", i, i)] + 1))
                        prev = ad_use[("oT", i)]
                        if i >= 2:
                            act.wait_ge(g.ad_drain.sem, g.ad_drain.done(q, ad_use[("oT", i - 2)] + 1))
                        else:
                            act.wait_ge(g.ad_drain.sem, g.ad_drain.before(q, ad_use[("oT", i + 2)] + 1))
                        act.activation(oS[:, i % 2].rearrange("p l t -> p (l t)"), ps_o, ACT.Copy).then_inc(g.o_out.sem, 1)
                    if s[0] == "oC":
                        i = s[1]
                        act.wait_ge(g.aa_fill.sem, g.aa_fill.done(q, aa_use[s] + 1))
                        if i >= 2:
                            act.wait_ge(g.ad_fill.sem, g.ad_fill.done(q, ad_use[("pr", i - 2)] + 1))
                        else:
                            act.wait_ge(g.ad_fill.sem, g.ad_fill.before(q, ad_use[("pr", i + 2)] + 1))
                        act.activation(oNT[:, i % 2].rearrange("p k t -> p (k t)"), ps_act[:, 0:KC * P],
                                       ACT.Copy).then_inc(g.aa_drain.sem, 1)
                    if s[0] == "h2T":
                        i = s[1]
                        act.wait_ge(g.aa_fill.sem, g.aa_fill.done(q, aa_use[s] + 1))
                        act.activation(h2T[:, :, i * P:(i + 1) * P], ps_act[:, 0:KC * P].rearrange("p (k t) -> p k t", k=KC),
                                       ACT.Copy).then_inc(g.aa_drain.sem, 1)
                    if s[0] == "lg":
                        act.wait_ge(g.aa_fill.sem, g.aa_fill.done(q, aa_use[s] + 1))
                        act.wait_ge(g.lg_store.sem, g.lg_store.before(q, 16))
                        act.activation(lg[:], ps_act[0:E, :], ACT.Identity, bias=bg[:, 0:1]).then_inc(g.aa_drain.sem, 1)

                act.wait_ge(w_loaded, 6 * 16)
                program(act, step)

            @block.tensor
            def _(pe):
                bank = {}

                def free(name, q, signal, n):
                    for last, value in bank.get(name, []):
                        pe.wait_ge(last.sem, value)
                    bank[name] = [(signal, signal.done(q, n))]

                def enter(q):
                    for name, a, b in (("act", g.pa_drain, g.aa_drain), ("dve", g.pd_drain, g.ad_drain)):
                        bank[name] = [(a, a.done(q, a.per)), (b, b.before(q, b.per))]

                def step(q, s):
                    if s[0] == "hT":
                        k = s[1]
                        pe.wait_ge(g.xn.sem, g.xn.done(q, NT))
                        free("act", q, g.pa_drain, pa_use[s] + 1)
                        for i in range(NT):
                            last = pe.transpose(ps_act[:, i * P:(i + 1) * P], xn[:, i, k * P:(k + 1) * P], ident)
                        last.then_inc(g.pa_fill.sem, 1)
                    if s[0] == "qkv":
                        i = s[1]
                        pe.wait_ge(g.pa_drain.sem, g.pa_drain.done(q, pa_use[("hT", 1)] + 1))
                        free("dve", q, g.pd_drain, pd_use[s] + 1)
                        for k in range(KC):
                            last = pe.matmul(ps_dve[:, 0:C + 2 * HD], hT[:, k, i * P:(i + 1) * P], wqkv[:, k, :],
                                             start=k == 0, stop=k == KC - 1)
                        last.then_inc(g.pd_fill.sem, 1)
                    if s[0] == "kT":
                        pe.wait_ge(g.split.sem, g.split.done(q, NT))
                        free("act", q, g.pa_drain, pa_use[s] + 1)
                        out = ps_act[0:6 * HD].bitcast(BF16)
                        for i in range(NT):
                            last = pe.transpose(out[:, i * P:(i + 1) * P], k6[:, i, :], m.ident_bf[:])
                        last.then_inc(g.pa_fill.sem, 1)
                    if s[0] == "qT":
                        _, i, half = s
                        pe.wait_ge(g.q6.sem, g.q6.done(q, i + 1))
                        free("act", q, g.pa_drain, pa_use[s] + 1)
                        out = ps_act[0:6 * HD].bitcast(BF16)
                        for h in range(8):
                            last = pe.transpose(out[:, h * P:(h + 1) * P], q6[:, i, half * 8 + h, :], m.ident_bf[:])
                        last.then_inc(g.pa_fill.sem, 1)
                    if s[0] == "S":
                        _, i, u = s
                        nh, n = S_HEADS[i], s_use[s]
                        if u == 0:
                            pe.wait_ge(g.pa_drain.sem, g.pa_drain.done(q, pa_use[("qT", i, 1)] + 1))
                        if n >= SR:
                            pe.wait_ge(g.s_max.sem, g.s_max.done(q, n - SR + 1))
                        else:
                            pe.wait_ge(g.s_max.sem, g.s_max.before(q, n_s + n - SR + 1))
                        w = (i + 1) * P
                        out = ps_s[:, n % SR, 0:nh * w].rearrange("p (h k) -> p h k", h=nh)
                        for a in range(nh):
                            pe.matmul(out[:, a, :], q6T[0:6 * HD, q.s, u * nh + a, i * P:(i + 1) * P],
                                      k6T[0:6 * HD, q.s, 0:w], start=a == 0, stop=False, skip_group_check=True)
                        pe.matmul(out[:, :, i * P:w], m.ident_bf[:], m.negs_bf[:].unsqueeze(1).to_broadcast([P, nh, P]),
                                  start=False, stop=True, skip_group_check=True).then_inc(g.s_fill.sem, 1)
                    if s[0] == "mT":
                        i = s[1]
                        pe.wait_ge(g.msp.sem, g.msp.done(q, i + 1))
                        free("act", q, g.aa_drain, aa_use[s] + 1)
                        settle(pe, m.passed)
                        pe.transpose(ps_act[0:3 * H].bitcast(BF16)[:, 0:P], msp[:, i].rearrange("p r h -> p (r h)"),
                                     m.ident_bf[:]).then_inc(g.aa_fill.sem, 1)
                    if s[0] == "ST":
                        _, i, j, hg = s
                        n = t_use[s]
                        if j == 0 and hg == 0:
                            pe.wait_ge(m_placed[i], q.n * 16 + 16)
                        if n >= TR:
                            pe.wait_ge(g.probs.sem, g.probs.done(q, n - TR + 1))
                        else:
                            last = max(k for k in range(n_t) if k % TR == n)
                            pe.wait_ge(g.probs.sem, g.probs.before(q, last + 1))
                        out = ps_t[:, (n) % TR, :].rearrange("p (h t) -> p h t", h=4)
                        last = pe.matmul(out, k6T[:, q.s, j * P:(j + 1) * P],
                                         q6T[:, q.s, hg * 4:hg * 4 + 4, i * P:(i + 1) * P], start=True, stop=j < i)
                        if j == i:
                            last = pe.matmul(out, m.ident_bf[:], m.negt_bf[:].unsqueeze(1).to_broadcast([P, 4, P]),
                                             start=False, stop=True)
                        last.then_inc(g.t_fill.sem, 1)
                    if s[0] == "PV":
                        _, i, j = s
                        n = t_use[("ST", i, j, 0)]
                        pe.wait_ge(g.probs.sem, g.probs.done(q, n + HG))
                        if j == 0:
                            pe.wait_ge(g.o_out.sem, g.o_out.done(q, i) if i else g.o_out.before(q, NT))
                        for hg in range(HG):
                            last = pe.matmul(ps_o[32 * hg:32 * hg + 32, :], v32[:, q.s, j, :],
                                             pT[:, (n + hg) % PR].rearrange("p h t -> p (h t)"),
                                             start=j == 0, stop=j == i, tile_position=(0, 32 * hg))
                        last.then_inc(g.pv.sem, 1)
                    if s[0] == "oT":
                        i = s[1]
                        pe.wait_ge(g.o_out.sem, g.o_out.done(q, i + 1))
                        free("dve", q, g.ad_drain, ad_use[s] + 1)
                        for l in range(4):
                            last = pe.transpose(ps_dve[:, l * P:(l + 1) * P], oS[:, i % 2, l, :], ident)
                        last.then_inc(g.ad_fill.sem, 1)
                    if s[0] == "oC":
                        i = s[1]
                        pe.wait_ge(g.ad_drain.sem, g.ad_drain.done(q, ad_use[("oT", i)] + 1))
                        free("act", q, g.aa_drain, aa_use[s] + 1)
                        for k in range(KC):
                            last = pe.transpose(ps_act[:, k * P:(k + 1) * P], oN[:, i % 2, k * P:(k + 1) * P], ident)
                        last.then_inc(g.aa_fill.sem, 1)
                    if s[0] == "pr":
                        i = s[1]
                        pe.wait_ge(g.aa_drain.sem, g.aa_drain.done(q, aa_use[("oC", i)] + 1))
                        pe.wait_ge(g.gated.sem, g.gated.done(q, 1))
                        free("dve", q, g.ad_drain, ad_use[s] + 1)
                        for k in range(KC):
                            last = pe.matmul(ps_dve[:, 0:C], oNT[:, i % 2, k, :], gwo[:, q.s, k, :],
                                             start=k == 0, stop=k == KC - 1)
                        last.then_inc(g.ad_fill.sem, 1)
                    if s[0] == "h2T":
                        i = s[1]
                        pe.wait_ge(g.h2.sem, g.h2.done(q, i + 1))
                        free("act", q, g.aa_drain, aa_use[s] + 1)
                        for k in range(KC):
                            last = pe.transpose(ps_act[:, k * P:(k + 1) * P], h2[:, i, k * P:(k + 1) * P], ident)
                        last.then_inc(g.aa_fill.sem, 1)
                    if s[0] == "lg":
                        free("act", q, g.aa_drain, aa_use[s] + 1)
                        for k in range(KC):
                            last = pe.matmul(ps_act[0:E, :], wg[:, k, :], h2T[:, k, :],
                                             start=k == 0, stop=k == KC - 1)
                        last.then_inc(g.aa_fill.sem, 1)

                pe.wait_ge(w_loaded, 6 * 16)
                program(pe, step, enter)


def routing_phase(nc, m):
    with ExitStack() as ctx:
        def sb(name, shape, dt=F32):
            return ctx.enter_context(nc.sbuf_tensor(name, shape, dt))

        def sem(name):
            return ctx.enter_context(nc.semaphore(name))

        logits = sb("logits", [B * E, T])
        probs = sb("probs", [B * E, T])
        nmax = sb("route_nmax", [B * E, 1])
        total = sb("route_total", [B * E, 1])
        vals = sb("route_vals", [B * E, 2, TOPK])
        idx = sb("route_idx", [B * E, TOPK], U32)
        idxf = sb("route_idxf", [B * E, 2, TOPK])
        loaded = sem("route_loaded")
        chain = sem("route_vector_steps")
        max_ready = sem("route_max_ready")
        exp_ready = sem("route_exp_ready")
        tables = sem("route_tables_ready")
        turned = sem("route_turned")
        with nc.Block() as block:
            @block.sync
            def _(sp):
                sp.dma_start(logits[:], m.lg_d.rearrange("b e t -> (b e) t")).then_inc(loaded, 16)
                sp.dma_start(m.par_e[:, :, 4:7], m.d["eb"]).then_inc(loaded, 16)
                for b in range(B):
                    lo = (b % 2) * TOPK
                    sp.dma_start(m.gb_rows[lo:lo + TOPK, b // 2, :],
                                 m.mod_rows[0, b:b + 1, 5 * C:6 * C].to_broadcast([TOPK, C])).then_inc(loaded, 16)

            @block.scalar
            def _(act):
                act.wait_ge(max_ready, 1)
                act.activation(probs[:], logits[:], ACT.Exp, bias=nmax[:, 0:1],
                               accum_out=total[:, 0:1]).then_inc(exp_ready, 1)

            @block.tensor
            def _(pe):
                pe.wait_ge(tables, 1)
                ident = m.const[:, C_IDENT:C_IDENT + P]
                pe.transpose(m.psum[:, 0, 0:P], idxf[:].rearrange("p r s -> p (r s)"), ident)
                pe.transpose(m.psum[:, 1, 0:P], vals[:].rearrange("p r s -> p (r s)"), ident).then_inc(turned, 1)

            @block.vector
            def _(dve):
                count = [0]

                def link(ins):
                    count[0] += 1
                    ins.then_inc(chain, 1)
                    dve.wait_ge(chain, count[0])

                dve.wait_ge(loaded, 16 * (2 + B))
                dve.tensor_reduce(nmax[:], logits[:], AX_X, ALU.max, negate=True).then_inc(max_ready, 1)
                dve.wait_ge(exp_ready, 1)
                link(dve.reciprocal(total[:], total[:]))
                link(dve.tensor_scalar(probs[:], probs[:], total[:, 0:1], None, ALU.mult))
                for r in range(TOPK // 8):
                    part = slice(8 * r, 8 * r + 8)
                    link(dve.max(out=vals[:, 0, part], in_=probs[:]))
                    link(dve.max_index(out=idx[:, part], in_max=vals[:, 0, part], in_values=probs[:]))
                    link(dve.match_replace(out=probs[:], in_to_replace=vals[:, 0, part], in_values=probs[:],
                                           imm_value=-1.0))
                link(dve.tensor_copy(vals[:, 1, :], vals[:, 0, :]))
                seq = m.const[:, C_SEQ:C_SEQ + 1]
                link(dve.tensor_scalar(idxf[:, 0, :], idx[:], seq, None, ALU.add))
                link(dve.tensor_copy(idxf[:, 1, :], idxf[:, 0, :]))
                dve.sem_inc(tables, 1)
                dve.wait_ge(turned, 1)
                for half in range(2):
                    lo = half * TOPK
                    for bank, dst in ((0, m.idx_e[lo:lo + TOPK]), (1, m.par_e[lo:lo + TOPK, :, 0:4])):
                        src = m.psum[lo:lo + TOPK, bank, 0:P].rearrange("p (s two e) -> p e s two", two=2, e=E)
                        link(dve.tensor_copy(dst, src[:, :, :, half]))
                for i in range(4):
                    link(dve.tensor_tensor(m.par_e[:, :, 7 + i], m.par_e[:, :, i], m.par_e[:, :, 6], ALU.mult))


class ExpertSignals:

    def __init__(self, new):
        self.params = new("exp_params_ready", 1)
        self.picked = new("exp_indices_ready", 1)
        self.back = new("exp_scatter_indices_ready", 1)
        self.t_fill = new("exp_tokensT_filled", KC)
        self.t_act = new("exp_tokensT_by_act", 1)
        self.t_dve = new("exp_tokensT_by_vector", 1)
        self.l1_fill = new("exp_layer1_filled", KC)
        self.l1_act = new("exp_layer1_by_act", 1)
        self.l1_dve = new("exp_layer1_by_vector", 1)
        self.l2_fill = new("exp_layer2_filled", KC)
        self.l2_act = new("exp_layer2_by_act", 1)
        self.l2_dve = new("exp_layer2_by_vector", 1)
        self.l3_fill = new("exp_layer3_filled", 4)
        self.weighted = new("exp_layer3_weighted", 4)
        self.gated = new("exp_outputs_gated", 4)
        self.y_free = new("exp_outputs_seen_added", 1)


def expert_phase(nc, m):
    g = m.exp
    with ExitStack() as ctx:
        def sb(name, shape, dt=F32):
            return ctx.enter_context(nc.sbuf_tensor(name, shape, dt))

        def sem(name):
            return ctx.enter_context(nc.semaphore(name))

        wts = sb("expert_w", [P, 2, 3, KC, C])
        idx = sb("expert_idx", [P, 2, 4], U32)
        idx_back = sb("expert_idx_back", [P, 4], U32)
        par = sb("expert_par", [P, 2, 11])
        tok = sb("expert_tokens", [P, 2, 4, C])
        tokT = sb("expert_tokensT", [P, 2, KC, 512])
        h1 = sb("expert_h1", [P, KC, 512])
        h2 = sb("expert_h2", [P, KC, 512])
        yw = sb("expert_weighted", [P, 4, C])
        y = sb("expert_y", [P, 2, 4, C])
        w_in = [sem(f"exp_weights_loaded{s}") for s in range(2)]
        added = sem("exp_outputs_added")
        gathered = [sem(f"exp_tokens_gathered{s}") for s in range(2)]
        ps_t, ps_1, ps_2 = m.psum[:, 0:2, :], m.psum[:, 2:4, :], m.psum[:, 4:6, :]
        ps_3 = m.psum[:, 6:8, :].rearrange("p b (i c) -> p (b i) c", i=2)
        rows = m.x1_d.rearrange("i p c -> (i p) c")
        tokens = m.h2_d.rearrange("i p c -> (i p) c")
        ident = m.const[:, C_IDENT:C_IDENT + P]

        def is_first(q):
            return isinstance(q.n, int) and q.n == 0

        def program(eng, ahead, main):
            def one(q, last=False):
                if not last:
                    ahead(q.next())
                main(q, last)

            ahead(Seq(0, 0))
            one(Seq(0, 0))
            with eng.Fori(0, E // 2 - 1) as it:
                one(Seq(it, 1))
                one(Seq(it, 1).next())
            one(Seq(E // 2 - 1, 1), last=True)

        with nc.Block() as block:
            @block.sync
            def _(sp):
                def load(q):
                    sp.wait_ge(g.l3_fill.sem, g.l3_fill.before(q, 4, 2))
                    sp.dma_start(wts[:, q.s].rearrange("p l k c -> p (l k c)"),
                                 m.d["ew"][bass.ds(q.n, 1)].rearrange("e p n -> p (e n)")).then_inc(w_in[q.s], 16)

                program(sp, load, lambda q, last: None)

            @block.gpsimd
            def _(pool):
                def gather(q):
                    pool.wait_ge(g.t_fill.sem, g.t_fill.before(q, KC, 2))
                    settle(pool, m.passed)
                    pool.tensor_copy(idx[:, q.s, :].unsqueeze(1), m.idx_e[:, bass.ds(q.n, 1), :]).then_inc(g.picked.sem, 1)
                    pool.wait_ge(g.picked.sem, g.picked.done(q, 1))
                    settle(pool, m.passed)
                    for i in range(4):
                        pool.indirect_dma_start(
                            out=tok[:, q.s, i, :], out_offset=None, in_=tokens,
                            in_offset=bass.IndirectOffsetOnAxis(ap=idx[:, q.s, i:i + 1], axis=0),
                        ).then_inc(gathered[q.s], 16)

                def scatter(q, last):
                    if not is_first(q):
                        pool.wait_ge(added, q.n * 64)
                        pool.sem_inc(g.y_free.sem, 1)
                    settle(pool, m.passed)
                    pool.tensor_copy(idx_back[:].unsqueeze(1), m.idx_e[:, bass.ds(q.n, 1), :]).then_inc(g.back.sem, 1)
                    pool.wait_ge(g.back.sem, g.back.done(q, 1))
                    for i in range(4):
                        pool.wait_ge(g.gated.sem, g.gated.done(q, i + 1))
                        settle(pool, m.passed)
                        pool.indirect_dma_start(
                            out=rows, out_offset=bass.IndirectOffsetOnAxis(ap=idx_back[:, i:i + 1], axis=0),
                            in_=y[:, q.s, i, :], in_offset=None, compute_op=ALU.add,
                        ).then_inc(added, 16)

                program(pool, gather, scatter)
                pool.wait_ge(added, E * 64)

            @block.tensor
            def _(pe):
                def turn(q, k):
                    if k == 0:
                        pe.wait_ge(gathered[q.s], q.it * 64 + 64)
                        pe.wait_ge(g.t_act.sem, g.t_act.before(q, 1))
                    else:
                        pe.wait_ge(g.t_dve.sem, g.t_dve.before(q, 1))
                    for i in range(4):
                        last = pe.transpose(ps_t[:, k, i * P:(i + 1) * P], tok[:, q.s, i, k * P:(k + 1) * P], ident)
                    last.then_inc(g.t_fill.sem, 1)

                def layer(q, n, ps, src, ready, banks_free, fill):
                    for k in range(KC):
                        signal, value = ready[k]
                        pe.wait_ge(signal.sem, value)
                        for o in range(KC):
                            if k == 0:
                                pe.wait_ge(banks_free[o].sem, banks_free[o].before(q, 1))
                            ins = pe.matmul(ps[:, o, :], wts[:, q.s, n, k, o * P:(o + 1) * P], src[:, k, :],
                                            start=k == 0, stop=k == KC - 1)
                            if k == KC - 1:
                                ins.then_inc(fill.sem, 1)

                def ahead(q):
                    if is_first(q):
                        turn(q, 0)
                        turn(q, 1)

                def main(q, last):
                    nxt = None if last else q.next()
                    pe.wait_ge(w_in[q.s], q.it * 16 + 16)
                    layer(q, 0, ps_1, tokT[:, q.s], [(g.t_act, g.t_act.done(q, 1)), (g.t_dve, g.t_dve.done(q, 1))],
                          (g.l1_act, g.l1_dve), g.l1_fill)
                    if nxt:
                        turn(nxt, 0)
                    layer(q, 1, ps_2, h1, [(g.l1_act, g.l1_act.done(q, 1)), (g.l1_dve, g.l1_dve.done(q, 1))],
                          (g.l2_act, g.l2_dve), g.l2_fill)
                    if nxt:
                        turn(nxt, 1)
                    pe.wait_ge(g.l2_act.sem, g.l2_act.done(q, 1))
                    pe.wait_ge(g.l2_dve.sem, g.l2_dve.done(q, 1))
                    for i in range(4):
                        pe.wait_ge(g.weighted.sem, g.weighted.before(q, i + 1 if i % 2 else i + 2))
                        for k in range(KC):
                            ins = pe.matmul(ps_3[:, i, :], h2[:, k, i * P:(i + 1) * P], wts[:, q.s, 2, k, :],
                                            start=k == 0, stop=k == KC - 1)
                        ins.then_inc(g.l3_fill.sem, 1)

                program(pe, ahead, main)

            @block.scalar
            def _(act):
                def copy_tokens(q):
                    act.wait_ge(g.t_fill.sem, g.t_fill.done(q, 1))
                    act.wait_ge(g.l1_fill.sem, g.l1_fill.before(q, KC, 2))
                    act.activation(tokT[:, q.s, 0, :], ps_t[:, 0, :], ACT.Copy).then_inc(g.t_act.sem, 1)

                def ahead(q):
                    if is_first(q):
                        copy_tokens(q)

                def main(q, last):
                    act.wait_ge(g.params.sem, g.params.done(q, 1))
                    act.wait_ge(g.l1_fill.sem, g.l1_fill.done(q, 1))
                    act.wait_ge(g.l2_fill.sem, g.l2_fill.before(q, KC))
                    act.activation(h1[:, 0, :], ps_1[:, 0, :], ACT.Relu, bias=par[:, q.s, 4:5]).then_inc(g.l1_act.sem, 1)
                    if not last:
                        copy_tokens(q.next())
                    act.wait_ge(g.l2_fill.sem, g.l2_fill.done(q, 1))
                    act.wait_ge(g.l3_fill.sem, g.l3_fill.before(q, 4))
                    act.activation(h2[:, 0, :], ps_2[:, 0, :], ACT.Relu, bias=par[:, q.s, 5:6]).then_inc(g.l2_act.sem, 1)
                    for i in range(4):
                        act.wait_ge(g.l3_fill.sem, g.l3_fill.done(q, i + 1 if i % 2 else i + 2))
                        act.wait_ge(g.gated.sem, g.gated.before(q, i + 1))
                        act.activation(yw[:, i, :], ps_3[:, i, :], ACT.Identity, scale=par[:, q.s, i:i + 1],
                                       bias=par[:, q.s, 7 + i:8 + i]).then_inc(g.weighted.sem, 1)

                program(act, ahead, main)

            @block.vector
            def _(dve):
                def copy_tokens(q):
                    dve.wait_ge(g.t_fill.sem, g.t_fill.done(q, 2))
                    dve.wait_ge(g.l1_fill.sem, g.l1_fill.before(q, KC, 2))
                    dve.tensor_copy(tokT[:, q.s, 1, :], ps_t[:, 1, :]).then_inc(g.t_dve.sem, 1)

                def ahead(q):
                    dve.wait_ge(g.weighted.sem, g.weighted.before(q, 4, 2))
                    dve.tensor_copy(par[:, q.s, :].unsqueeze(1), m.par_e[:, bass.ds(q.n, 1), :]).then_inc(g.params.sem, 1)
                    if is_first(q):
                        copy_tokens(q)

                def main(q, last):
                    dve.wait_ge(g.params.sem, g.params.done(q, 1))
                    dve.wait_ge(g.l1_fill.sem, g.l1_fill.done(q, 2))
                    dve.wait_ge(g.l2_fill.sem, g.l2_fill.before(q, KC))
                    dve.tensor_scalar(h1[:, 1, :], ps_1[:, 1, :], par[:, q.s, 4:5], 0.0, ALU.add, ALU.max).then_inc(g.l1_dve.sem, 1)
                    dve.wait_ge(g.l2_fill.sem, g.l2_fill.done(q, 2))
                    dve.wait_ge(g.l3_fill.sem, g.l3_fill.before(q, 4))
                    dve.tensor_scalar(h2[:, 1, :], ps_2[:, 1, :], par[:, q.s, 5:6], 0.0, ALU.add, ALU.max).then_inc(g.l2_dve.sem, 1)
                    if not last:
                        copy_tokens(q.next())
                    for i in range(4):
                        dve.wait_ge(g.weighted.sem, g.weighted.done(q, i + 1))
                        dve.wait_ge(g.y_free.sem, g.y_free.before(q, 1, 2))
                        dve.tensor_tensor(y[:, q.s, i, :], yw[:, i, :], m.gb_rows[:, i, :], ALU.mult).then_inc(g.gated.sem, 1)

                program(dve, ahead, main)


def linear_orders():
    pro = [("ln",), ("hT", 0), ("hT", 1)] + [("qk", n) for n in range(4)] + [("v", i) for i in range(NT)]
    att = []
    for i in range(NT):
        tail = [("oE", i - 1), ("oT", i - 1), ("oC", i - 1), ("pr", i - 1)] if i else []
        head = [("kt", i), ("A", i, 0), ("A", i, 1)] + ([("KV", i)] if i < NT - 1 else [])
        att += mix(head + [("A", i, 2), ("A", i, 3)], tail) + [("PV", i)]
    return pro, att + [("oE", NT - 1), ("oT", NT - 1), ("oC", NT - 1), ("pr", NT - 1)]


class LinearSignals:

    def __init__(self, new):
        self.stats = new("lin_stats", NT)
        self.moments = new("lin_moments", NT)
        self.cols = new("lin_mod_cols", 1)
        self.pool_steps = new("lin_pool_steps", 2 + 3 + 3)
        self.xn = new("lin_xn_ready", NT)
        self.gated = new("lin_gated_ready", 1)
        self.pa_fill = new("lin_prologue_act_bank_filled", 2)
        self.pa_drain = new("lin_prologue_act_bank_drained", 2)
        self.pd_fill = new("lin_prologue_vector_bank_filled", NT)
        self.pd_drain = new("lin_prologue_vector_bank_drained", NT)
        self.aa_fill = new("lin_act_bank_filled", 2 * NT)
        self.aa_drain = new("lin_act_bank_drained", 2 * NT)
        self.ad_fill = new("lin_vector_bank_filled", 2 * NT)
        self.ad_drain = new("lin_vector_bank_drained", 2 * NT)
        self.qk_fill = new("lin_qk_filled", 4)
        self.qk_relu = new("lin_qk_relu", 4)
        self.qk_exp = new("lin_qk_exp", 4)
        self.qk_map = new("lin_qk_mapped", 4)
        self.masked = new("lin_q_masked", 4)
        self.a_fill = new("lin_scores_filled", 4 * NT)
        self.a_keep = new("lin_scores_masked", 4 * NT)
        self.kv_fill = new("lin_state_filled", NT - 1)
        self.kv_copy = new("lin_state_copied", NT - 1)
        self.pv = new("lin_out_filled", NT)
        self.o_out = new("lin_out_copied", NT)
        self.dve_steps = new("lin_vector_steps", 2 * NT)
        self.x3_store = new("lin_x3_stored", 16 * NT)


def linear_phase(nc, m):
    pro, att = linear_orders()
    merged = mix([(s, False) for s in att], [(s, True) for s in pro], 0.0, 0.95)
    aa_use, n_aa = index_of(att, ("kt", "oC"))
    ad_use, n_ad = index_of(att, ("oT", "pr"))
    a_use, n_a = index_of(att, ("A",))
    AR, SR = 2, 8
    g = m.lin
    with ExitStack() as ctx:
        def sb(name, shape, dt=F32):
            return ctx.enter_context(nc.sbuf_tensor(name, shape, dt))

        def sem(name):
            return ctx.enter_context(nc.semaphore(name))

        w = sb("l_w", [P, KC, 3 * C])
        wo = sb("l_wo", [P, KC, C])
        bo = sb("l_bo", [P, C])
        bv = sb("l_bv", [P, C])
        bqk = sb("l_bqk", [P, 4])
        bneg = sb("l_bneg", [P, 4])
        bone = sb("l_bone", [P, 4])
        mhalf = sb("l_mhalf", [P, NT])
        x_in = sb("l_x", [P, 2, NT, C])
        rowb = sb("l_rows", [P, 2, C])
        cols = sb("l_cols", [P, 4])
        gwo = sb("l_gwo", [P, 2, KC, C])
        gbo = sb("l_gbo", [P, C])
        bst = sb("l_bst", [P, NT, 6])
        mv = sb("l_mv", [P, NT, 2])
        rstd = sb("l_rstd", [P, NT])
        vtmp = sb("l_vtmp", [P, NT])
        xn = sb("l_xn", [P, NT, C])
        hT = sb("l_hT", [P, KC, T])
        rt = sb("l_relu", [P, 2, T])
        et = sb("l_exp", [P, 2, T])
        qm = sb("l_q_masked", [P, 2, KC, 2, T])
        kf = sb("l_k", [P, 2, KC, T])
        qs = sb("l_q_all", [P, 2, KC, T])
        v32 = sb("l_v", [P, 2, NT, H, 32])
        ktok = sb("l_k_tokens", [P, NT, C])
        kept = sb("l_scores", [P, SR, 4, P])
        state = sb("l_state", [P, 2, KC, 2 * P])
        oS = sb("l_oS", [P, 2, 4, P])
        linv = sb("l_linv", [P, NT, H])
        oN = sb("l_oN", [P, 2, C])
        oNT = sb("l_oNT", [P, 2, KC, P])
        x3 = sb("l_x3", [P, NT, C])
        ps_a = m.psum[:, 0:AR, :]
        ps_kv = m.psum[:, 2, :]
        ps_o = m.psum[:, 3, :]
        ps_act = m.psum[:, 4, :]
        ps_dve = m.psum[:, 5, :]
        ps_qk = m.psum[:, 6:8, :]
        ident = m.const[:, C_IDENT:C_IDENT + P]
        keep = m.const[:, C_KEEP:C_KEEP + P]
        blocks = m.const[:, C_BD:C_BD + 2 * P]
        w_loaded = sem("lin_weights_loaded")
        ready = sem("lin_constants_ready")
        in_loaded = [sem(f"lin_inputs_loaded{s}") for s in range(2)]

        def program(eng, step, enter=lambda q: None):
            def one(q, last=False):
                enter(q)
                for s, following in merged:
                    if not following:
                        step(q, s)
                    elif not last:
                        step(q.next(), s)

            for s in pro:
                step(Seq(0, 0), s)
            with eng.Fori(0, B // 2 - 1) as it:
                one(Seq(it, 0))
                one(Seq(it, 1))
            one(Seq(B // 2 - 1, 0))
            one(Seq(B // 2 - 1, 1), last=True)

        with nc.Block() as block:
            @block.sync
            def _(sp):
                for dst, src in ((w, m.d["lw"]), (wo, m.d["lwo"]), (bo, m.d["lbo"]), (bv, m.d["lbv"]), (bqk, m.d["lbqk"])):
                    sp.dma_start(dst[:], src).then_inc(w_loaded, 16)

                def step(q, s):
                    if s[0] == "ln":
                        sp.wait_ge(g.ad_drain.sem, g.ad_drain.before(q, n_ad, 2))
                        sp.dma_start(x_in[:, q.s], m.x1_d[bass.ds(q.n * NT, NT)].rearrange("i p c -> p i c")).then_inc(in_loaded[q.s], 16)
                        sp.dma_start(rowb[:, q.s, :], m.mod_rows[1, bass.ds(q.n, 1), 2 * C:3 * C].to_broadcast([P, C])).then_inc(in_loaded[q.s], 16)
                    if s[0] == "pr":
                        i = s[1]
                        sp.wait_ge(g.ad_drain.sem, g.ad_drain.done(q, ad_use[s] + 1))
                        sp.dma_start(m.x3_d[bass.ds(q.n * NT + i, 1)].rearrange("i p c -> p (i c)"), x3[:, i, :]).then_inc(g.x3_store.sem, 16)

                program(sp, step)
                sp.wait_ge(g.x3_store.sem, g.x3_store.done(Seq(B // 2 - 1, 1), 16 * NT))

            @block.gpsimd
            def _(pool):
                chain = Chain(pool, g.pool_steps, m.passed)

                def step(q, s):
                    if s[0] == "ln":
                        chain.start(q)
                        link = chain.link
                        pool.wait_ge(in_loaded[q.s], q.it * 32 + 32)
                        pool.wait_ge(g.moments.sem, g.moments.done(q, NT))
                        pool.wait_ge(g.pa_drain.sem, g.pa_drain.before(q, 2))
                        settle(pool, m.passed)
                        link(pool.tensor_scalar(vtmp[:], mv[:, :, 1], EPS, None, ALU.add))
                        link(pool.tensor_tensor(rstd[:], vtmp[:], mhalf[:], ALU.pow))
                        for i in range(NT):
                            pool.tensor_scalar(xn[:, i, :], x_in[:, q.s, i, :], mv[:, i, 0:1], rstd[:, i:i + 1],
                                               ALU.subtract, ALU.mult).then_inc(g.xn.sem, 1)
                        link(pool.tensor_tensor(gbo[:], bo[:], rowb[:, q.s, :], ALU.mult))
                        for k in range(KC):
                            link(pool.tensor_tensor(gwo[:, q.s, k, :], wo[:, k, :], rowb[:, q.s, :], ALU.mult))
                        pool.wait_ge(g.xn.sem, g.xn.done(q, NT))
                        settle(pool, m.passed)
                        for i in range(NT):
                            ins = pool.tensor_tensor(x_in[:, q.s, i, :], x_in[:, q.s, i, :], gbo[:], ALU.add)
                            if i < NT - 1:
                                link(ins)
                            else:
                                ins.then_inc(g.gated.sem, 1)
                                pool.wait_ge(g.gated.sem, g.gated.done(q, 1))
                                settle(pool, m.passed)
                        chain.end()
                    if s[0] == "qk" and s[1] < 2:
                        k = s[1]
                        pool.wait_ge(g.qk_map.sem, g.qk_map.done(q, k + 1))
                        settle(pool, m.passed)
                        for odd in range(2):
                            c = C_PARITY + odd
                            pool.tensor_scalar(qm[:, q.s, k, odd, :], qs[:, q.s, k, :], m.const[:, c:c + 1], None,
                                               ALU.mult).then_inc(g.masked.sem, 1)

                pool.wait_ge(w_loaded, 5 * 16)
                pool.wait_ge(ready, 1)
                program(pool, step)

            @block.vector
            def _(dve):
                chain = Chain(dve, g.dve_steps, m.passed)

                def step(q, s):
                    if s[0] == "ln":
                        dve.wait_ge(in_loaded[q.s], q.it * 32 + 32)
                        dve.wait_ge(g.pa_drain.sem, g.pa_drain.before(q, 2))
                        dve.tensor_copy(cols[:].unsqueeze(2), m.modT[:, 1, 0:4, bass.ds(q.n, 1)]).then_inc(g.cols.sem, 1)
                        for i in range(NT):
                            dve.bn_stats(bst[:, i, :], x_in[:, q.s, i, :]).then_inc(g.stats.sem, 1)
                        dve.wait_ge(g.stats.sem, g.stats.done(q, NT))
                        dve.wait_ge(g.xn.sem, g.xn.before(q, NT))
                        settle(dve, m.passed)
                        for i in range(NT):
                            dve.bn_aggr(mv[:, i, :], bst[:, i, :]).then_inc(g.moments.sem, 1)
                    if s[0] == "qk":
                        n = s[1]
                        dve.wait_ge(g.qk_exp.sem, g.qk_exp.done(q, n + 1))
                        dst = qs if n < KC else kf
                        dve.scalar_tensor_tensor(out=dst[:, q.s, n % KC, :], in0=ps_qk[:, n % 2, :], scalar=bone[:, n:n + 1],
                                                 in1=et[:, n % 2, :], op0=ALU.add, op1=ALU.max).then_inc(g.qk_map.sem, 1)
                    if s[0] == "v":
                        i = s[1]
                        dve.wait_ge(g.pd_fill.sem, g.pd_fill.done(q, i + 1))
                        dve.tensor_tensor(v32[:, q.s, i, :, 0:HD], ps_dve[:, 0:C].rearrange("p (h d) -> p h d", h=H),
                                          bv[:].rearrange("p (h d) -> p h d", h=H), ALU.add).then_inc(g.pd_drain.sem, 1)
                    if s[0] == "A":
                        n = a_use[s]
                        dve.wait_ge(g.a_fill.sem, g.a_fill.done(q, n + 1))
                        i = s[1]
                        dve.wait_ge(g.pv.sem, g.pv.done(q, i - 1) if i >= 2 else g.pv.before(q, NT + i - 1))
                        dve.tensor_tensor(kept[:, n % SR], ps_a[:, n % AR, :].rearrange("p (h t) -> p h t", h=4),
                                          keep.unsqueeze(1).to_broadcast([P, 4, P]), ALU.mult).then_inc(g.a_keep.sem, 1)
                    if s[0] == "KV":
                        i = s[1]
                        dve.wait_ge(g.kv_fill.sem, g.kv_fill.done(q, i + 1))
                        dve.wait_ge(g.pv.sem, g.pv.done(q, i) if i else g.pv.before(q, NT))
                        dve.tensor_tensor(state[:, i % 2], ps_kv.rearrange("p (k n) -> p k n", k=KC),
                                          blocks.unsqueeze(1).to_broadcast([P, KC, 2 * P]), ALU.mult).then_inc(g.kv_copy.sem, 1)
                    if s[0] == "oT":
                        i = s[1]
                        if i == 0:
                            chain.start(q)
                        dve.wait_ge(g.ad_fill.sem, g.ad_fill.done(q, ad_use[s] + 1))
                        src = ps_dve.rearrange("p (h d) -> p h d", h=H)
                        chain.link(dve.tensor_scalar(linv[:, i, :], src[:, :, HD], 1e-6, None, ALU.add))
                        chain.link(dve.reciprocal(linv[:, i, :], linv[:, i, :]))
                        if i >= 2:
                            dve.wait_ge(g.aa_drain.sem, g.aa_drain.done(q, aa_use[("oC", i - 2)] + 1))
                        dve.tensor_tensor(oN[:, i % 2, :].rearrange("p (h d) -> p h d", h=H), src[:, :, 0:HD],
                                          linv[:, i, :].unsqueeze(2).to_broadcast([P, H, HD]), ALU.mult).then_inc(g.ad_drain.sem, 1)
                        if i == NT - 1:
                            chain.end()
                    if s[0] == "pr":
                        i = s[1]
                        dve.wait_ge(g.ad_fill.sem, g.ad_fill.done(q, ad_use[s] + 1))
                        dve.wait_ge(g.gated.sem, g.gated.done(q, 1))
                        dve.wait_ge(g.x3_store.sem, g.x3_store.before(q, 16 * NT))
                        dve.tensor_tensor(x3[:, i, :], ps_dve[:, 0:C], x_in[:, q.s, i, :], ALU.add).then_inc(g.ad_drain.sem, 1)

                dve.memset(mhalf[:], -0.5)
                dve.memset(v32[:], 0.0).then_inc(ready, 1)
                dve.wait_ge(ready, 1)
                dve.memset(v32[:, :, :, :, HD:HD + 1], 1.0)
                dve.wait_ge(w_loaded, 5 * 16)
                dve.tensor_scalar(bneg[:], bqk[:], -1.0, None, ALU.mult)
                dve.tensor_scalar(bone[:], bqk[:], 1.0, None, ALU.add).then_inc(ready, 1)
                dve.wait_ge(ready, 2)
                program(dve, step)

            @block.scalar
            def _(act):
                def step(q, s):
                    if s[0] == "hT":
                        k = s[1]
                        act.wait_ge(g.pa_fill.sem, g.pa_fill.done(q, k + 1))
                        act.wait_ge(g.cols.sem, g.cols.done(q, 1))
                        act.wait_ge(g.pd_drain.sem, g.pd_drain.before(q, NT))
                        act.activation(hT[:, k, :], ps_act, ACT.Identity, bias=cols[:, k:k + 1],
                                       scale=cols[:, KC + k:KC + k + 1]).then_inc(g.pa_drain.sem, 1)
                    if s[0] == "qk":
                        n = s[1]
                        act.wait_ge(g.qk_fill.sem, g.qk_fill.done(q, n + 1))
                        act.wait_ge(g.qk_map.sem, g.qk_map.done(q, n - 1) if n >= 2 else g.qk_map.before(q, 4 + n - 1))
                        act.activation(rt[:, n % 2, :], ps_qk[:, n % 2, :], ACT.Relu, bias=bneg[:, n:n + 1],
                                       scale=-1.0).then_inc(g.qk_relu.sem, 1)
                        act.wait_ge(g.qk_relu.sem, g.qk_relu.done(q, n + 1))
                        act.activation(et[:, n % 2, :], rt[:, n % 2, :], ACT.Exp, scale=-1.0).then_inc(g.qk_exp.sem, 1)
                    if s[0] == "kt":
                        i = s[1]
                        act.wait_ge(g.aa_fill.sem, g.aa_fill.done(q, aa_use[s] + 1))
                        act.wait_ge(g.kv_fill.sem, g.kv_fill.before(q, NT - 1))
                        act.activation(ktok[:, i, :], ps_act[:, 0:C], ACT.Copy).then_inc(g.aa_drain.sem, 1)
                    if s[0] == "oE":
                        i = s[1]
                        act.wait_ge(g.pv.sem, g.pv.done(q, i + 1))
                        if i >= 2:
                            act.wait_ge(g.ad_drain.sem, g.ad_drain.done(q, ad_use[("oT", i - 2)] + 1))
                        else:
                            act.wait_ge(g.ad_drain.sem, g.ad_drain.before(q, ad_use[("oT", i + 2)] + 1))
                        act.activation(oS[:, i % 2].rearrange("p l t -> p (l t)"), ps_o, ACT.Copy).then_inc(g.o_out.sem, 1)
                    if s[0] == "oC":
                        i = s[1]
                        act.wait_ge(g.aa_fill.sem, g.aa_fill.done(q, aa_use[s] + 1))
                        if i >= 2:
                            act.wait_ge(g.ad_fill.sem, g.ad_fill.done(q, ad_use[("pr", i - 2)] + 1))
                        else:
                            act.wait_ge(g.ad_fill.sem, g.ad_fill.before(q, ad_use[("pr", i + 2)] + 1))
                        act.activation(oNT[:, i % 2].rearrange("p k t -> p (k t)"), ps_act[:, 0:KC * P],
                                       ACT.Copy).then_inc(g.aa_drain.sem, 1)

                act.wait_ge(ready, 2)
                program(act, step)

            @block.tensor
            def _(pe):
                bank = {}

                def free(name, q, signal, n):
                    for last, value in bank.get(name, []):
                        pe.wait_ge(last.sem, value)
                    bank[name] = [(signal, signal.done(q, n))]

                def enter(q):
                    for name, a, b in (("act", g.pa_drain, g.aa_drain), ("dve", g.pd_drain, g.ad_drain)):
                        bank[name] = [(a, a.done(q, a.per)), (b, b.before(q, b.per))]

                def step(q, s):
                    if s[0] == "hT":
                        k = s[1]
                        pe.wait_ge(g.xn.sem, g.xn.done(q, NT))
                        free("act", q, g.pa_drain, k + 1)
                        for i in range(NT):
                            last = pe.transpose(ps_act[:, i * P:(i + 1) * P], xn[:, i, k * P:(k + 1) * P], ident)
                        last.then_inc(g.pa_fill.sem, 1)
                    if s[0] == "qk":
                        n = s[1]
                        pe.wait_ge(g.pa_drain.sem, g.pa_drain.done(q, 2))
                        pe.wait_ge(g.qk_map.sem, g.qk_map.done(q, n - 1) if n >= 2 else g.qk_map.before(q, 4 + n - 1))
                        for k in range(KC):
                            last = pe.matmul(ps_qk[:, n % 2, :], w[:, k, n * P:(n + 1) * P], hT[:, k, :],
                                             start=k == 0, stop=k == KC - 1)
                        last.then_inc(g.qk_fill.sem, 1)
                    if s[0] == "v":
                        i = s[1]
                        free("dve", q, g.pd_drain, i + 1)
                        for k in range(KC):
                            last = pe.matmul(ps_dve[:, 0:C], hT[:, k, i * P:(i + 1) * P], w[:, k, 2 * C:3 * C],
                                             start=k == 0, stop=k == KC - 1)
                        last.then_inc(g.pd_fill.sem, 1)
                    if s[0] == "kt":
                        i = s[1]
                        pe.wait_ge(g.qk_map.sem, g.qk_map.done(q, 4))
                        free("act", q, g.aa_drain, aa_use[s] + 1)
                        for k in range(KC):
                            last = pe.transpose(ps_act[:, k * P:(k + 1) * P], kf[:, q.s, k, i * P:(i + 1) * P], ident)
                        last.then_inc(g.aa_fill.sem, 1)
                    if s[0] == "A":
                        _, i, r = s
                        n = a_use[s]
                        if i == 0 and r == 0:
                            pe.wait_ge(g.masked.sem, g.masked.done(q, 4))
                        pe.wait_ge(g.a_keep.sem, g.a_keep.done(q, n - 1) if n >= AR else g.a_keep.before(q, n_a + n - 1))
                        at, t = 32 * r, slice(i * P, (i + 1) * P)
                        for l in range(4):
                            last = pe.matmul(ps_a[:, n % AR, l * P:(l + 1) * P], kf[at:at + 32, q.s, l // 2, t],
                                             qm[at:at + 32, q.s, l // 2, l % 2, t], start=True, stop=True,
                                             tile_position=(at, 0))
                        last.then_inc(g.a_fill.sem, 1)
                    if s[0] == "KV":
                        i = s[1]
                        pe.wait_ge(g.aa_drain.sem, g.aa_drain.done(q, aa_use[("kt", i)] + 1))
                        pe.wait_ge(g.kv_copy.sem, g.kv_copy.done(q, i) if i else g.kv_copy.before(q, NT - 1))
                        pe.wait_ge(g.pd_drain.sem, g.pd_drain.done(q, NT))
                        for k in range(KC):
                            last = pe.matmul(ps_kv[:, k * 2 * P:(k + 1) * 2 * P], ktok[:, i, k * P:(k + 1) * P],
                                             v32[:, q.s, i, 8 * k:8 * k + 8, :].rearrange("p h d -> p (h d)"),
                                             start=i == 0 and k == 0, stop=True, skip_group_check=True)
                        last.then_inc(g.kv_fill.sem, 1)
                    if s[0] == "PV":
                        i = s[1]
                        pe.wait_ge(g.a_keep.sem, g.a_keep.done(q, a_use[("A", i, 3)] + 1))
                        pe.wait_ge(g.o_out.sem, g.o_out.done(q, i) if i else g.o_out.before(q, NT))
                        if i:
                            pe.wait_ge(g.kv_copy.sem, g.kv_copy.done(q, i))
                            for hg in range(HG):
                                pe.matmul(ps_o[:, hg * P:(hg + 1) * P], state[:, (i - 1) % 2, hg // 2, (hg % 2) * P:(hg % 2) * P + P],
                                          qs[:, q.s, hg // 2, i * P:(i + 1) * P], start=hg == 0, stop=False,
                                          skip_group_check=True)
                        for h in range(H):
                            hg, l = h // 4, h % 4
                            n = a_use[("A", i, h % 8 // 2)]
                            last = pe.matmul(ps_o[32 * l:32 * l + 32, hg * P:(hg + 1) * P], v32[:, q.s, i, h, :],
                                             kept[:, n % SR, 2 * (h // 8) + h % 2, :], start=i == 0 and hg == 0, stop=True,
                                             tile_position=(0, 32 * l), skip_group_check=True)
                        last.then_inc(g.pv.sem, 1)
                    if s[0] == "oT":
                        i = s[1]
                        pe.wait_ge(g.o_out.sem, g.o_out.done(q, i + 1))
                        free("dve", q, g.ad_drain, ad_use[s] + 1)
                        for hg in range(HG):
                            last = pe.transpose(ps_dve[:, hg * P:(hg + 1) * P], oS[:, i % 2, hg, :], ident)
                        last.then_inc(g.ad_fill.sem, 1)
                    if s[0] == "oC":
                        i = s[1]
                        pe.wait_ge(g.ad_drain.sem, g.ad_drain.done(q, ad_use[("oT", i)] + 1))
                        free("act", q, g.aa_drain, aa_use[s] + 1)
                        for k in range(KC):
                            last = pe.transpose(ps_act[:, k * P:(k + 1) * P], oN[:, i % 2, k * P:(k + 1) * P], ident)
                        last.then_inc(g.aa_fill.sem, 1)
                    if s[0] == "pr":
                        i = s[1]
                        pe.wait_ge(g.aa_drain.sem, g.aa_drain.done(q, aa_use[("oC", i)] + 1))
                        pe.wait_ge(g.gated.sem, g.gated.done(q, 1))
                        free("dve", q, g.ad_drain, ad_use[s] + 1)
                        for k in range(KC):
                            last = pe.matmul(ps_dve[:, 0:C], oNT[:, i % 2, k, :], gwo[:, q.s, k, :],
                                             start=k == 0, stop=k == KC - 1)
                        last.then_inc(g.ad_fill.sem, 1)

                pe.wait_ge(ready, 2)
                program(pe, step, enter)


CYCLES = 3


def coupling_orders():
    pro = [("ln",)] + [("hT", a, k) for a in range(2) for k in range(KC)] + [("g1",), ("g2",), ("g3",)]
    main = []
    for c in range(CYCLES):
        for kind in ("L1", "L2", "L3", "L4", "up"):
            main += [(kind, c, a) for a in range(2)]
    main += [("gate", a) for a in range(2)]
    main += [("oT", a, i) for a in range(2) for i in range(2)]
    return pro, main


class CouplingSignals:

    def __init__(self, new):
        n = 2 * CYCLES
        self.stats = new("cpl_stats", 2 * NT)
        self.moments = new("cpl_moments", 2 * NT)
        self.cols = new("cpl_mod_cols", 1)
        self.pool_steps = new("cpl_pool_steps", 2)
        self.xn = new("cpl_xn_ready", 2 * NT)
        self.pa_fill = new("cpl_act_bank_filled", 7)
        self.pa_drain = new("cpl_act_bank_drained", 7)
        self.coef = new("cpl_coefficients", 1)
        self.l1_fill = new("cpl_layer1_filled", 2 * n)
        self.l1 = new("cpl_layer1_ready", 2 * n)
        self.l2_fill = new("cpl_layer2_filled", n)
        self.l2 = new("cpl_layer2_ready", n)
        self.l3_fill = new("cpl_layer3_filled", n)
        self.l3 = new("cpl_layer3_ready", n)
        self.l4_fill = new("cpl_layer4_filled", n)
        self.l4 = new("cpl_layer4_ready", n)
        self.steps = new("cpl_vector_steps", 2 * n)
        self.state = new("cpl_state_ready", 2 * n)
        self.gate = new("cpl_output_gated", 4)
        self.o_fill = new("cpl_output_turned", 4)
        self.o_done = new("cpl_output_ready", 4)
        self.store = new("cpl_output_stored", 16 * 4)


def coupling_phase(nc, m):
    pro, main = coupling_orders()
    merged = mix([(s, False) for s in main], [(s, True) for s in pro], 0.1, 0.7)
    pa_use, _ = index_of(pro, ("hT", "g1", "g2", "g3"))
    g = m.cpl
    R = B // 2
    with ExitStack() as ctx:
        def sb(name, shape, dt=F32):
            return ctx.enter_context(nc.sbuf_tensor(name, shape, dt))

        def sem(name):
            return ctx.enter_context(nc.semaphore(name))

        w1 = sb("c_w1", [P, KC, C])
        w2 = sb("c_w2", [P, KC, P])
        w34 = sb("c_w34", [P, 64])
        w4 = sb("c_w4", [64, P])
        g1w = sb("c_g1", [P, KC, P])
        g2w = sb("c_g2", [P, 64])
        g3w = sb("c_g3", [64, P])
        bias = sb("c_bias", [P, 9])
        half = sb("c_half", [P, 4])
        mhalf = sb("c_mhalf", [P, 2 * NT])
        nsgn = sb("c_nsgn", [P, 1])
        x_in = sb("c_x", [P, 2, 2, NT, C])
        cols = sb("c_cols", [P, 2, 6, 2])
        bst = sb("c_bst", [P, 2 * NT, 6])
        mv = sb("c_mv", [P, 2 * NT, 2])
        rstd = sb("c_rstd", [P, 2 * NT])
        vtmp = sb("c_vtmp", [P, 2 * NT])
        xn = sb("c_xn", [P, 2 * NT, C])
        o = sb("c_state", [P, 2, 2, KC, T])
        sums = sb("c_sums", [P, KC, 2])
        gs1 = sb("c_gs1", [P, 2])
        gs2 = sb("c_gs2", [64, 2])
        gs3 = sb("c_gs3", [P, 2])
        coef = sb("c_coef", [P, 2, 2])
        a1 = sb("c_a1", [P, 2, KC, T])
        a2 = sb("c_a2", [P, 2, T])
        a3 = sb("c_a3", [64, 2, T])
        th = sb("c_th", [P, 2, T])
        cc = sb("c_cc", [P, 2, T])
        uv = sb("c_uv", [P, 2, 2, T])
        og = sb("c_og", [P, 2, KC, T])
        ot = sb("c_ot", [P, 2, 2, 2, C])
        ps_1 = m.psum[:, 0:4, :].rearrange("p (a o) t -> p a o t", a=2)
        ps_2 = m.psum[:, 4:6, :]
        ps_act = m.psum[:, 6, :]
        ps_dve = m.psum[:, 7, :]
        ident = m.const[:, C_IDENT:C_IDENT + P]
        sgn = m.const[:, C_SGN:C_SGN + 1]
        w_loaded = sem("cpl_weights_loaded")
        ready = sem("cpl_constants_ready")
        in_loaded = [sem(f"cpl_inputs_loaded{s}") for s in range(2)]

        def ca(c, a):
            return 2 * c + a

        def program(eng, step):
            def one(q, last=False):
                for s, following in merged:
                    if not following:
                        step(q, s)
                    elif not last:
                        step(q.next(), s)

            for s in pro:
                step(Seq(0, 0), s)
            with eng.Fori(0, R // 2 - 1) as it:
                one(Seq(it, 0))
                one(Seq(it, 1))
            one(Seq(R // 2 - 1, 0))
            one(Seq(R // 2 - 1, 1), last=True)

        with nc.Block() as block:
            @block.sync
            def _(sp):
                for dst, src in ((w1, m.d["c1"]), (w2, m.d["c2"]), (w34, m.d["c3"]), (w4, m.d["c4"]), (g1w, m.d["g1"]),
                                 (g2w, m.d["g2"]), (g3w, m.d["g3"]), (bias, m.d["cb"])):
                    sp.dma_start(dst[:], src).then_inc(w_loaded, 16)

                def step(q, s):
                    if s[0] == "ln":
                        sp.wait_ge(g.o_done.sem, g.o_done.before(q, 4, 2))
                        sp.dma_start(x_in[:, q.s].rearrange("p a i c -> p (a i) c"),
                                     m.x3_d[bass.ds(q.n * 2 * NT, 2 * NT)].rearrange("i p c -> p i c")).then_inc(in_loaded[q.s], 16)
                    if s[0] == "oT":
                        _, a, i = s
                        sp.wait_ge(g.o_done.sem, g.o_done.done(q, 2 * a + i + 1))
                        sp.dma_start(m.out_t[bass.ds(q.n * 2 * NT + a * NT + 2 * i, 2)].rearrange("i p c -> p i c"),
                                     ot[:, a, i]).then_inc(g.store.sem, 16)

                program(sp, step)
                sp.wait_ge(g.store.sem, g.store.done(Seq(R // 2 - 1, 1), g.store.per))

            @block.gpsimd
            def _(pool):
                chain = Chain(pool, g.pool_steps, m.passed)

                def step(q, s):
                    if s[0] == "ln":
                        chain.start(q)
                        pool.wait_ge(g.moments.sem, g.moments.done(q, 2 * NT))
                        pool.wait_ge(g.pa_drain.sem, g.pa_drain.before(q, 7))
                        settle(pool, m.passed)
                        chain.link(pool.tensor_scalar(vtmp[:], mv[:, :, 1], EPS, None, ALU.add))
                        chain.link(pool.tensor_tensor(rstd[:], vtmp[:], mhalf[:], ALU.pow))
                        for i in range(2 * NT):
                            pool.tensor_scalar(xn[:, i, :], x_in[:, q.s, i // NT, i % NT, :], mv[:, i, 0:1], rstd[:, i:i + 1],
                                               ALU.subtract, ALU.mult).then_inc(g.xn.sem, 1)
                        chain.end()

                pool.wait_ge(ready, 1)
                program(pool, step)

            @block.vector
            def _(dve):
                chain = Chain(dve, g.steps, m.passed)

                def step(q, s):
                    if s[0] == "ln":
                        dve.wait_ge(in_loaded[q.s], q.it * 16 + 16)
                        dve.wait_ge(g.gate.sem, g.gate.before(q, 4, 2))
                        dve.tensor_copy(cols[:, q.s], m.modT[:, 1, 6:12, bass.ds(q.n * 2, 2)]).then_inc(g.cols.sem, 1)
                        for i in range(2 * NT):
                            dve.bn_stats(bst[:, i, :], x_in[:, q.s, i // NT, i % NT, :]).then_inc(g.stats.sem, 1)
                        dve.wait_ge(g.stats.sem, g.stats.done(q, 2 * NT))
                        dve.wait_ge(g.xn.sem, g.xn.before(q, 2 * NT))
                        settle(dve, m.passed)
                        for i in range(2 * NT):
                            dve.bn_aggr(mv[:, i, :], bst[:, i, :]).then_inc(g.moments.sem, 1)
                    if s[0] == "g3":
                        dve.wait_ge(g.pa_drain.sem, g.pa_drain.done(q, pa_use[s] + 1))
                        dve.tensor_scalar(coef[:, q.s, :], gs3[:], half[:, 3:4], 0.1, ALU.mult, ALU.add).then_inc(g.coef.sem, 1)
                    if s[0] == "up":
                        _, c, a = s
                        n = ca(c, a)
                        if n == 0:
                            chain.start(q)
                            dve.wait_ge(g.coef.sem, g.coef.done(q, 1))
                        dve.wait_ge(g.l4.sem, g.l4.done(q, n + 1))
                        chain.link(dve.tensor_scalar(cc[:, a, :], th[:, a, :], half[:, 2:3], coef[:, q.s, a:a + 1], ALU.mult, ALU.add))
                        st = o[:, q.s, a]
                        dve.scalar_tensor_tensor(out=uv[:, a, 0, :], in0=st[:, 1, :], scalar=sgn, in1=cc[:, a, :],
                                                 op0=ALU.mult, op1=ALU.mult)
                        chain.link(dve.scalar_tensor_tensor(out=uv[:, a, 1, :], in0=st[:, 0, :], scalar=nsgn[:, 0:1], in1=cc[:, a, :],
                                                            op0=ALU.mult, op1=ALU.mult))
                        for k in range(KC):
                            dve.tensor_tensor(st[:, k, :], st[:, k, :], uv[:, a, k, :], ALU.add).then_inc(g.state.sem, 1)
                        dve.wait_ge(g.state.sem, g.state.done(q, 2 * n + 2))
                        if n == 2 * CYCLES - 1:
                            chain.end()
                    if s[0] == "oT":
                        _, a, i = s
                        n = 2 * a + i
                        dve.wait_ge(g.o_fill.sem, g.o_fill.done(q, n + 1))
                        dve.wait_ge(g.store.sem, g.store.before(q, 16 * 4))
                        dve.tensor_tensor(ot[:, a, i].rearrange("p i c -> p (i c)"), ps_dve,
                                          x_in[:, q.s, a, 2 * i:2 * i + 2, :].rearrange("p i c -> p (i c)"),
                                          ALU.add).then_inc(g.o_done.sem, 1)

                dve.wait_ge(w_loaded, 8 * 16)
                dve.tensor_scalar(nsgn[:], sgn, -1.0, None, ALU.mult)
                dve.tensor_scalar(half[:, 0:1], bias[:, 4:5], 0.5, None, ALU.mult)
                dve.tensor_scalar(half[:, 1:2], bias[:, 7:8], 0.5, None, ALU.mult)
                dve.tensor_scalar(half[:, 2:3], bias[:, 8:9], 0.3, None, ALU.mult)
                dve.tensor_scalar(half[:, 3:4], bias[:, 8:9], 0.7, None, ALU.mult)
                dve.memset(mhalf[:], -0.5).then_inc(ready, 1)
                dve.wait_ge(ready, 1)
                program(dve, step)

            @block.scalar
            def _(act):
                def step(q, s):
                    if s[0] == "hT":
                        _, a, k = s
                        act.wait_ge(g.pa_fill.sem, g.pa_fill.done(q, pa_use[s] + 1))
                        act.wait_ge(g.cols.sem, g.cols.done(q, 1))
                        act.activation(o[:, q.s, a, k, :], ps_act, ACT.Identity, bias=cols[:, q.s, k, a:a + 1],
                                       scale=cols[:, q.s, KC + k, a:a + 1], accum_out=sums[:, k, a:a + 1]).then_inc(g.pa_drain.sem, 1)
                    if s[0] == "g1":
                        act.wait_ge(g.pa_fill.sem, g.pa_fill.done(q, pa_use[s] + 1))
                        act.activation(gs1[:], ps_act[:, 0:2], ACT.Gelu, bias=bias[:, 5:6], scale=1.0 / T).then_inc(g.pa_drain.sem, 1)
                    if s[0] == "g2":
                        act.wait_ge(g.pa_fill.sem, g.pa_fill.done(q, pa_use[s] + 1))
                        act.activation(gs2[:], ps_act[0:64, 0:2], ACT.Gelu, bias=bias[0:64, 6:7]).then_inc(g.pa_drain.sem, 1)
                    if s[0] == "g3":
                        act.wait_ge(g.pa_fill.sem, g.pa_fill.done(q, pa_use[s] + 1))
                        act.wait_ge(g.coef.sem, g.coef.before(q, 1))
                        act.activation(gs3[:], ps_act[:, 0:2], ACT.Tanh, bias=half[:, 1:2], scale=0.5).then_inc(g.pa_drain.sem, 1)
                    if s[0] == "L1":
                        _, c, a = s
                        n = ca(c, a)
                        for k in range(KC):
                            act.wait_ge(g.l1_fill.sem, g.l1_fill.done(q, 2 * n + k + 1))
                            act.activation(a1[:, a, k, :], ps_1[:, a, k, :], ACT.Gelu, bias=bias[:, k:k + 1]).then_inc(g.l1.sem, 1)
                    if s[0] == "L2":
                        _, c, a = s
                        act.wait_ge(g.l2_fill.sem, g.l2_fill.done(q, ca(c, a) + 1))
                        act.activation(a2[:, a, :], ps_2[:, a, :], ACT.Gelu, bias=bias[:, 2:3]).then_inc(g.l2.sem, 1)
                    if s[0] == "L3":
                        _, c, a = s
                        act.wait_ge(g.l3_fill.sem, g.l3_fill.done(q, ca(c, a) + 1))
                        act.activation(a3[:, a, :], ps_2[0:64, a, :], ACT.Gelu, bias=bias[0:64, 3:4]).then_inc(g.l3.sem, 1)
                    if s[0] == "L4":
                        _, c, a = s
                        act.wait_ge(g.l4_fill.sem, g.l4_fill.done(q, ca(c, a) + 1))
                        act.activation(th[:, a, :], ps_2[:, a, :], ACT.Tanh, bias=half[:, 0:1], scale=0.5).then_inc(g.l4.sem, 1)
                    if s[0] == "gate":
                        a = s[1]
                        act.wait_ge(g.state.sem, g.state.done(q, 2 * ca(CYCLES - 1, a) + 2))
                        act.wait_ge(g.o_fill.sem, g.o_fill.before(q, 4))
                        for k in range(KC):
                            act.activation(og[:, a, k, :], o[:, q.s, a, k, :], ACT.Copy,
                                           scale=cols[:, q.s, 2 * KC + k, a:a + 1]).then_inc(g.gate.sem, 1)

                act.wait_ge(ready, 1)
                program(act, step)

            @block.tensor
            def _(pe):
                def step(q, s):
                    if s[0] in ("hT", "g1", "g2", "g3"):
                        n = pa_use[s]
                        pe.wait_ge(g.pa_drain.sem, g.pa_drain.done(q, n) if n else g.pa_drain.before(q, 7))
                    if s[0] == "hT":
                        _, a, k = s
                        pe.wait_ge(g.xn.sem, g.xn.done(q, NT * (a + 1)))
                        for i in range(NT):
                            last = pe.transpose(ps_act[:, i * P:(i + 1) * P], xn[:, a * NT + i, k * P:(k + 1) * P], ident)
                        last.then_inc(g.pa_fill.sem, 1)
                    if s[0] == "g1":
                        for k in range(KC):
                            last = pe.matmul(ps_act[:, 0:2], g1w[:, k, :], sums[:, k, :], start=k == 0, stop=k == KC - 1)
                        last.then_inc(g.pa_fill.sem, 1)
                    if s[0] == "g2":
                        pe.matmul(ps_act[0:64, 0:2], g2w[:], gs1[:], start=True, stop=True).then_inc(g.pa_fill.sem, 1)
                    if s[0] == "g3":
                        pe.matmul(ps_act[:, 0:2], g3w[:], gs2[:], start=True, stop=True).then_inc(g.pa_fill.sem, 1)
                    if s[0] == "L1":
                        _, c, a = s
                        n = ca(c, a)
                        if c:
                            pe.wait_ge(g.state.sem, g.state.done(q, 2 * ca(c - 1, a) + 2))
                            pe.wait_ge(g.l1.sem, g.l1.done(q, 2 * ca(c - 1, a) + 2))
                        else:
                            pe.wait_ge(g.pa_drain.sem, g.pa_drain.done(q, pa_use[("hT", a, 1)] + 1))
                            pe.wait_ge(g.l1.sem, g.l1.before(q, 2 * ca(CYCLES - 1, a) + 2))
                        for h in range(KC):
                            for k in range(KC):
                                last = pe.matmul(ps_1[:, a, h, :], w1[:, k, h * P:(h + 1) * P], o[:, q.s, a, k, :],
                                                 start=k == 0, stop=k == KC - 1)
                            last.then_inc(g.l1_fill.sem, 1)
                    if s[0] == "L2":
                        _, c, a = s
                        n = ca(c, a)
                        pe.wait_ge(g.l4.sem, g.l4.done(q, n - 1) if c else g.l4.before(q, ca(CYCLES - 1, a) + 1))
                        for k in range(KC):
                            pe.wait_ge(g.l1.sem, g.l1.done(q, 2 * n + k + 1))
                            last = pe.matmul(ps_2[:, a, :], w2[:, k, :], a1[:, a, k, :], start=k == 0, stop=k == KC - 1)
                        last.then_inc(g.l2_fill.sem, 1)
                    if s[0] == "L3":
                        _, c, a = s
                        pe.wait_ge(g.l2.sem, g.l2.done(q, ca(c, a) + 1))
                        pe.matmul(ps_2[0:64, a, :], w34[:], a2[:, a, :], start=True, stop=True).then_inc(g.l3_fill.sem, 1)
                    if s[0] == "L4":
                        _, c, a = s
                        pe.wait_ge(g.l3.sem, g.l3.done(q, ca(c, a) + 1))
                        pe.matmul(ps_2[:, a, :], w4[:], a3[:, a, :], start=True, stop=True).then_inc(g.l4_fill.sem, 1)
                    if s[0] == "oT":
                        _, a, i = s
                        n = 2 * a + i
                        pe.wait_ge(g.gate.sem, g.gate.done(q, 2 * a + 2))
                        pe.wait_ge(g.o_done.sem, g.o_done.done(q, n) if n else g.o_done.before(q, 4))
                        for t in range(2):
                            for k in range(KC):
                                last = pe.transpose(ps_dve[:, (2 * t + k) * P:(2 * t + k + 1) * P],
                                                    og[:, a, k, (2 * i + t) * P:(2 * i + t + 1) * P], ident)
                        last.then_inc(g.o_fill.sem, 1)

                pe.wait_ge(ready, 1)
                program(pe, step)


INPUTS = {
    "const": (P, C_END), "x": (B * NT, P, C), "cT": (P, 2, KC, B), "wmod": (P, 2, KC, 6 * C),
    "wqkv": (P, KC, C + 2 * HD), "bqkv": (P, C + 2 * HD), "wo": (P, KC, C), "bo": (P, C),
    "wg": (P, KC, E), "bg": (E, 1), "eb": (P, E, 3), "ew": (E, P, 3 * KC * C),
    "lw": (P, KC, 3 * C), "lwo": (P, KC, C), "lbo": (P, C), "lbv": (P, C), "lbqk": (P, 4),
    "c1": (P, KC, C), "c2": (P, KC, P), "c3": (P, 64), "c4": (64, P),
    "g1": (P, KC, P), "g2": (P, 64), "g3": (64, P), "cb": (P, 9),
}


class Shared:
    pass


def build(nc, d, out):
    m = Shared()
    m.d, m.primed = d, []
    with ExitStack() as ctx:
        def new(name, per):
            signal = Signal(ctx.enter_context(nc.semaphore(name)), per)
            m.primed.append(signal)
            return signal

        def sb(name, shape, dt=F32):
            return ctx.enter_context(nc.sbuf_tensor(name, shape, dt))

        def dram(name, shape):
            return nc.dram_tensor(name, shape, F32, kind="Internal").ap()

        m.passed = ctx.enter_context(nc.semaphore("waits_passed"))
        m.att = AttentionSignals(new)
        m.exp = ExpertSignals(new)
        m.lin = LinearSignals(new)
        m.cpl = CouplingSignals(new)
        m.out_t = out.rearrange("b (i p) c -> (b i) p c", p=P)
        m.const = sb("const_sb", [P, C_END])
        m.ident_bf = sb("ident_bf", [P, P], BF16)
        m.negs_bf = sb("negs_bf", [P, P], BF16)
        m.negt_bf = sb("negt_bf", [P, P], BF16)
        m.modT = sb("modT", [P, 2, 12, B])
        m.psum = ctx.enter_context(nc.psum_tensor("psum", [P, 8, 512], F32))
        m.mod_rows = dram("mod_rows", (2, B, 6 * C))
        m.x1_d = dram("residual", (B * NT, P, C))
        m.h2_d = dram("router_input", (B * NT, P, C))
        m.lg_d = dram("router_logits", (B, E, T))
        m.x3_d = dram("x3_dram", (B * NT, P, C))
        with ExitStack() as inner:
            m.k6T = inner.enter_context(nc.sbuf_tensor("k6T", [6 * HD + 3, 2, T], BF16))
            m.v32 = inner.enter_context(nc.sbuf_tensor("v32", [P, 2, NT, 32], F32))
            m.mhalf = inner.enter_context(nc.sbuf_tensor("mhalf", [P, NT], F32))
            setup_phase(nc, m)
            attention_phase(nc, m)
        with ExitStack() as inner:
            m.idx_e = inner.enter_context(nc.sbuf_tensor("idx_e", [P, E, 4], U32))
            m.par_e = inner.enter_context(nc.sbuf_tensor("par_e", [P, E, 11], F32))
            m.gb_rows = inner.enter_context(nc.sbuf_tensor("gb_rows", [P, 4, C], F32))
            routing_phase(nc, m)
            expert_phase(nc, m)
        linear_phase(nc, m)
        coupling_phase(nc, m)


def halves(w):
    return w.reshape(KC, P, -1).transpose(1, 0, 2)


def pack(i):
    def rows(v, n=P):
        return np.broadcast_to(np.asarray(v).reshape(1, -1), (n, np.asarray(v).size))

    def columns(*vectors):
        c = np.zeros((P, len(vectors)), np.float32)
        for n, v in enumerate(vectors):
            c[:v.size if v.size > 1 else P, n] = v
        return c

    i = {k: np.asarray(v) for k, v in i.items()}
    return {
        "const": shape_constants(),
        "x": i["L0_attn_x"].reshape(B * NT, P, C),
        "cT": np.stack([i[f"L{n}_c"].T.reshape(KC, P, B) for n in range(2)]).transpose(2, 0, 1, 3),
        "wmod": np.stack([halves(i[f"L{n}_wmod"]) for n in range(2)], axis=1),
        "wqkv": halves(np.concatenate([i["L0_attn_Wq"], i["L0_attn_Wk"], i["L0_attn_Wv"]], axis=1)),
        "bqkv": rows(np.concatenate([i["L0_attn_bq"], i["L0_attn_bk"], i["L0_attn_bv"]])),
        "wo": halves(i["L0_attn_Wo"]), "bo": rows(i["L0_attn_bo"]),
        "wg": halves(i["L0_ffn_Wg"]), "bg": i["L0_ffn_bg"].reshape(E, 1),
        "eb": np.broadcast_to(np.stack([i[f"L0_ffn_b{n}"][:, 0] for n in (1, 2, 3)], axis=1)[None], (P, E, 3)),
        "ew": np.stack([i[f"L0_ffn_w{n}"].reshape(E, KC, P, C).transpose(0, 2, 1, 3) for n in (1, 2, 3)],
                       axis=2).reshape(E, P, 3 * KC * C),
        "lw": halves(i["L1_attn_qkv_w"]), "lwo": halves(i["L1_attn_out_w"]), "lbo": rows(i["L1_attn_out_b"]),
        "lbv": rows(i["L1_attn_qkv_b"][2 * C:]), "lbqk": i["L1_attn_qkv_b"][:2 * C].reshape(4, P).T,
        "c1": halves(i["L1_ffn_cn_w1"]), "c2": halves(i["L1_ffn_cn_w2"]), "c3": i["L1_ffn_cn_w3"],
        "c4": np.broadcast_to(i["L1_ffn_cn_w4"], (64, P)),
        "g1": halves(i["L1_ffn_gc_w1"]), "g2": i["L1_ffn_gc_w2"], "g3": np.broadcast_to(i["L1_ffn_gc_w3"], (64, P)),
        "cb": columns(i["L1_ffn_cn_b1"][:P], i["L1_ffn_cn_b1"][P:], i["L1_ffn_cn_b2"], i["L1_ffn_cn_b3"],
                      i["L1_ffn_cn_b4"], i["L1_ffn_gc_b1"], i["L1_ffn_gc_b2"], i["L1_ffn_gc_b3"],
                      i["L1_ffn_adaptive_range"]),
    }


def kernel(**inputs):
    import concourse.bacc as bacc
    from concourse.bass_utils import run_bass_kernel_spmd

    nc = bacc.Bacc("TRN2", target_bir_lowering=False, num_devices=1)
    arrays, d = {}, {}
    for name, a in pack(inputs).items():
        assert a.shape == INPUTS[name], (name, a.shape)
        arrays[f"in_{name}"] = np.ascontiguousarray(a, dtype=np.float32)
        d[name] = nc.dram_tensor(f"in_{name}", a.shape, F32, kind="ExternalInput").ap()
    out = nc.dram_tensor("out_0", (B, T, C), F32, kind="ExternalOutput").ap()
    build(nc, d, out)
    r = run_bass_kernel_spmd(nc, [arrays], core_ids=[0])
    return r.results[0]["out_0"]
```

```python
from contextlib import ExitStack

import numpy as np
import concourse.bass as bass
from concourse import mybir

F32 = mybir.dt.float32
BF16 = mybir.dt.bfloat16
U32 = mybir.dt.uint32
ALU = mybir.AluOpType
ACT = mybir.ActivationFunctionType
AX_X = mybir.AxisListType.X

P = 128
B, T, C = 8, 512, 256
NT = T // P
KC = C // P
H, HD = 16, 16
E, TOPK = 16, 64
EPS = 1e-5
NEG = -1e30
ROWS, ROW_GATE_A, ROW_SHIFT_B, ROW_SCALE_B, ROW_GATE_B, ROW_GATE_L1 = 5, 0, 1, 2, 3, 4
HG = 4
C_IDENT, C_NEGS, C_NEGT, C_KEEP, C_BD, C_SEQ, C_SGN, C_PARITY, C_ROPE = 0, 128, 256, 384, 512, 768, 769, 770, 772
C_END = C_ROPE + NT * 2 * HD


def shape_constants():
    c = np.zeros((P, C_END), np.float32)
    i = np.arange(P)
    c[:, C_IDENT:C_IDENT + P] = np.eye(P)
    c[:, C_NEGS:C_NEGS + P] = np.where(i[None, :] > i[:, None], NEG, 0)
    c[:, C_NEGT:C_NEGT + P] = np.where(i[None, :] < i[:, None], NEG, 0)
    c[:, C_KEEP:C_KEEP + P] = (i[None, :] >= i[:, None])
    col = np.arange(256)
    c[:, C_BD:C_BD + 256] = (i[:, None] // HD == col[None, :] // 32) & (col[None, :] % 32 <= HD)
    c[:, C_SEQ] = (i // E) * T
    c[:, C_SGN] = np.where(i < P // 2, 1, -1)
    c[:, C_PARITY] = i // HD % 2 == 0
    c[:, C_PARITY + 1] = i // HD % 2 == 1
    pos = np.arange(T, dtype=np.float32)
    freqs = (np.float32(1.0) / np.float32(10000.0) ** (np.arange(0, HD, 2, dtype=np.float32) / np.float32(HD)))
    ang = (pos[:, None] * freqs[None, :].astype(np.float32)).astype(np.float32)
    sin, cos = np.sin(ang), np.cos(ang)
    rope = np.concatenate([cos, -cos, sin, sin], axis=1).reshape(NT, P, 2 * HD)
    c[:, C_ROPE:] = rope.transpose(1, 0, 2).reshape(P, -1)
    return c


class Seq:

    def __init__(self, it, s):
        self.it, self.s, self.n = it, s, it * 2 + s

    def next(self):
        return Seq(self.it, 1) if self.s == 0 else Seq(self.it + 1, 0)


class Signal:

    def __init__(self, sem, per):
        self.sem, self.per = sem, per

    def done(self, q, n):
        return q.n * self.per + 2 * self.per + n

    def before(self, q, n, back=1):
        return q.n * self.per + (2 - back) * self.per + n


def settle(eng, passed):
    eng.sem_inc(passed, 1)


class Chain:

    def __init__(self, eng, signal, passed):
        self.eng, self.counter, self.passed, self.q, self.n = eng, signal, passed, None, 0

    def start(self, q):
        self.q, self.n = q, 0

    def go_on(self, q):
        self.q = q

    def link(self, ins):
        self.n += 1
        ins.then_inc(self.counter.sem, 1)
        self.eng.wait_ge(self.counter.sem, self.counter.done(self.q, self.n))
        settle(self.eng, self.passed)

    def end(self):
        assert self.n == self.counter.per, (self.n, self.counter.per)


S_HEADS = [4, 2, 1, 1]


def prologue_order():
    pause = [("pause",)]
    head = [("ln",)] + 3 * pause + [("st", i) for i in range(NT)] + [("ag",)] + 2 * pause + [("xn", i) for i in range(NT)]
    head += [("hT", 0), ("hT", 1), ("qkv", 0), ("qkv", 1)]
    for i in range(2, NT):
        head += [("qkv", i), ("sp", i - 2)]
    head += [("sp", NT - 2)] + pause + [("sp", NT - 1)] + pause + [("kT",)]
    head += [("qT", i, half) for i in range(2) for half in range(2)]
    late = [("qT", i, half) for i in (2, 3) for half in range(2)]
    return head, mix(scores_order(0) + scores_order(1), late)


def mix(a, b, start=0.0, end=1.0):
    out, n = [], 0
    for k, s in enumerate(a):
        out.append(s)
        while n < len(b) and len(a) * (start + (end - start) * (n + 1) / (len(b) + 1)) <= k + 1:
            out.append(b[n])
            n += 1
    return out + b[n:]


def scores_order(i):
    return [("S", i, u) for u in range(H // S_HEADS[i])]


def probs_order(i):
    steps = []
    for j in range(i + 1):
        steps += [("ST", i, j, g) for g in range(HG)]
        if j:
            steps.append(("PV", i, j - 1))
    return steps + [("PV", i, i), ("oE", i)]


def tail_order(i):
    return [("oT", i)] + ([("h2T", i - 1)] if i else []) + [("oC", i), ("pr", i)] + [("pause",), ("h2", i)]


def attention_order():
    first = probs_order(1)
    side = probs_order(0) + first[:3]
    main = [("mT", 0)] + mix(scores_order(2), [("mT", 1)] + side, 0.05)
    rest = mix(first[3:] + probs_order(2), tail_order(0), 0.5, 0.95)
    rest = rest[:3] + [("mT", 2)] + rest[3:]
    main += mix(scores_order(3), rest, 0.05)
    t = tail_order(1)
    tail = t[:1] + [("mT", 3)] + t[1:] + mix(probs_order(3), tail_order(2), 0.35, 0.95)
    return main, tail, tail_order(3) + [("h2T", 3), ("lg",)]


def attention_merged():
    def mark(steps, following):
        return [(s, following) for s in steps]

    main, tail, end = attention_order()
    head, late = prologue_order()
    return mix(mark(main, False), mark(head, True)) + (
        mix(mark(tail, False), mark(late[:5], True), 0.0)
        + mix(mark(end, False), mark(late[5:], True), 0.0, 0.95))


def index_of(order, kinds):
    steps = [s for s in order if s[0] in kinds]
    return {s: n for n, s in enumerate(steps)}, len(steps)


def setup_phase(nc, m):
    with ExitStack() as ctx:
        def sb(name, shape, dt=F32):
            return ctx.enter_context(nc.sbuf_tensor(name, shape, dt))

        def sem(name):
            return ctx.enter_context(nc.semaphore(name))

        cT = sb("cT", [P, 2, KC, B])
        wmod = sb("wmod", [P, 2, KC, 6 * C])
        eneg = sb("eneg", [P, 2, KC, B])
        silu = sb("silu", [P, 2, KC, B])
        rows = sb("rows", [B, ROWS * C])
        rtmp = sb("rtmp", [B, 2, C])
        ctmp = sb("ctmp", [P, 2, 2, 2, KC, B])
        ps_row = m.psum[0:B, 0:3, :].rearrange("b n f -> b (n f)")
        ps_col = m.psum[:, 6, 0:2 * 12 * B]
        loaded = sem("setup_loaded")
        c_loaded = sem("setup_c_loaded")
        w_loaded = [sem(f"setup_wmod_loaded{n}") for n in range(2)]
        exp_done = sem("setup_exp_done")
        silu_ready = sem("silu_ready")
        rows_ready = sem("mod_rows_psum")
        cols_ready = sem("mod_cols_psum")
        chain = sem("setup_vector_steps")
        rows_final = sem("mod_rows_final")
        stored = sem("mod_rows_stored")

        with nc.Block() as block:
            @block.sync
            def _(sp):
                sp.dma_start(cT[:], m.d["cT"]).then_inc(c_loaded, 16)
                for l in range(2):
                    sp.dma_start(wmod[:, l], m.d["wmod"][:, l]).then_inc(w_loaded[l], 16)
                sp.dma_start(m.const[:], m.d["const"]).then_inc(loaded, 16)
                for dst, src in m.att_weights:
                    sp.dma_start(dst[:], src).then_inc(m.att_w_loaded, 16)
                sp.dma_start(m.x_in[:, 0], m.d["x"][0:NT].rearrange("i p c -> p i c")).then_inc(m.in_loaded[0], 16)
                sp.wait_ge(rows_final, 1)
                sp.dma_start(m.mod_rows, rows[:]).then_inc(stored, 16)
                sp.wait_ge(stored, 16)

            @block.gpsimd
            def _(pool):
                for signal in m.primed:
                    pool.sem_inc(signal.sem, 2 * signal.per)

            @block.scalar
            def _(act):
                act.wait_ge(c_loaded, 16)
                act.activation(eneg[:], cT[:], ACT.Exp, scale=-1.0).then_inc(exp_done, 1)

            @block.tensor
            def _(pe):
                pe.wait_ge(silu_ready, 1)
                for l, first, place, width in ((0, 2, 0, 2), (0, 4, 2, 2), (1, 2, 4, 1)):
                    if first == 2:
                        pe.wait_ge(w_loaded[l], 16)
                    for k in range(KC):
                        last = pe.matmul(ps_row[:, place * C:(place + width) * C], silu[:, l, k, :],
                                         wmod[:, l, k, first * C:(first + width) * C], start=k == 0, stop=k == KC - 1)
                last.then_inc(rows_ready, 1)
                for l in range(2):
                    for j in range(12):
                        for k in range(KC):
                            last = pe.matmul(ps_col[:, (12 * l + j) * B:(12 * l + j + 1) * B],
                                             wmod[:, l, k, j * P:(j + 1) * P], silu[:, l, k, :],
                                             start=k == 0, stop=k == KC - 1)
                last.then_inc(cols_ready, 1)

            @block.vector
            def _(dve):
                count = [0]

                def link(ins):
                    count[0] += 1
                    ins.then_inc(chain, 1)
                    dve.wait_ge(chain, count[0])

                link(dve.memset(m.mhalf[:], -0.5))
                link(dve.memset(m.k6T[6 * HD:6 * HD + 3], 1.0))
                link(dve.memset(m.v32[:], 0.0))
                link(dve.memset(m.v32[:, :, :, HD:HD + 1], 1.0))
                dve.wait_ge(exp_done, 1)
                link(dve.tensor_scalar(eneg[:], eneg[:], 1.0, None, ALU.add))
                link(dve.reciprocal(eneg[:], eneg[:]))
                dve.tensor_tensor(silu[:], cT[:], eneg[:], ALU.mult).then_inc(silu_ready, 1)
                dve.wait_ge(loaded, 16)
                link(dve.tensor_copy(m.ident_bf[:], m.const[:, C_IDENT:C_IDENT + P]))
                link(dve.tensor_copy(m.negs_bf[:], m.const[:, C_NEGS:C_NEGS + P]))
                link(dve.tensor_copy(m.negt_bf[:], m.const[:, C_NEGT:C_NEGT + P]))
                dve.wait_ge(rows_ready, 1)
                link(dve.tensor_copy(rows[:], ps_row[:, 0:ROWS * C]))
                def scale(v):
                    link(dve.tensor_scalar(v, v, 1.0, None, ALU.add))

                def gate(v, tmp):
                    a, s = tmp
                    link(dve.scalar_tensor_tensor(out=a, in0=v, scalar=-1.0, in1=v, op0=ALU.mult, op1=ALU.max))
                    link(dve.tensor_scalar(a, a, 0.25, None, ALU.max))
                    link(dve.tensor_scalar(s, v, 0.0, 2.0, ALU.is_ge, ALU.mult))
                    link(dve.scalar_tensor_tensor(out=v, in0=s, scalar=-1.0, in1=a, op0=ALU.add, op1=ALU.mult))

                scale(rows[:, ROW_SCALE_B * C:(ROW_SCALE_B + 1) * C])
                for n in (ROW_GATE_A, ROW_GATE_B, ROW_GATE_L1):
                    gate(rows[:, n * C:(n + 1) * C], (rtmp[:, 0], rtmp[:, 1]))
                dve.sem_inc(rows_final, 1)
                dve.wait_ge(cols_ready, 1)
                link(dve.tensor_copy(m.modT[:].rearrange("p l j b -> p (l j b)"), ps_col))
                cv = m.modT[:].rearrange("p l (g v k) b -> p l g v k b", g=2, v=3)
                for l in range(2):
                    scale(cv[:, l, :, 1])
                    gate(cv[:, l, :, 2], (ctmp[:, 0, l], ctmp[:, 1, l]))


ATT_ACT = ("mT", "oC", "h2T", "lg")
ATT_DVE = ("oT", "pr")
PRO_ACT = ("hT", "kT", "qT")
PRO_DVE = ("qkv",)


class AttentionSignals:

    def __init__(self, new):
        def n(order, kinds):
            return index_of(order, kinds)[1]

        pro, att = sum(prologue_order(), []), sum(attention_order(), [])
        self.stats = new("att_stats", NT)
        self.moments = new("att_moments", NT)
        self.cols = new("att_mod_cols", 1)
        self.pool_pro = new("att_pool_prologue_steps", 1 + 3 + 3 + 3 * NT)
        self.pool_att = new("att_pool_steps", NT)
        self.dve_pro = new("att_vector_prologue_steps", 3 * NT)
        self.dve_att = new("att_vector_steps", 3 * NT)
        self.xn = new("att_xn_ready", NT)
        self.gated = new("att_gated_ready", 1)
        self.rope = new("att_rope_ready", NT)
        self.split = new("att_split_ready", NT)
        self.k6 = new("att_k6_ready", 1)
        self.first = new("att_first_parts_ready", NT)
        self.pa_fill = new("att_prologue_act_bank_filled", n(pro, PRO_ACT))
        self.pa_drain = new("att_prologue_act_bank_drained", n(pro, PRO_ACT))
        self.pd_fill = new("att_prologue_vector_bank_filled", n(pro, PRO_DVE))
        self.pd_drain = new("att_prologue_vector_bank_drained", n(pro, PRO_DVE))
        self.aa_fill = new("att_act_bank_filled", n(att, ATT_ACT))
        self.aa_drain = new("att_act_bank_drained", n(att, ATT_ACT))
        self.ad_fill = new("att_vector_bank_filled", n(att, ATT_DVE))
        self.ad_drain = new("att_vector_bank_drained", n(att, ATT_DVE))
        self.s_fill = new("att_scores_filled", n(pro + att, ("S",)))
        self.s_max = new("att_scores_maxed", n(pro + att, ("S",)))
        self.max_steps = new("att_max_split_steps", 3 * NT)
        self.msp = new("att_max_split", NT)
        self.t_fill = new("att_scoresT_filled", n(att, ("ST",)))
        self.probs = new("att_probs_ready", n(att, ("ST",)))
        self.pv = new("att_pv_done", n(att, ("PV",)))
        self.o_out = new("att_out_copied", NT)
        self.h2 = new("att_h2_ready", NT)
        self.rstd = new("att_rstd_ready", 1)
        self.moments2 = new("att_moments2", NT)
        self.rstd2 = new("att_rstd2_ready", NT)
        self.x1_store = new("att_x1_stored", 16 * NT)
        self.h2_store = new("att_h2_stored", 16 * NT)
        self.lg_store = new("att_logits_stored", 16)


def attention_phase(nc, m):
    pro, att = sum(prologue_order(), []), sum(attention_order(), [])
    merged = attention_merged()
    pa_use, _ = index_of(pro, PRO_ACT)
    aa_use, n_aa = index_of(att, ATT_ACT)
    pd_use, _ = index_of(pro, PRO_DVE)
    ad_use, _ = index_of(att, ATT_DVE)
    s_use, n_s = index_of(pro + att, ("S",))
    t_use, n_t = index_of(att, ("ST",))
    pv_use, n_pv = index_of(att, ("PV",))
    SR, TR, PR = 2, 2, 8
    assert n_s % SR == 0 and n_t % TR == 0 and n_t % PR == 0
    act_uses = [s for s, _ in merged if s[0] in PRO_ACT + ATT_ACT]
    assert len(act_uses) % 2 == 0
    act_bank = {s: n % 2 for n, s in enumerate(act_uses)}
    g = m.att
    with ExitStack() as ctx:
        def sb(name, shape, dt=F32):
            return ctx.enter_context(nc.sbuf_tensor(name, shape, dt))

        def sem(name):
            return ctx.enter_context(nc.semaphore(name))

        k6T, v32, mhalf = m.k6T, m.v32, m.mhalf
        wqkv, wo, wg, bqkv, bo, bg = (dst for dst, _ in m.att_weights)
        x_in, in_loaded, w_loaded = m.x_in, m.in_loaded, m.att_w_loaded
        rowb = sb("rowb", [P, 2, 3, C])
        cols = sb("cols", [P, 4])
        gwo = sb("gwo", [P, 2, KC, C])
        gbo = sb("gbo", [P, C])
        bst = sb("bst", [P, NT, 6])
        mv = sb("mv", [P, NT, 2])
        rstd = sb("rstd", [P, NT])
        vtmp = sb("vtmp", [P, NT])
        xn = sb("xn", [P, NT, C])
        hT = sb("hT", [P, KC, T])
        qkv = sb("qkv", [P, NT, C + 2 * HD])
        ra = sb("ra", [P, NT, H + 1, HD])
        rb = sb("rb", [P, NT, H + 1, HD])
        q6 = sb("q6", [P, NT, H + 1, 6, HD], BF16)
        k6 = sb("k6", [P, NT, 6 * HD], BF16)
        q6T = sb("q6T", [6 * HD + 3, 2, H, T], BF16)
        nmax = sb("nmax", [P, NT, H])
        mres = sb("mres", [P, NT, H])
        msp = sb("msp", [P, NT, 3, H], BF16)
        mT = sb("mT", [3 * H, NT, P], BF16)
        pT = sb("pT", [P, PR, 4, P])
        oS = sb("oS", [P, 2, 4, P])
        linv = sb("linv", [P, NT, H])
        oN = sb("oN", [P, 2, C])
        oNT = sb("oNT", [P, 2, KC, P])
        x1 = sb("x1", [P, NT, C])
        bst2 = sb("bst2", [P, NT, 6])
        mv2 = sb("mv2", [P, NT, 2])
        rstd2 = sb("rstd2", [P, NT])
        vtmp2 = sb("vtmp2", [P, NT])
        h2 = sb("h2", [P, NT, C])
        h2T = sb("h2T", [P, KC, T])
        lg = sb("lg", [E, T])
        ps_s = m.psum[:, 0:SR, :]
        ps_t = m.psum[:, SR:SR + TR, :]
        ps_o = m.psum[:, 4, :]
        ps_2act = m.psum[:, 5:7, :]
        ps_dve = m.psum[:, 7, :]
        ident = m.const[:, C_IDENT:C_IDENT + P]
        m_placed = [sem(f"att_max_rows_placed{i}") for i in range(NT)]

        def program(eng, step, enter=lambda q: None):
            def one(q, last=False):
                enter(q)
                for s, following in merged:
                    if not following:
                        step(q, s)
                    elif not last:
                        step(q.next(), s)

            for s in pro:
                step(Seq(0, 0), s)
            with eng.Fori(0, B // 2 - 1) as it:
                one(Seq(it, 0))
                one(Seq(it, 1))
            one(Seq(B // 2 - 1, 0))
            one(Seq(B // 2 - 1, 1), last=True)

        with nc.Block() as block:
            @block.sync
            def _(sp):
                def step(q, s):
                    if s[0] == "ln":
                        sp.wait_ge(g.ad_drain.sem, g.ad_drain.before(q, g.ad_drain.per, 2))
                        sp.wait_ge(g.h2.sem, g.h2.before(q, NT, 2))
                        if not (isinstance(q.n, int) and q.n == 0):
                            sp.dma_start(x_in[:, q.s], m.d["x"][bass.ds(q.n * NT, NT)].rearrange("i p c -> p i c")).then_inc(in_loaded[q.s], 16)
                        for n, r in enumerate((ROW_GATE_A, ROW_SCALE_B, ROW_SHIFT_B)):
                            sp.dma_start(rowb[:, q.s, n, :], m.mod_rows[bass.ds(q.n, 1), r * C:(r + 1) * C].to_broadcast([P, C])).then_inc(in_loaded[q.s], 16)
                    if s[0] == "mT":
                        i = s[1]
                        sp.wait_ge(g.aa_drain.sem, g.aa_drain.done(q, aa_use[s] + 1))
                        sp.dma_start(q6T[6 * HD:6 * HD + 3, q.s, :, i * P:(i + 1) * P],
                                     mT[:, i, :]).then_inc(m_placed[i], 16)
                    if s[0] == "h2T":
                        i = s[1]
                        sp.wait_ge(g.h2.sem, g.h2.done(q, i + 1))
                        sp.dma_start(m.x1_d[bass.ds(q.n * NT + i, 1)].rearrange("i p c -> p (i c)"), x1[:, i, :]).then_inc(g.x1_store.sem, 16)
                        sp.dma_start(m.h2_d[bass.ds(q.n * NT + i, 1)].rearrange("i p c -> p (i c)"), h2[:, i, :]).then_inc(g.h2_store.sem, 16)
                    if s[0] == "lg":
                        sp.wait_ge(g.aa_drain.sem, g.aa_drain.done(q, aa_use[s] + 1))
                        sp.dma_start(m.lg_d[bass.ds(q.n, 1)].rearrange("b e t -> (b e) t"), lg[:]).then_inc(g.lg_store.sem, 16)

                program(sp, step)
                end = Seq(B // 2 - 1, 1)
                for store in (g.x1_store, g.h2_store, g.lg_store):
                    sp.wait_ge(store.sem, store.done(end, store.per))

            @block.gpsimd
            def _(pool):
                pro_chain, att_chain = Chain(pool, g.pool_pro, m.passed), Chain(pool, g.pool_att, m.passed)

                def step(q, s):
                    if s[0] == "ag":
                        pro_chain.start(q)
                        link = pro_chain.link
                        pool.wait_ge(g.moments.sem, g.moments.done(q, NT))
                        settle(pool, m.passed)
                        pool.wait_ge(g.xn.sem, g.xn.before(q, NT))
                        settle(pool, m.passed)
                        link(pool.tensor_scalar(vtmp[:], mv[:, :, 1], EPS, None, ALU.add))
                        pool.tensor_tensor(rstd[:], vtmp[:], mhalf[:], ALU.pow).then_inc(g.rstd.sem, 1)
                    if s[0] == "kT":
                        link = pro_chain.link
                        link(pool.tensor_tensor(gbo[:], bo[:], rowb[:, q.s, 0, :], ALU.mult))
                        for k in range(KC):
                            link(pool.tensor_tensor(gwo[:, q.s, k, :], wo[:, k, :], rowb[:, q.s, 0, :], ALU.mult))
                        pool.wait_ge(g.xn.sem, g.xn.done(q, NT))
                        for i in range(NT):
                            ins = pool.tensor_tensor(x_in[:, q.s, i, :], x_in[:, q.s, i, :], gbo[:], ALU.add)
                            if i < NT - 1:
                                link(ins)
                            else:
                                ins.then_inc(g.gated.sem, 1)
                                pool.wait_ge(g.gated.sem, g.gated.done(q, 1))
                                settle(pool, m.passed)
                        pro_chain.end()
                    if s[0] == "qkv":
                        i = s[1]
                        link = pro_chain.link
                        pool.wait_ge(g.pd_drain.sem, g.pd_drain.done(q, pd_use[s] + 1))
                        settle(pool, m.passed)
                        pool.wait_ge(g.split.sem, g.split.before(q, NT))
                        settle(pool, m.passed)
                        tab = m.const[:, C_ROPE + i * 2 * HD:C_ROPE + (i + 1) * 2 * HD]
                        src = qkv[:, i, 0:C + HD].rearrange("p (h d) -> p h d", d=HD)
                        hh = HD // 2
                        pool.tensor_tensor(ra[:, i], src, tab[:, 0:HD].unsqueeze(1).to_broadcast([P, H + 1, HD]), ALU.mult)
                        for half in range(2):
                            a, c = half * hh, (1 - half) * hh
                            link(pool.tensor_tensor(rb[:, i, :, a:a + hh], src[:, :, c:c + hh],
                                                    tab[:, HD + a:HD + a + hh].unsqueeze(1).to_broadcast([P, H + 1, hh]), ALU.mult))
                        link(pool.tensor_copy(v32[:, q.s, i, 0:HD], qkv[:, i, C + HD:C + 2 * HD]))
                        pool.tensor_tensor(ra[:, i], ra[:, i], rb[:, i], ALU.add).then_inc(g.rope.sem, 1)
                        pool.wait_ge(g.rope.sem, g.rope.done(q, i + 1))
                        settle(pool, m.passed)
                    if s[0] == "pr":
                        i = s[1]
                        pool.wait_ge(g.moments2.sem, g.moments2.done(q, i + 1))
                        settle(pool, m.passed)
                        pool.wait_ge(g.h2.sem, g.h2.before(q, NT))
                        settle(pool, m.passed)
                        if i == 0:
                            att_chain.start(q)
                        att_chain.link(pool.tensor_scalar(vtmp2[:, i:i + 1], mv2[:, i, 1:2], EPS, None, ALU.add))
                        pool.tensor_tensor(rstd2[:, i:i + 1], vtmp2[:, i:i + 1], mhalf[:, 0:1], ALU.pow).then_inc(g.rstd2.sem, 1)
                        if i == NT - 1:
                            att_chain.end()

                def with_inputs(q, s):
                    if s[0] == "ag":
                        pool.wait_ge(in_loaded[q.s], q.it * 64 + 64)
                        settle(pool, m.passed)
                    step(q, s)

                pool.wait_ge(w_loaded, 6 * 16)
                program(pool, with_inputs)

            @block.vector
            def _(dve):
                pro_chain, att_chain = Chain(dve, g.dve_pro, m.passed), Chain(dve, g.dve_att, m.passed)
                max_chain = Chain(dve, g.max_steps, m.passed)

                def step(q, s):
                    if s == ("st", 0):
                        pro_chain.start(q)
                        dve.wait_ge(in_loaded[q.s], q.it * 64 + 64)
                        dve.wait_ge(g.pa_drain.sem, g.pa_drain.before(q, pa_use[("hT", 1)] + 1))
                        dve.tensor_copy(cols[:].unsqueeze(2), m.modT[:, 0, 0:4, bass.ds(q.n, 1)]).then_inc(g.cols.sem, 1)
                    if s[0] == "st":
                        dve.bn_stats(bst[:, s[1], :], x_in[:, q.s, s[1], :]).then_inc(g.stats.sem, 1)
                    if s[0] == "ag":
                        dve.wait_ge(g.stats.sem, g.stats.done(q, NT))
                        dve.wait_ge(g.xn.sem, g.xn.before(q, NT))
                        settle(dve, m.passed)
                        for i in range(NT):
                            dve.bn_aggr(mv[:, i, :], bst[:, i, :]).then_inc(g.moments.sem, 1)
                    if s[0] == "xn":
                        i = s[1]
                        dve.wait_ge(g.rstd.sem, g.rstd.done(q, 1))
                        dve.tensor_scalar(xn[:, i, :], x_in[:, q.s, i, :], mv[:, i, 0:1], rstd[:, i:i + 1],
                                          ALU.subtract, ALU.mult).then_inc(g.xn.sem, 1)
                    if s[0] == "qkv":
                        i = s[1]
                        dve.wait_ge(g.pd_fill.sem, g.pd_fill.done(q, pd_use[s] + 1))
                        dve.wait_ge(g.rope.sem, g.rope.before(q, NT))
                        dve.tensor_tensor(qkv[:, i, :], ps_dve[:, 0:C + 2 * HD], bqkv[:], ALU.add).then_inc(g.pd_drain.sem, 1)
                    if s[0] == "sp":
                        i = s[1]
                        link = pro_chain.link
                        dve.wait_ge(g.first.sem, g.first.done(q, i + 1))
                        link(dve.tensor_tensor(ra[:, i], ra[:, i], q6[:, i, :, 0, :], ALU.subtract))
                        link(dve.tensor_copy(q6[:, i, :, 3:5, :], ra[:, i].unsqueeze(2).to_broadcast([P, H + 1, 2, HD])))
                        link(dve.tensor_tensor(q6[:, i, :, 5, :], ra[:, i], q6[:, i, :, 3, :], ALU.subtract))
                        dve.sem_inc(g.split.sem, 1)
                        if i == NT - 1:
                            for place, part in enumerate((0, 3, 5, 0, 3, 0)):
                                ins = dve.tensor_copy(k6[:, :, place * HD:(place + 1) * HD], q6[:, :, H, part, :])
                            ins.then_inc(g.k6.sem, 1)
                            pro_chain.end()
                    if s[0] == "S":
                        _, i, u = s
                        nh, n = S_HEADS[i], s_use[s]
                        dve.wait_ge(g.s_fill.sem, g.s_fill.done(q, n + 1))
                        if u == 0:
                            dve.wait_ge(g.msp.sem, g.msp.before(q, i + 1))
                        dve.tensor_reduce(nmax[:, i, u * nh:(u + 1) * nh],
                                          ps_s[:, n % SR, 0:nh * (i + 1) * P].rearrange("p (h k) -> p h k", h=nh),
                                          AX_X, ALU.max, negate=True).then_inc(g.s_max.sem, 1)
                        if u == H // nh - 1:
                            if i == 0:
                                max_chain.start(q)
                            max_chain.go_on(q)
                            link = max_chain.link
                            dve.wait_ge(g.s_max.sem, g.s_max.done(q, n + 1))
                            dve.wait_ge(g.aa_drain.sem, g.aa_drain.before(q, aa_use[("mT", i)] + 1))
                            link(dve.tensor_copy(msp[:, i, 0, :], nmax[:, i, :]))
                            link(dve.tensor_tensor(mres[:, i, :], nmax[:, i, :], msp[:, i, 0, :], ALU.subtract))
                            link(dve.tensor_copy(msp[:, i, 1, :], mres[:, i, :]))
                            dve.tensor_tensor(msp[:, i, 2, :], mres[:, i, :], msp[:, i, 1, :], ALU.subtract).then_inc(g.msp.sem, 1)
                            if i == NT - 1:
                                max_chain.end()
                    if s[0] == "oT":
                        i = s[1]
                        if i == 0:
                            att_chain.start(q)
                        dve.wait_ge(g.ad_fill.sem, g.ad_fill.done(q, ad_use[s] + 1))
                        src = ps_dve.rearrange("p (l g d) -> p g l d", l=4, g=HG)
                        lv = linv[:, i, :].rearrange("p (g l) -> p g l", g=HG)
                        att_chain.link(dve.reciprocal(lv, src[:, :, :, HD]))
                        if i >= 2:
                            dve.wait_ge(g.aa_drain.sem, g.aa_drain.done(q, aa_use[("oC", i - 2)] + 1))
                        dve.tensor_tensor(oN[:, i % 2, :].rearrange("p (g l d) -> p g l d", g=HG, l=4),
                                          src[:, :, :, 0:HD], lv.unsqueeze(3).to_broadcast([P, HG, 4, HD]),
                                          ALU.mult).then_inc(g.ad_drain.sem, 1)
                    if s[0] == "pr":
                        i = s[1]
                        dve.wait_ge(g.ad_fill.sem, g.ad_fill.done(q, ad_use[s] + 1))
                        dve.wait_ge(g.gated.sem, g.gated.done(q, 1))
                        dve.wait_ge(g.x1_store.sem, g.x1_store.before(q, 16 * NT))
                        dve.wait_ge(g.h2.sem, g.h2.before(q, NT))
                        dve.tensor_tensor(x1[:, i, :], ps_dve[:, 0:C], x_in[:, q.s, i, :], ALU.add).then_inc(g.ad_drain.sem, 1)
                        dve.wait_ge(g.ad_drain.sem, g.ad_drain.done(q, ad_use[s] + 1))
                        link = att_chain.link
                        link(dve.bn_stats(bst2[:, i, :], x1[:, i, :]))
                        dve.bn_aggr(mv2[:, i, :], bst2[:, i, :]).then_inc(g.moments2.sem, 1)
                    if s[0] == "h2":
                        i = s[1]
                        link = att_chain.link
                        dve.wait_ge(g.rstd2.sem, g.rstd2.done(q, i + 1))
                        dve.wait_ge(g.aa_drain.sem, g.aa_drain.before(q, n_aa))
                        dve.wait_ge(g.h2_store.sem, g.h2_store.before(q, 16 * NT))
                        link(dve.scalar_tensor_tensor(out=h2[:, i, :], in0=x1[:, i, :], scalar=mv2[:, i, 0:1],
                                                      in1=rowb[:, q.s, 1, :], op0=ALU.subtract, op1=ALU.mult))
                        dve.scalar_tensor_tensor(out=h2[:, i, :], in0=h2[:, i, :], scalar=rstd2[:, i:i + 1],
                                                 in1=rowb[:, q.s, 2, :], op0=ALU.mult, op1=ALU.add).then_inc(g.h2.sem, 1)
                        if i == NT - 1:
                            att_chain.end()

                dve.wait_ge(w_loaded, 6 * 16)
                program(dve, step)

            @block.scalar
            def _(act):
                def step(q, s):
                    if s[0] == "hT":
                        k = s[1]
                        act.wait_ge(g.pa_fill.sem, g.pa_fill.done(q, pa_use[s] + 1))
                        act.wait_ge(g.cols.sem, g.cols.done(q, 1))
                        act.wait_ge(g.pd_drain.sem, g.pd_drain.before(q, NT))
                        act.activation(hT[:, k, :], ps_2act[:, act_bank[s]], ACT.Identity, bias=cols[:, k:k + 1],
                                       scale=cols[:, KC + k:KC + k + 1]).then_inc(g.pa_drain.sem, 1)
                    if s[0] == "sp":
                        i = s[1]
                        act.wait_ge(g.rope.sem, g.rope.done(q, i + 1))
                        act.wait_ge(g.pa_drain.sem, g.pa_drain.before(q, g.pa_drain.per))
                        act.activation(q6[:, i, :, 0:3, :], ra[:, i].unsqueeze(2).to_broadcast([P, H + 1, 3, HD]),
                                       ACT.Copy).then_inc(g.first.sem, 1)
                    if s[0] == "kT":
                        act.wait_ge(g.pa_fill.sem, g.pa_fill.done(q, pa_use[s] + 1))
                        act.activation(k6T[0:6 * HD, q.s, :], ps_2act[0:6 * HD, act_bank[s]].bitcast(BF16)[:, 0:T],
                                       ACT.Copy).then_inc(g.pa_drain.sem, 1)
                    if s[0] == "qT":
                        _, i, half = s
                        act.wait_ge(g.pa_fill.sem, g.pa_fill.done(q, pa_use[s] + 1))
                        act.activation(q6T[0:6 * HD, q.s, half * 8:half * 8 + 8, i * P:(i + 1) * P],
                                       ps_2act[0:6 * HD, act_bank[s]].bitcast(BF16).rearrange("p (h t) -> p h t", h=8),
                                       ACT.Copy).then_inc(g.pa_drain.sem, 1)
                    if s[0] == "mT":
                        i = s[1]
                        act.wait_ge(g.aa_fill.sem, g.aa_fill.done(q, aa_use[s] + 1))
                        act.activation(mT[:, i, :], ps_2act[0:3 * H, act_bank[s]].bitcast(BF16)[:, 0:P],
                                       ACT.Copy).then_inc(g.aa_drain.sem, 1)
                    if s[0] == "ST":
                        n = t_use[s]
                        act.wait_ge(g.t_fill.sem, g.t_fill.done(q, n + 1))
                        prev = (n - PR) // HG
                        if n >= PR:
                            act.wait_ge(g.pv.sem, g.pv.done(q, prev + 1))
                        else:
                            act.wait_ge(g.pv.sem, g.pv.before(q, n_pv + prev + 1))
                        act.activation(pT[:, n % PR].rearrange("p h t -> p (h t)"), ps_t[:, n % TR, :], ACT.Exp,
                                       scale=HD ** -0.5).then_inc(g.probs.sem, 1)
                    if s[0] == "oE":
                        i = s[1]
                        act.wait_ge(g.pv.sem, g.pv.done(q, pv_use[("PV", i, i)] + 1))
                        if i >= 2:
                            act.wait_ge(g.ad_drain.sem, g.ad_drain.done(q, ad_use[("oT", i - 2)] + 1))
                        else:
                            act.wait_ge(g.ad_drain.sem, g.ad_drain.before(q, ad_use[("oT", i + 2)] + 1))
                        act.activation(oS[:, i % 2].rearrange("p l t -> p (l t)"), ps_o, ACT.Copy).then_inc(g.o_out.sem, 1)
                    if s[0] == "oC":
                        i = s[1]
                        act.wait_ge(g.aa_fill.sem, g.aa_fill.done(q, aa_use[s] + 1))
                        if i >= 2:
                            act.wait_ge(g.ad_fill.sem, g.ad_fill.done(q, ad_use[("pr", i - 2)] + 1))
                        else:
                            act.wait_ge(g.ad_fill.sem, g.ad_fill.before(q, ad_use[("pr", i + 2)] + 1))
                        act.activation(oNT[:, i % 2].rearrange("p k t -> p (k t)"), ps_2act[:, act_bank[s], 0:KC * P],
                                       ACT.Copy).then_inc(g.aa_drain.sem, 1)
                    if s[0] == "h2T":
                        i = s[1]
                        act.wait_ge(g.aa_fill.sem, g.aa_fill.done(q, aa_use[s] + 1))
                        act.activation(h2T[:, :, i * P:(i + 1) * P], ps_2act[:, act_bank[s], 0:KC * P].rearrange("p (k t) -> p k t", k=KC),
                                       ACT.Copy).then_inc(g.aa_drain.sem, 1)
                    if s[0] == "lg":
                        act.wait_ge(g.aa_fill.sem, g.aa_fill.done(q, aa_use[s] + 1))
                        act.wait_ge(g.lg_store.sem, g.lg_store.before(q, 16))
                        act.activation(lg[:], ps_2act[0:E, act_bank[s], :], ACT.Identity, bias=bg[:, 0:1]).then_inc(g.aa_drain.sem, 1)

                act.wait_ge(w_loaded, 6 * 16)
                program(act, step)

            @block.tensor
            def _(pe):
                bank = {}

                def free(name, q, signal, n):
                    for last, value in bank.get(name, []):
                        pe.wait_ge(last.sem, value)
                    bank[name] = [(signal, signal.done(q, n))]

                def enter(q):
                    bank["dve"] = [(g.pd_drain, g.pd_drain.done(q, g.pd_drain.per)),
                                   (g.ad_drain, g.ad_drain.before(q, g.ad_drain.per))]
                    for b in range(2):
                        pro_n, att_n = (1 + max(n for s, n in use.items() if act_bank[s] == b) for use in (pa_use, aa_use))
                        bank[b] = [(g.pa_drain, g.pa_drain.done(q, pro_n)), (g.aa_drain, g.aa_drain.before(q, att_n))]

                def step(q, s):
                    if s[0] == "hT":
                        k = s[1]
                        pe.wait_ge(g.xn.sem, g.xn.done(q, NT))
                        free(act_bank[s], q, g.pa_drain, pa_use[s] + 1)
                        for i in range(NT):
                            last = pe.transpose(ps_2act[:, act_bank[s], i * P:(i + 1) * P], xn[:, i, k * P:(k + 1) * P], ident)
                        last.then_inc(g.pa_fill.sem, 1)
                    if s[0] == "qkv":
                        i = s[1]
                        pe.wait_ge(g.pa_drain.sem, g.pa_drain.done(q, pa_use[("hT", 1)] + 1))
                        free("dve", q, g.pd_drain, pd_use[s] + 1)
                        for k in range(KC):
                            last = pe.matmul(ps_dve[:, 0:C + 2 * HD], hT[:, k, i * P:(i + 1) * P], wqkv[:, k, :],
                                             start=k == 0, stop=k == KC - 1)
                        last.then_inc(g.pd_fill.sem, 1)
                    if s[0] == "kT":
                        pe.wait_ge(g.k6.sem, g.k6.done(q, 1))
                        free(act_bank[s], q, g.pa_drain, pa_use[s] + 1)
                        out = ps_2act[0:6 * HD, act_bank[s]].bitcast(BF16)
                        for i in range(NT):
                            last = pe.transpose(out[:, i * P:(i + 1) * P], k6[:, i, :], m.ident_bf[:])
                        last.then_inc(g.pa_fill.sem, 1)
                    if s[0] == "qT":
                        _, i, half = s
                        pe.wait_ge(g.split.sem, g.split.done(q, i + 1))
                        free(act_bank[s], q, g.pa_drain, pa_use[s] + 1)
                        out = ps_2act[0:6 * HD, act_bank[s]].bitcast(BF16)
                        for h in range(8):
                            last = pe.transpose(out[:, h * P:(h + 1) * P],
                                                q6[:, i, half * 8 + h].rearrange("p r d -> p (r d)"), m.ident_bf[:])
                        last.then_inc(g.pa_fill.sem, 1)
                    if s[0] == "S":
                        _, i, u = s
                        nh, n = S_HEADS[i], s_use[s]
                        if u == 0:
                            pe.wait_ge(g.pa_drain.sem, g.pa_drain.done(q, pa_use[("qT", i, 1)] + 1))
                        if n >= SR:
                            pe.wait_ge(g.s_max.sem, g.s_max.done(q, n - SR + 1))
                        else:
                            pe.wait_ge(g.s_max.sem, g.s_max.before(q, n_s + n - SR + 1))
                        w = (i + 1) * P
                        out = ps_s[:, n % SR, 0:nh * w].rearrange("p (h k) -> p h k", h=nh)
                        for a in range(nh):
                            pe.matmul(out[:, a, :], q6T[0:6 * HD, q.s, u * nh + a, i * P:(i + 1) * P],
                                      k6T[0:6 * HD, q.s, 0:w], start=a == 0, stop=False, skip_group_check=True)
                        pe.matmul(out[:, :, i * P:w], m.ident_bf[:], m.negs_bf[:].unsqueeze(1).to_broadcast([P, nh, P]),
                                  start=False, stop=True, skip_group_check=True).then_inc(g.s_fill.sem, 1)
                    if s[0] == "mT":
                        i = s[1]
                        pe.wait_ge(g.msp.sem, g.msp.done(q, i + 1))
                        free(act_bank[s], q, g.aa_drain, aa_use[s] + 1)
                        settle(pe, m.passed)
                        pe.transpose(ps_2act[0:3 * H, act_bank[s]].bitcast(BF16)[:, 0:P], msp[:, i].rearrange("p r h -> p (r h)"),
                                     m.ident_bf[:]).then_inc(g.aa_fill.sem, 1)
                    if s[0] == "ST":
                        _, i, j, hg = s
                        n = t_use[s]
                        if j == 0 and hg == 0:
                            pe.wait_ge(m_placed[i], q.n * 16 + 16)
                        if n >= TR:
                            pe.wait_ge(g.probs.sem, g.probs.done(q, n - TR + 1))
                        else:
                            last = max(k for k in range(n_t) if k % TR == n)
                            pe.wait_ge(g.probs.sem, g.probs.before(q, last + 1))
                        out = ps_t[:, (n) % TR, :].rearrange("p (h t) -> p h t", h=4)
                        last = pe.matmul(out, k6T[:, q.s, j * P:(j + 1) * P],
                                         q6T[:, q.s, hg * 4:hg * 4 + 4, i * P:(i + 1) * P], start=True, stop=j < i)
                        if j == i:
                            last = pe.matmul(out, m.ident_bf[:], m.negt_bf[:].unsqueeze(1).to_broadcast([P, 4, P]),
                                             start=False, stop=True)
                        last.then_inc(g.t_fill.sem, 1)
                    if s[0] == "PV":
                        _, i, j = s
                        n = t_use[("ST", i, j, 0)]
                        pe.wait_ge(g.probs.sem, g.probs.done(q, n + HG))
                        if j == 0:
                            pe.wait_ge(g.o_out.sem, g.o_out.done(q, i) if i else g.o_out.before(q, NT))
                        for hg in range(HG):
                            last = pe.matmul(ps_o[32 * hg:32 * hg + 32, :], v32[:, q.s, j, :],
                                             pT[:, (n + hg) % PR].rearrange("p h t -> p (h t)"),
                                             start=j == 0, stop=j == i, tile_position=(0, 32 * hg))
                        last.then_inc(g.pv.sem, 1)
                    if s[0] == "oT":
                        i = s[1]
                        pe.wait_ge(g.o_out.sem, g.o_out.done(q, i + 1))
                        free("dve", q, g.ad_drain, ad_use[s] + 1)
                        for l in range(4):
                            last = pe.transpose(ps_dve[:, l * P:(l + 1) * P], oS[:, i % 2, l, :], ident)
                        last.then_inc(g.ad_fill.sem, 1)
                    if s[0] == "oC":
                        i = s[1]
                        pe.wait_ge(g.ad_drain.sem, g.ad_drain.done(q, ad_use[("oT", i)] + 1))
                        free(act_bank[s], q, g.aa_drain, aa_use[s] + 1)
                        for k in range(KC):
                            last = pe.transpose(ps_2act[:, act_bank[s], k * P:(k + 1) * P], oN[:, i % 2, k * P:(k + 1) * P], ident)
                        last.then_inc(g.aa_fill.sem, 1)
                    if s[0] == "pr":
                        i = s[1]
                        pe.wait_ge(g.aa_drain.sem, g.aa_drain.done(q, aa_use[("oC", i)] + 1))
                        pe.wait_ge(g.gated.sem, g.gated.done(q, 1))
                        free("dve", q, g.ad_drain, ad_use[s] + 1)
                        for k in range(KC):
                            last = pe.matmul(ps_dve[:, 0:C], oNT[:, i % 2, k, :], gwo[:, q.s, k, :],
                                             start=k == 0, stop=k == KC - 1)
                        last.then_inc(g.ad_fill.sem, 1)
                    if s[0] == "h2T":
                        i = s[1]
                        pe.wait_ge(g.h2.sem, g.h2.done(q, i + 1))
                        free(act_bank[s], q, g.aa_drain, aa_use[s] + 1)
                        for k in range(KC):
                            last = pe.transpose(ps_2act[:, act_bank[s], k * P:(k + 1) * P], h2[:, i, k * P:(k + 1) * P], ident)
                        last.then_inc(g.aa_fill.sem, 1)
                    if s[0] == "lg":
                        pe.wait_ge(g.aa_drain.sem, g.aa_drain.done(q, aa_use[("h2T", NT - 1)] + 1))
                        free(act_bank[s], q, g.aa_drain, aa_use[s] + 1)
                        for k in range(KC):
                            last = pe.matmul(ps_2act[0:E, act_bank[s], :], wg[:, k, :], h2T[:, k, :],
                                             start=k == 0, stop=k == KC - 1)
                        last.then_inc(g.aa_fill.sem, 1)

                pe.wait_ge(w_loaded, 6 * 16)
                program(pe, step, enter)


def routing_phase(nc, m):
    with ExitStack() as ctx:
        def sb(name, shape, dt=F32):
            return ctx.enter_context(nc.sbuf_tensor(name, shape, dt))

        def sem(name):
            return ctx.enter_context(nc.semaphore(name))

        logits = sb("logits", [B * E, T])
        probs = sb("probs", [B * E, T])
        nmax = sb("route_nmax", [B * E, 1])
        total = sb("route_total", [B * E, 1])
        vals = sb("route_vals", [B * E, 2, TOPK])
        idx = sb("route_idx", [B * E, TOPK], U32)
        idxf = sb("route_idxf", [B * E, 2, TOPK])
        loaded = sem("route_loaded")
        chain = sem("route_vector_steps")
        max_ready = sem("route_max_ready")
        exp_ready = sem("route_exp_ready")
        tables = sem("route_tables_ready")
        turned = sem("route_turned")
        with nc.Block() as block:
            @block.sync
            def _(sp):
                sp.dma_start(logits[:], m.lg_d.rearrange("b e t -> (b e) t")).then_inc(loaded, 16)
                sp.dma_start(m.par_e[:, :, 4:7], m.d["eb"]).then_inc(loaded, 16)
                for b in range(B):
                    lo = (b % 2) * TOPK
                    sp.dma_start(m.gb_rows[lo:lo + TOPK, b // 2, :],
                                 m.mod_rows[b:b + 1, ROW_GATE_B * C:(ROW_GATE_B + 1) * C].to_broadcast([TOPK, C])).then_inc(loaded, 16)

            @block.scalar
            def _(act):
                act.wait_ge(max_ready, 1)
                act.activation(probs[:], logits[:], ACT.Exp, bias=nmax[:, 0:1],
                               accum_out=total[:, 0:1]).then_inc(exp_ready, 1)

            @block.tensor
            def _(pe):
                pe.wait_ge(tables, 1)
                ident = m.const[:, C_IDENT:C_IDENT + P]
                pe.transpose(m.psum[:, 0, 0:P], idxf[:].rearrange("p r s -> p (r s)"), ident)
                pe.transpose(m.psum[:, 1, 0:P], vals[:].rearrange("p r s -> p (r s)"), ident).then_inc(turned, 1)

            @block.vector
            def _(dve):
                count = [0]

                def link(ins):
                    count[0] += 1
                    ins.then_inc(chain, 1)
                    dve.wait_ge(chain, count[0])

                dve.wait_ge(loaded, 16 * (2 + B))
                dve.tensor_reduce(nmax[:], logits[:], AX_X, ALU.max, negate=True).then_inc(max_ready, 1)
                dve.wait_ge(exp_ready, 1)
                link(dve.reciprocal(total[:], total[:]))
                link(dve.tensor_scalar(probs[:], probs[:], total[:, 0:1], None, ALU.mult))
                for r in range(TOPK // 8):
                    part = slice(8 * r, 8 * r + 8)
                    link(dve.max(out=vals[:, 0, part], in_=probs[:]))
                    link(dve.max_index(out=idx[:, part], in_max=vals[:, 0, part], in_values=probs[:]))
                    if r < TOPK // 8 - 1:
                        link(dve.match_replace(out=probs[:], in_to_replace=vals[:, 0, part], in_values=probs[:],
                                               imm_value=-1.0))
                link(dve.tensor_copy(vals[:, 1, :], vals[:, 0, :]))
                seq = m.const[:, C_SEQ:C_SEQ + 1]
                link(dve.tensor_scalar(idxf[:, 0, :], idx[:], seq, None, ALU.add))
                link(dve.tensor_copy(idxf[:, 1, :], idxf[:, 0, :]))
                dve.sem_inc(tables, 1)
                dve.wait_ge(turned, 1)
                for half in range(2):
                    lo = half * TOPK
                    for bank, dst in ((0, m.idx_e[lo:lo + TOPK]), (1, m.par_e[lo:lo + TOPK, :, 0:4])):
                        src = m.psum[lo:lo + TOPK, bank, 0:P].rearrange("p (s two e) -> p e s two", two=2, e=E)
                        link(dve.tensor_copy(dst, src[:, :, :, half]))
                for i in range(4):
                    link(dve.tensor_tensor(m.par_e[:, :, 7 + i], m.par_e[:, :, i], m.par_e[:, :, 6], ALU.mult))


class ExpertSignals:

    def __init__(self, new):
        self.params = new("exp_params_ready", 1)
        self.picked = new("exp_indices_ready", 1)
        self.back = new("exp_scatter_indices_ready", 1)
        self.t_fill = new("exp_tokensT_filled", KC)
        self.t_act = new("exp_tokensT_by_act", 1)
        self.t_dve = new("exp_tokensT_by_vector", 1)
        self.l1_fill = new("exp_layer1_filled", KC)
        self.l1_act = new("exp_layer1_by_act", 1)
        self.l1_dve = new("exp_layer1_by_vector", 1)
        self.l2_fill = new("exp_layer2_filled", KC)
        self.l2_act = new("exp_layer2_by_act", 1)
        self.l2_dve = new("exp_layer2_by_vector", 1)
        self.l3_fill = new("exp_layer3_filled", 4)
        self.weighted = new("exp_layer3_weighted", 4)
        self.gated = new("exp_outputs_gated", 4)
        self.y_free = new("exp_outputs_seen_added", 1)


def expert_phase(nc, m):
    g = m.exp
    with ExitStack() as ctx:
        def sb(name, shape, dt=F32):
            return ctx.enter_context(nc.sbuf_tensor(name, shape, dt))

        def sem(name):
            return ctx.enter_context(nc.semaphore(name))

        wts = sb("expert_w", [P, 2, 3, KC, C])
        idx = sb("expert_idx", [P, 2, 4], U32)
        idx_back = sb("expert_idx_back", [P, 4], U32)
        par = sb("expert_par", [P, 2, 11])
        tok = sb("expert_tokens", [P, 2, 4, C])
        tokT = sb("expert_tokensT", [P, 2, KC, 512])
        h1 = sb("expert_h1", [P, KC, 512])
        h2 = sb("expert_h2", [P, KC, 512])
        yw = sb("expert_weighted", [P, 4, C])
        y = sb("expert_y", [P, 2, 4, C])
        w_in = [sem(f"exp_weights_loaded{s}") for s in range(2)]
        added = sem("exp_outputs_added")
        gathered = [sem(f"exp_tokens_gathered{s}") for s in range(2)]
        ps_t, ps_1, ps_2 = m.psum[:, 0:2, :], m.psum[:, 2:4, :], m.psum[:, 4:6, :]
        ps_3 = m.psum[:, 6:8, :].rearrange("p b (i c) -> p (b i) c", i=2)
        rows = m.x1_d.rearrange("i p c -> (i p) c")
        tokens = m.h2_d.rearrange("i p c -> (i p) c")
        ident = m.const[:, C_IDENT:C_IDENT + P]

        def is_first(q):
            return isinstance(q.n, int) and q.n == 0

        def program(eng, ahead, main):
            def one(q, last=False):
                if not last:
                    ahead(q.next())
                main(q, last)

            ahead(Seq(0, 0))
            one(Seq(0, 0))
            with eng.Fori(0, E // 2 - 1) as it:
                one(Seq(it, 1))
                one(Seq(it, 1).next())
            one(Seq(E // 2 - 1, 1), last=True)

        with nc.Block() as block:
            @block.sync
            def _(sp):
                def load(q):
                    sp.wait_ge(g.l3_fill.sem, g.l3_fill.before(q, 4, 2))
                    sp.dma_start(wts[:, q.s].rearrange("p l k c -> p (l k c)"),
                                 m.d["ew"][bass.ds(q.n, 1)].rearrange("e p n -> p (e n)")).then_inc(w_in[q.s], 16)

                program(sp, load, lambda q, last: None)

            @block.gpsimd
            def _(pool):
                def gather(q):
                    pool.wait_ge(g.t_fill.sem, g.t_fill.before(q, KC, 2))
                    settle(pool, m.passed)
                    pool.tensor_copy(idx[:, q.s, :].unsqueeze(1), m.idx_e[:, bass.ds(q.n, 1), :]).then_inc(g.picked.sem, 1)
                    pool.wait_ge(g.picked.sem, g.picked.done(q, 1))
                    settle(pool, m.passed)
                    for i in range(4):
                        pool.indirect_dma_start(
                            out=tok[:, q.s, i, :], out_offset=None, in_=tokens,
                            in_offset=bass.IndirectOffsetOnAxis(ap=idx[:, q.s, i:i + 1], axis=0),
                        ).then_inc(gathered[q.s], 16)

                def scatter(q):
                    if not is_first(q):
                        pool.wait_ge(added, q.n * 64)
                        pool.sem_inc(g.y_free.sem, 1)
                    settle(pool, m.passed)
                    pool.tensor_copy(idx_back[:].unsqueeze(1), m.idx_e[:, bass.ds(q.n, 1), :]).then_inc(g.back.sem, 1)
                    pool.wait_ge(g.back.sem, g.back.done(q, 1))
                    for i in range(4):
                        pool.wait_ge(g.gated.sem, g.gated.done(q, i + 1))
                        settle(pool, m.passed)
                        pool.indirect_dma_start(
                            out=rows, out_offset=bass.IndirectOffsetOnAxis(ap=idx_back[:, i:i + 1], axis=0),
                            in_=y[:, q.s, i, :], in_offset=None, compute_op=ALU.add,
                        ).then_inc(added, 16)

                gather(Seq(0, 0))
                gather(Seq(0, 1))
                gather(Seq(1, 0))
                scatter(Seq(0, 0))
                with pool.Fori(0, E // 2 - 2) as it:
                    for q in (Seq(it, 1), Seq(it, 1).next()):
                        gather(q.next().next())
                        scatter(q)
                gather(Seq(E // 2 - 1, 1))
                for n in range(E - 3, E):
                    scatter(Seq(n // 2, n % 2))
                pool.wait_ge(added, E * 64)

            @block.tensor
            def _(pe):
                def turn(q, k, tiles=range(4)):
                    if k == 0 and tiles[0] == 0:
                        pe.wait_ge(gathered[q.s], q.it * 64 + 64)
                        pe.wait_ge(g.t_act.sem, g.t_act.before(q, 1))
                    if k == 1:
                        pe.wait_ge(g.t_dve.sem, g.t_dve.before(q, 1))
                    for i in tiles:
                        ins = pe.transpose(ps_t[:, k, i * P:(i + 1) * P], tok[:, q.s, i, k * P:(k + 1) * P], ident)
                        if i == 3:
                            ins.then_inc(g.t_fill.sem, 1)

                def layer(q, n, ps, src, ready, banks_free, fill):
                    for k in range(KC):
                        signal, value = ready[k]
                        pe.wait_ge(signal.sem, value)
                        for o in range(KC):
                            if k == 0:
                                pe.wait_ge(banks_free[o].sem, banks_free[o].before(q, 1))
                            ins = pe.matmul(ps[:, o, :], wts[:, q.s, n, k, o * P:(o + 1) * P], src[:, k, :],
                                            start=k == 0, stop=k == KC - 1)
                            if k == KC - 1:
                                ins.then_inc(fill.sem, 1)

                def ahead(q):
                    if is_first(q):
                        turn(q, 0)
                        turn(q, 1)

                def main(q, last):
                    nxt = None if last else q.next()
                    pe.wait_ge(w_in[q.s], q.it * 16 + 16)
                    layer(q, 0, ps_1, tokT[:, q.s], [(g.t_act, g.t_act.done(q, 1)), (g.t_dve, g.t_dve.done(q, 1))],
                          (g.l1_act, g.l1_dve), g.l1_fill)
                    if nxt:
                        turn(nxt, 0, range(0, 2))
                    layer(q, 1, ps_2, h1, [(g.l1_act, g.l1_act.done(q, 1)), (g.l1_dve, g.l1_dve.done(q, 1))],
                          (g.l2_act, g.l2_dve), g.l2_fill)
                    if nxt:
                        turn(nxt, 0, range(2, 4))
                        turn(nxt, 1)
                    pe.wait_ge(g.l2_act.sem, g.l2_act.done(q, 1))
                    for i in range(4):
                        if i % 2 == 0:
                            pe.wait_ge(g.weighted.sem, g.weighted.before(q, i + 2))
                        pe.matmul(ps_3[:, i, :], h2[:, 0, i * P:(i + 1) * P], wts[:, q.s, 2, 0, :],
                                  start=i % 2 == 0, stop=False, skip_group_check=True)
                    pe.wait_ge(g.l2_dve.sem, g.l2_dve.done(q, 1))
                    for i in range(4):
                        pe.matmul(ps_3[:, i, :], h2[:, 1, i * P:(i + 1) * P], wts[:, q.s, 2, 1, :],
                                  start=False, stop=True, skip_group_check=True).then_inc(g.l3_fill.sem, 1)

                program(pe, ahead, main)

            @block.scalar
            def _(act):
                def copy_tokens(q):
                    act.wait_ge(g.t_fill.sem, g.t_fill.done(q, 1))
                    act.wait_ge(g.l1_fill.sem, g.l1_fill.before(q, KC, 2))
                    act.activation(tokT[:, q.s, 0, :], ps_t[:, 0, :], ACT.Copy).then_inc(g.t_act.sem, 1)

                def ahead(q):
                    if is_first(q):
                        copy_tokens(q)

                def main(q, last):
                    act.wait_ge(g.params.sem, g.params.done(q, 1))
                    act.wait_ge(g.l1_fill.sem, g.l1_fill.done(q, 1))
                    act.wait_ge(g.l2_fill.sem, g.l2_fill.before(q, KC))
                    act.activation(h1[:, 0, :], ps_1[:, 0, :], ACT.Relu, bias=par[:, q.s, 4:5]).then_inc(g.l1_act.sem, 1)
                    act.wait_ge(g.l2_fill.sem, g.l2_fill.done(q, 1))
                    act.wait_ge(g.l3_fill.sem, g.l3_fill.before(q, 4))
                    act.activation(h2[:, 0, :], ps_2[:, 0, :], ACT.Relu, bias=par[:, q.s, 5:6]).then_inc(g.l2_act.sem, 1)
                    if not last:
                        copy_tokens(q.next())
                    for i in range(4):
                        act.wait_ge(g.l3_fill.sem, g.l3_fill.done(q, i + 1 if i % 2 else i + 2))
                        act.wait_ge(g.gated.sem, g.gated.before(q, i + 1))
                        act.activation(yw[:, i, :], ps_3[:, i, :], ACT.Identity, scale=par[:, q.s, i:i + 1],
                                       bias=par[:, q.s, 7 + i:8 + i]).then_inc(g.weighted.sem, 1)

                program(act, ahead, main)

            @block.vector
            def _(dve):
                def copy_tokens(q):
                    dve.wait_ge(g.t_fill.sem, g.t_fill.done(q, 2))
                    dve.wait_ge(g.l1_fill.sem, g.l1_fill.before(q, KC, 2))
                    dve.tensor_copy(tokT[:, q.s, 1, :], ps_t[:, 1, :]).then_inc(g.t_dve.sem, 1)

                def ahead(q):
                    dve.wait_ge(g.weighted.sem, g.weighted.before(q, 4, 2))
                    dve.tensor_copy(par[:, q.s, :].unsqueeze(1), m.par_e[:, bass.ds(q.n, 1), :]).then_inc(g.params.sem, 1)
                    if is_first(q):
                        copy_tokens(q)

                def main(q, last):
                    dve.wait_ge(g.params.sem, g.params.done(q, 1))
                    dve.wait_ge(g.l1_fill.sem, g.l1_fill.done(q, 2))
                    dve.wait_ge(g.l2_fill.sem, g.l2_fill.before(q, KC))
                    dve.tensor_scalar(h1[:, 1, :], ps_1[:, 1, :], par[:, q.s, 4:5], 0.0, ALU.add, ALU.max).then_inc(g.l1_dve.sem, 1)
                    dve.wait_ge(g.l2_fill.sem, g.l2_fill.done(q, 2))
                    dve.wait_ge(g.l3_fill.sem, g.l3_fill.before(q, 4))
                    dve.tensor_scalar(h2[:, 1, :], ps_2[:, 1, :], par[:, q.s, 5:6], 0.0, ALU.add, ALU.max).then_inc(g.l2_dve.sem, 1)
                    if not last:
                        copy_tokens(q.next())
                    for i in range(4):
                        dve.wait_ge(g.weighted.sem, g.weighted.done(q, i + 1))
                        dve.wait_ge(g.y_free.sem, g.y_free.before(q, 1, 2))
                        dve.tensor_tensor(y[:, q.s, i, :], yw[:, i, :], m.gb_rows[:, i, :], ALU.mult).then_inc(g.gated.sem, 1)

                program(dve, ahead, main)


def linear_orders():
    pause = [("pause",)]
    pro = [("ln",)] + 3 * pause + [("st",)] + [("xn",)] + [("hT", 0), ("hT", 1)]
    pro += [("qk", n) for n in range(4)] + [("v", i) for i in range(NT)]
    att = []
    for i in range(NT):
        late = [[], [("PV", i - 1), ("oE", i - 1)], [("oT", i - 1)]] if i else [[]] * 3
        later = [("oC", i - 2), ("pr", i - 2)] if i >= 2 else []
        att += [("kt", i), ("A", i, 0)] + late[1] + [("A", i, 1)] + later[:1]
        att += ([("KV", i)] if i < NT - 1 else []) + later[1:] + [("A", i, 2)] + late[2] + [("A", i, 3)]
    i = NT - 1
    tail = [("oC", i - 1), ("PV", i), ("oE", i), ("pr", i - 1), ("oT", i), ("oC", i), ("pr", i)]
    return pro, att, tail


def linear_merged():
    def mark(steps, following):
        return [(s, following) for s in steps]

    pro, att, tail = linear_orders()
    return (mix(mark(att, False), mark(pro[:-8], True), 0.0, 0.85)
            + mix(mark(tail, False), mark(pro[-8:], True)))


class LinearSignals:

    def __init__(self, new):
        self.stats = new("lin_stats", NT)
        self.moments = new("lin_moments", NT)
        self.cols = new("lin_mod_cols", 1)
        self.pool_steps = new("lin_pool_steps", 1 + 3 + 3)
        self.rstd = new("lin_rstd_ready", 1)
        self.xn = new("lin_xn_ready", NT)
        self.gated = new("lin_gated_ready", 1)
        self.pa_fill = new("lin_prologue_act_bank_filled", 2)
        self.pa_drain = new("lin_prologue_act_bank_drained", 2)
        self.pd_fill = new("lin_prologue_vector_bank_filled", NT)
        self.pd_drain = new("lin_prologue_vector_bank_drained", NT)
        self.aa_fill = new("lin_act_bank_filled", 2 * NT)
        self.aa_drain = new("lin_act_bank_drained", 2 * NT)
        self.ad_fill = new("lin_vector_bank_filled", 2 * NT)
        self.ad_drain = new("lin_vector_bank_drained", 2 * NT)
        self.qk_fill = new("lin_qk_filled", 4)
        self.qk_relu = new("lin_qk_relu", 4)
        self.qk_exp = new("lin_qk_exp", 4)
        self.qk_map = new("lin_qk_mapped", 4)
        self.masked = new("lin_q_masked", 4)
        self.a_fill = new("lin_scores_filled", 4 * NT)
        self.a_keep = new("lin_scores_masked", 4 * NT)
        self.kv_fill = new("lin_state_filled", NT - 1)
        self.kv_copy = new("lin_state_copied", NT - 1)
        self.pv = new("lin_out_filled", NT)
        self.o_out = new("lin_out_copied", NT)
        self.dve_steps = new("lin_vector_steps", 2 * NT)
        self.x3_store = new("lin_x3_stored", 16 * NT)


def linear_phase(nc, m):
    pro, att, tail = linear_orders()
    att = att + tail
    merged = linear_merged()
    aa_use, n_aa = index_of(att, ("kt", "oC"))
    ad_use, n_ad = index_of(att, ("oT", "pr"))
    a_use, n_a = index_of(att, ("A",))
    AR, SR = 2, 8
    g = m.lin
    with ExitStack() as ctx:
        def sb(name, shape, dt=F32):
            return ctx.enter_context(nc.sbuf_tensor(name, shape, dt))

        def sem(name):
            return ctx.enter_context(nc.semaphore(name))

        w = sb("l_w", [P, KC, 3 * C])
        wo = sb("l_wo", [P, KC, C])
        bo = sb("l_bo", [P, C])
        bv = sb("l_bv", [P, C])
        bqk = sb("l_bqk", [P, 4])
        bneg = sb("l_bneg", [P, 4])
        bone = sb("l_bone", [P, 4])
        mhalf = sb("l_mhalf", [P, NT])
        x_in = sb("l_x", [P, 2, NT, C])
        rowb = sb("l_rows", [P, 2, C])
        cols = sb("l_cols", [P, 4])
        gwo = sb("l_gwo", [P, 2, KC, C])
        gbo = sb("l_gbo", [P, C])
        bst = sb("l_bst", [P, NT, 6])
        mv = sb("l_mv", [P, NT, 2])
        rstd = sb("l_rstd", [P, NT])
        vtmp = sb("l_vtmp", [P, NT])
        xn = sb("l_xn", [P, NT, C])
        hT = sb("l_hT", [P, KC, T])
        rt = sb("l_relu", [P, 2, T])
        et = sb("l_exp", [P, 2, T])
        qm = sb("l_q_masked", [P, 2, KC, 2, T])
        kf = sb("l_k", [P, 2, KC, T])
        qs = sb("l_q_all", [P, 2, KC, T])
        v32 = sb("l_v", [P, 2, NT, H, 32])
        ktok = sb("l_k_tokens", [P, NT, C])
        kept = sb("l_scores", [P, SR, 4, P])
        state = sb("l_state", [P, 2, KC, 2 * P])
        oS = sb("l_oS", [P, 2, 4, P])
        linv = sb("l_linv", [P, NT, H])
        oN = sb("l_oN", [P, 2, C])
        oNT = sb("l_oNT", [P, 2, KC, P])
        x3 = sb("l_x3", [P, NT, C])
        ps_a = m.psum[:, 0:AR, :]
        ps_kv = m.psum[:, 2, :]
        ps_o = m.psum[:, 3, :]
        ps_act = m.psum[:, 4, :]
        ps_dve = m.psum[:, 5, :]
        ps_qk = m.psum[:, 6:8, :]
        ident = m.const[:, C_IDENT:C_IDENT + P]
        keep = m.const[:, C_KEEP:C_KEEP + P]
        blocks = m.const[:, C_BD:C_BD + 2 * P]
        w_loaded = sem("lin_weights_loaded")
        ready = sem("lin_constants_ready")
        in_loaded = [sem(f"lin_inputs_loaded{s}") for s in range(2)]

        def program(eng, step, enter=lambda q: None):
            def one(q, last=False):
                enter(q)
                for s, following in merged:
                    if not following:
                        step(q, s)
                    elif not last:
                        step(q.next(), s)

            for s in pro:
                step(Seq(0, 0), s)
            with eng.Fori(0, B // 2 - 1) as it:
                one(Seq(it, 0))
                one(Seq(it, 1))
            one(Seq(B // 2 - 1, 0))
            one(Seq(B // 2 - 1, 1), last=True)

        with nc.Block() as block:
            @block.sync
            def _(sp):
                for dst, src in ((w, m.d["lw"]), (wo, m.d["lwo"]), (bo, m.d["lbo"]), (bv, m.d["lbv"]), (bqk, m.d["lbqk"])):
                    sp.dma_start(dst[:], src).then_inc(w_loaded, 16)

                def step(q, s):
                    if s[0] == "ln":
                        sp.wait_ge(g.ad_drain.sem, g.ad_drain.before(q, n_ad, 2))
                        sp.dma_start(x_in[:, q.s], m.x1_d[bass.ds(q.n * NT, NT)].rearrange("i p c -> p i c")).then_inc(in_loaded[q.s], 16)
                        sp.dma_start(rowb[:, q.s, :], m.mod_rows[bass.ds(q.n, 1), ROW_GATE_L1 * C:(ROW_GATE_L1 + 1) * C].to_broadcast([P, C])).then_inc(in_loaded[q.s], 16)
                    if s[0] == "pr":
                        i = s[1]
                        sp.wait_ge(g.ad_drain.sem, g.ad_drain.done(q, ad_use[s] + 1))
                        sp.dma_start(m.x3_d[bass.ds(q.n * NT + i, 1)].rearrange("i p c -> p (i c)"), x3[:, i, :]).then_inc(g.x3_store.sem, 16)

                program(sp, step)
                sp.wait_ge(g.x3_store.sem, g.x3_store.done(Seq(B // 2 - 1, 1), 16 * NT))

            @block.gpsimd
            def _(pool):
                chain = Chain(pool, g.pool_steps, m.passed)

                def step(q, s):
                    if s[0] == "st":
                        chain.start(q)
                        link = chain.link
                        pool.wait_ge(in_loaded[q.s], q.it * 32 + 32)
                        pool.wait_ge(g.moments.sem, g.moments.done(q, NT))
                        pool.wait_ge(g.xn.sem, g.xn.before(q, NT))
                        settle(pool, m.passed)
                        link(pool.tensor_scalar(vtmp[:], mv[:, :, 1], EPS, None, ALU.add))
                        pool.tensor_tensor(rstd[:], vtmp[:], mhalf[:], ALU.pow).then_inc(g.rstd.sem, 1)
                        link(pool.tensor_tensor(gbo[:], bo[:], rowb[:, q.s, :], ALU.mult))
                        for k in range(KC):
                            link(pool.tensor_tensor(gwo[:, q.s, k, :], wo[:, k, :], rowb[:, q.s, :], ALU.mult))
                    if s == ("hT", 1):
                        link = chain.link
                        pool.wait_ge(g.xn.sem, g.xn.done(q, NT))
                        settle(pool, m.passed)
                        for i in range(NT):
                            ins = pool.tensor_tensor(x_in[:, q.s, i, :], x_in[:, q.s, i, :], gbo[:], ALU.add)
                            if i < NT - 1:
                                link(ins)
                            else:
                                ins.then_inc(g.gated.sem, 1)
                                pool.wait_ge(g.gated.sem, g.gated.done(q, 1))
                                settle(pool, m.passed)
                        chain.end()
                    if s[0] == "qk" and s[1] < 2:
                        k = s[1]
                        pool.wait_ge(g.qk_map.sem, g.qk_map.done(q, k + 1))
                        settle(pool, m.passed)
                        for odd in range(2):
                            c = C_PARITY + odd
                            pool.tensor_scalar(qm[:, q.s, k, odd, :], qs[:, q.s, k, :], m.const[:, c:c + 1], None,
                                               ALU.mult).then_inc(g.masked.sem, 1)

                pool.wait_ge(w_loaded, 5 * 16)
                pool.wait_ge(ready, 1)
                program(pool, step)

            @block.vector
            def _(dve):
                chain = Chain(dve, g.dve_steps, m.passed)

                def step(q, s):
                    if s[0] == "st":
                        dve.wait_ge(in_loaded[q.s], q.it * 32 + 32)
                        dve.wait_ge(g.pa_drain.sem, g.pa_drain.before(q, 2))
                        dve.tensor_copy(cols[:].unsqueeze(2), m.modT[:, 1, 0:4, bass.ds(q.n, 1)]).then_inc(g.cols.sem, 1)
                        for i in range(NT):
                            dve.bn_stats(bst[:, i, :], x_in[:, q.s, i, :]).then_inc(g.stats.sem, 1)
                        dve.wait_ge(g.stats.sem, g.stats.done(q, NT))
                        dve.wait_ge(g.xn.sem, g.xn.before(q, NT))
                        settle(dve, m.passed)
                        for i in range(NT):
                            dve.bn_aggr(mv[:, i, :], bst[:, i, :]).then_inc(g.moments.sem, 1)
                    if s[0] == "xn":
                        dve.wait_ge(g.rstd.sem, g.rstd.done(q, 1))
                        for i in range(NT):
                            dve.tensor_scalar(xn[:, i, :], x_in[:, q.s, i, :], mv[:, i, 0:1], rstd[:, i:i + 1],
                                              ALU.subtract, ALU.mult).then_inc(g.xn.sem, 1)
                    if s[0] == "qk":
                        n = s[1]
                        dve.wait_ge(g.qk_exp.sem, g.qk_exp.done(q, n + 1))
                        dst = qs if n < KC else kf
                        dve.scalar_tensor_tensor(out=dst[:, q.s, n % KC, :], in0=ps_qk[:, n % 2, :], scalar=bone[:, n:n + 1],
                                                 in1=et[:, n % 2, :], op0=ALU.add, op1=ALU.max).then_inc(g.qk_map.sem, 1)
                    if s[0] == "v":
                        i = s[1]
                        dve.wait_ge(g.pd_fill.sem, g.pd_fill.done(q, i + 1))
                        dve.tensor_tensor(v32[:, q.s, i, :, 0:HD], ps_qk[:, i % 2, 0:C].rearrange("p (h d) -> p h d", h=H),
                                          bv[:].rearrange("p (h d) -> p h d", h=H), ALU.add).then_inc(g.pd_drain.sem, 1)
                    if s[0] == "A":
                        n = a_use[s]
                        dve.wait_ge(g.a_fill.sem, g.a_fill.done(q, n + 1))
                        i = s[1]
                        dve.wait_ge(g.pv.sem, g.pv.done(q, i - 1) if i >= 2 else g.pv.before(q, NT + i - 1))
                        dve.tensor_tensor(kept[:, n % SR], ps_a[:, n % AR, :].rearrange("p (h t) -> p h t", h=4),
                                          keep.unsqueeze(1).to_broadcast([P, 4, P]), ALU.mult).then_inc(g.a_keep.sem, 1)
                    if s[0] == "KV":
                        i = s[1]
                        dve.wait_ge(g.kv_fill.sem, g.kv_fill.done(q, i + 1))
                        dve.wait_ge(g.pv.sem, g.pv.done(q, i) if i else g.pv.before(q, NT))
                        dve.tensor_tensor(state[:, i % 2], ps_kv.rearrange("p (k n) -> p k n", k=KC),
                                          blocks.unsqueeze(1).to_broadcast([P, KC, 2 * P]), ALU.mult).then_inc(g.kv_copy.sem, 1)
                    if s[0] == "oT":
                        i = s[1]
                        if i == 0:
                            chain.start(q)
                        dve.wait_ge(g.ad_fill.sem, g.ad_fill.done(q, ad_use[s] + 1))
                        src = ps_dve.rearrange("p (h d) -> p h d", h=H)
                        chain.link(dve.tensor_scalar(linv[:, i, :], src[:, :, HD], 1e-6, None, ALU.add))
                        chain.link(dve.reciprocal(linv[:, i, :], linv[:, i, :]))
                        if i >= 2:
                            dve.wait_ge(g.aa_drain.sem, g.aa_drain.done(q, aa_use[("oC", i - 2)] + 1))
                        dve.tensor_tensor(oN[:, i % 2, :].rearrange("p (h d) -> p h d", h=H), src[:, :, 0:HD],
                                          linv[:, i, :].unsqueeze(2).to_broadcast([P, H, HD]), ALU.mult).then_inc(g.ad_drain.sem, 1)
                        if i == NT - 1:
                            chain.end()
                    if s[0] == "pr":
                        i = s[1]
                        dve.wait_ge(g.ad_fill.sem, g.ad_fill.done(q, ad_use[s] + 1))
                        dve.wait_ge(g.gated.sem, g.gated.done(q, 1))
                        dve.wait_ge(g.x3_store.sem, g.x3_store.before(q, 16 * NT))
                        dve.tensor_tensor(x3[:, i, :], ps_dve[:, 0:C], x_in[:, q.s, i, :], ALU.add).then_inc(g.ad_drain.sem, 1)

                dve.memset(mhalf[:], -0.5)
                dve.memset(v32[:], 0.0).then_inc(ready, 1)
                dve.wait_ge(ready, 1)
                dve.memset(v32[:, :, :, :, HD:HD + 1], 1.0)
                dve.wait_ge(w_loaded, 5 * 16)
                dve.tensor_scalar(bneg[:], bqk[:], -1.0, None, ALU.mult)
                dve.tensor_scalar(bone[:], bqk[:], 1.0, None, ALU.add).then_inc(ready, 1)
                dve.wait_ge(ready, 2)
                program(dve, step)

            @block.scalar
            def _(act):
                def step(q, s):
                    if s[0] == "hT":
                        k = s[1]
                        act.wait_ge(g.pa_fill.sem, g.pa_fill.done(q, k + 1))
                        act.wait_ge(g.cols.sem, g.cols.done(q, 1))
                        act.wait_ge(g.pd_drain.sem, g.pd_drain.before(q, NT))
                        act.activation(hT[:, k, :], ps_act, ACT.Identity, bias=cols[:, k:k + 1],
                                       scale=cols[:, KC + k:KC + k + 1]).then_inc(g.pa_drain.sem, 1)
                    if s[0] == "qk":
                        n = s[1]
                        act.wait_ge(g.qk_fill.sem, g.qk_fill.done(q, n + 1))
                        act.wait_ge(g.qk_map.sem, g.qk_map.done(q, n - 1) if n >= 2 else g.qk_map.before(q, 4 + n - 1))
                        act.activation(rt[:, n % 2, :], ps_qk[:, n % 2, :], ACT.Relu, bias=bneg[:, n:n + 1],
                                       scale=-1.0).then_inc(g.qk_relu.sem, 1)
                        act.wait_ge(g.qk_relu.sem, g.qk_relu.done(q, n + 1))
                        act.activation(et[:, n % 2, :], rt[:, n % 2, :], ACT.Exp, scale=-1.0).then_inc(g.qk_exp.sem, 1)
                    if s[0] == "kt":
                        i = s[1]
                        act.wait_ge(g.aa_fill.sem, g.aa_fill.done(q, aa_use[s] + 1))
                        act.wait_ge(g.kv_fill.sem, g.kv_fill.before(q, NT - 1))
                        act.activation(ktok[:, i, :], ps_act[:, 0:C], ACT.Copy).then_inc(g.aa_drain.sem, 1)
                    if s[0] == "oE":
                        i = s[1]
                        act.wait_ge(g.pv.sem, g.pv.done(q, i + 1))
                        if i >= 2:
                            act.wait_ge(g.ad_drain.sem, g.ad_drain.done(q, ad_use[("oT", i - 2)] + 1))
                        else:
                            act.wait_ge(g.ad_drain.sem, g.ad_drain.before(q, ad_use[("oT", i + 2)] + 1))
                        act.activation(oS[:, i % 2].rearrange("p l t -> p (l t)"), ps_o, ACT.Copy).then_inc(g.o_out.sem, 1)
                    if s[0] == "oC":
                        i = s[1]
                        act.wait_ge(g.aa_fill.sem, g.aa_fill.done(q, aa_use[s] + 1))
                        if i >= 2:
                            act.wait_ge(g.ad_fill.sem, g.ad_fill.done(q, ad_use[("pr", i - 2)] + 1))
                        else:
                            act.wait_ge(g.ad_fill.sem, g.ad_fill.before(q, ad_use[("pr", i + 2)] + 1))
                        act.activation(oNT[:, i % 2].rearrange("p k t -> p (k t)"), ps_act[:, 0:KC * P],
                                       ACT.Copy).then_inc(g.aa_drain.sem, 1)

                act.wait_ge(ready, 2)
                program(act, step)

            @block.tensor
            def _(pe):
                bank = {}

                def free(name, q, signal, n):
                    for last, value in bank.get(name, []):
                        pe.wait_ge(last.sem, value)
                    bank[name] = [(signal, signal.done(q, n))]

                def enter(q):
                    bank["act"] = [(g.pa_drain, g.pa_drain.done(q, g.pa_drain.per)),
                                   (g.aa_drain, g.aa_drain.before(q, g.aa_drain.per))]
                    bank["dve"] = [(g.ad_drain, g.ad_drain.before(q, g.ad_drain.per))]

                def step(q, s):
                    if s[0] == "hT":
                        k = s[1]
                        pe.wait_ge(g.xn.sem, g.xn.done(q, NT))
                        free("act", q, g.pa_drain, k + 1)
                        for i in range(NT):
                            last = pe.transpose(ps_act[:, i * P:(i + 1) * P], xn[:, i, k * P:(k + 1) * P], ident)
                        last.then_inc(g.pa_fill.sem, 1)
                    if s[0] == "qk":
                        n = s[1]
                        pe.wait_ge(g.pa_drain.sem, g.pa_drain.done(q, 2))
                        if n >= 2:
                            pe.wait_ge(g.qk_map.sem, g.qk_map.done(q, n - 1))
                        else:
                            pe.wait_ge(g.pd_drain.sem, g.pd_drain.before(q, NT + n - 1))
                        for k in range(KC):
                            last = pe.matmul(ps_qk[:, n % 2, :], w[:, k, n * P:(n + 1) * P], hT[:, k, :],
                                             start=k == 0, stop=k == KC - 1)
                        last.then_inc(g.qk_fill.sem, 1)
                    if s[0] == "v":
                        i = s[1]
                        if i < 2:
                            pe.wait_ge(g.qk_map.sem, g.qk_map.done(q, 3 + i))
                        else:
                            pe.wait_ge(g.pd_drain.sem, g.pd_drain.done(q, i - 1))
                        for k in range(KC):
                            last = pe.matmul(ps_qk[:, i % 2, 0:C], hT[:, k, i * P:(i + 1) * P], w[:, k, 2 * C:3 * C],
                                             start=k == 0, stop=k == KC - 1)
                        last.then_inc(g.pd_fill.sem, 1)
                    if s[0] == "kt":
                        i = s[1]
                        pe.wait_ge(g.qk_map.sem, g.qk_map.done(q, 4))
                        free("act", q, g.aa_drain, aa_use[s] + 1)
                        for k in range(KC):
                            last = pe.transpose(ps_act[:, k * P:(k + 1) * P], kf[:, q.s, k, i * P:(i + 1) * P], ident)
                        last.then_inc(g.aa_fill.sem, 1)
                    if s[0] == "A":
                        _, i, r = s
                        n = a_use[s]
                        if i == 0 and r == 0:
                            pe.wait_ge(g.masked.sem, g.masked.done(q, 4))
                        pe.wait_ge(g.a_keep.sem, g.a_keep.done(q, n - 1) if n >= AR else g.a_keep.before(q, n_a + n - 1))
                        at, t = 32 * r, slice(i * P, (i + 1) * P)
                        for l in range(4):
                            last = pe.matmul(ps_a[:, n % AR, l * P:(l + 1) * P], kf[at:at + 32, q.s, l // 2, t],
                                             qm[at:at + 32, q.s, l // 2, l % 2, t], start=True, stop=True,
                                             tile_position=(at, 0))
                        last.then_inc(g.a_fill.sem, 1)
                    if s[0] == "KV":
                        i = s[1]
                        pe.wait_ge(g.aa_drain.sem, g.aa_drain.done(q, aa_use[("kt", i)] + 1))
                        pe.wait_ge(g.kv_copy.sem, g.kv_copy.done(q, i) if i else g.kv_copy.before(q, NT - 1))
                        pe.wait_ge(g.pd_drain.sem, g.pd_drain.done(q, NT))
                        for k in range(KC):
                            last = pe.matmul(ps_kv[:, k * 2 * P:(k + 1) * 2 * P], ktok[:, i, k * P:(k + 1) * P],
                                             v32[:, q.s, i, 8 * k:8 * k + 8, :].rearrange("p h d -> p (h d)"),
                                             start=i == 0 and k == 0, stop=True, skip_group_check=True)
                        last.then_inc(g.kv_fill.sem, 1)
                    if s[0] == "PV":
                        i = s[1]
                        pe.wait_ge(g.a_keep.sem, g.a_keep.done(q, a_use[("A", i, 3)] + 1))
                        pe.wait_ge(g.o_out.sem, g.o_out.done(q, i) if i else g.o_out.before(q, NT))
                        if i:
                            pe.wait_ge(g.kv_copy.sem, g.kv_copy.done(q, i))
                            for hg in range(HG):
                                pe.matmul(ps_o[:, hg * P:(hg + 1) * P], state[:, (i - 1) % 2, hg // 2, (hg % 2) * P:(hg % 2) * P + P],
                                          qs[:, q.s, hg // 2, i * P:(i + 1) * P], start=hg == 0, stop=False,
                                          skip_group_check=True)
                        for h in range(H):
                            hg, l = h // 4, h % 4
                            n = a_use[("A", i, h % 8 // 2)]
                            last = pe.matmul(ps_o[32 * l:32 * l + 32, hg * P:(hg + 1) * P], v32[:, q.s, i, h, :],
                                             kept[:, n % SR, 2 * (h // 8) + h % 2, :], start=i == 0 and hg == 0, stop=True,
                                             tile_position=(0, 32 * l), skip_group_check=True)
                        last.then_inc(g.pv.sem, 1)
                    if s[0] == "oT":
                        i = s[1]
                        pe.wait_ge(g.o_out.sem, g.o_out.done(q, i + 1))
                        free("dve", q, g.ad_drain, ad_use[s] + 1)
                        for hg in range(HG):
                            last = pe.transpose(ps_dve[:, hg * P:(hg + 1) * P], oS[:, i % 2, hg, :], ident)
                        last.then_inc(g.ad_fill.sem, 1)
                    if s[0] == "oC":
                        i = s[1]
                        pe.wait_ge(g.ad_drain.sem, g.ad_drain.done(q, ad_use[("oT", i)] + 1))
                        free("act", q, g.aa_drain, aa_use[s] + 1)
                        for k in range(KC):
                            last = pe.transpose(ps_act[:, k * P:(k + 1) * P], oN[:, i % 2, k * P:(k + 1) * P], ident)
                        last.then_inc(g.aa_fill.sem, 1)
                    if s[0] == "pr":
                        i = s[1]
                        pe.wait_ge(g.aa_drain.sem, g.aa_drain.done(q, aa_use[("oC", i)] + 1))
                        pe.wait_ge(g.gated.sem, g.gated.done(q, 1))
                        free("dve", q, g.ad_drain, ad_use[s] + 1)
                        for k in range(KC):
                            last = pe.matmul(ps_dve[:, 0:C], oNT[:, i % 2, k, :], gwo[:, q.s, k, :],
                                             start=k == 0, stop=k == KC - 1)
                        last.then_inc(g.ad_fill.sem, 1)

                pe.wait_ge(ready, 2)
                program(pe, step, enter)


CYCLES = 3


def half_cycle(c1, a1, c2, a2, first=False, second=False):
    u = [(("L1", c1, a1, n), first) for n in range(4)]
    return [(("L2", c2, a2), second), u[0], (("L3", c2, a2), second), u[1],
            (("L4", c2, a2), second), (("up", c2, a2), second), u[2], u[3]]


def coupling_prologue():
    pause = [("pause",)]
    pro = [("ln",)] + 2 * pause + [("st", i) for i in range(2 * NT)] + [("ag",)] + 3 * pause
    for a in range(2):
        pro += [("xn", a * NT + i) for i in range(NT)] + [("hT", a, k) for k in range(KC)]
    return pro + [("g1",), ("g2",), ("g3",)]


def first_steps():
    return [("L1", 0, 0, u) for u in range(4)] + [s for s, _ in half_cycle(0, 1, 0, 0)]


def coupling_merged():
    main = []
    for c in range(1, CYCLES):
        main += half_cycle(c, 0, c - 1, 1) + half_cycle(c, 1, c, 0)
    main = mix(main + [(("gate", 0), False)], [(s, True) for s in coupling_prologue()], 0.0, 0.95)
    tail = mix(half_cycle(0, 0, CYCLES - 1, 1, first=True), [(("oT", 0, i), False) for i in range(2)], 0.25, 1.0)
    end = [(("gate", 1), False)] + [(("oT", 1, i), False) for i in range(2)]
    return main + tail + mix(half_cycle(0, 1, 0, 0, first=True, second=True), end, 0.1, 0.7)


class CouplingSignals:

    def __init__(self, new):
        n = 2 * CYCLES
        self.stats = new("cpl_stats", 2 * NT)
        self.moments = new("cpl_moments", 2 * NT)
        self.cols = new("cpl_mod_cols", 1)
        self.pool_steps = new("cpl_pool_steps", 1)
        self.xn = new("cpl_xn_ready", 2 * NT)
        self.rstd = new("cpl_rstd_ready", 1)
        self.pa_fill = new("cpl_act_bank_filled", 7)
        self.pa_drain = new("cpl_act_bank_drained", 7)
        self.coef = new("cpl_coefficients", 1)
        self.l1_fill = new("cpl_layer1_filled", 2 * n)
        self.l1 = new("cpl_layer1_ready", 2 * n)
        self.l2_fill = new("cpl_layer2_filled", n)
        self.l2 = new("cpl_layer2_ready", n)
        self.l3_fill = new("cpl_layer3_filled", n)
        self.l3 = new("cpl_layer3_ready", n)
        self.l4_fill = new("cpl_layer4_filled", n)
        self.l4 = new("cpl_layer4_ready", n)
        self.steps = new("cpl_vector_steps", 2 * n)
        self.state = new("cpl_state_ready", 2 * n)
        self.gate = new("cpl_output_gated", 4)
        self.o_fill = new("cpl_output_turned", 4)
        self.o_done = new("cpl_output_ready", 4)
        self.store = new("cpl_output_stored", 16 * 4)


def coupling_phase(nc, m):
    pro, merged = coupling_prologue() + first_steps(), coupling_merged()
    pa_use, _ = index_of(pro, ("hT", "g1", "g2", "g3"))
    g = m.cpl
    R = B // 2
    with ExitStack() as ctx:
        def sb(name, shape, dt=F32):
            return ctx.enter_context(nc.sbuf_tensor(name, shape, dt))

        def sem(name):
            return ctx.enter_context(nc.semaphore(name))

        w1 = sb("c_w1", [P, KC, C])
        w2 = sb("c_w2", [P, KC, P])
        w34 = sb("c_w34", [P, 64])
        w4 = sb("c_w4", [64, P])
        g1w = sb("c_g1", [P, KC, P])
        g2w = sb("c_g2", [P, 64])
        g3w = sb("c_g3", [64, P])
        bias = sb("c_bias", [P, 9])
        half = sb("c_half", [P, 4])
        mhalf = sb("c_mhalf", [P, 2 * NT])
        nsgn = sb("c_nsgn", [P, 1])
        x_in = sb("c_x", [P, 2, 2, NT, C])
        cols = sb("c_cols", [P, 2, 6, 2])
        bst = sb("c_bst", [P, 2 * NT, 6])
        mv = sb("c_mv", [P, 2 * NT, 2])
        rstd = sb("c_rstd", [P, 2 * NT])
        vtmp = sb("c_vtmp", [P, 2 * NT])
        xn = sb("c_xn", [P, 2 * NT, C])
        o = sb("c_state", [P, 2, 2, KC, T])
        sums = sb("c_sums", [P, KC, 2])
        gs1 = sb("c_gs1", [P, 2])
        gs2 = sb("c_gs2", [64, 2])
        gs3 = sb("c_gs3", [P, 2])
        coef = sb("c_coef", [P, 2, 2])
        a1 = sb("c_a1", [P, 2, KC, T])
        a2 = sb("c_a2", [P, 2, T])
        a3 = sb("c_a3", [64, 2, T])
        th = sb("c_th", [P, 2, T])
        cc = sb("c_cc", [P, 2, T])
        uv = sb("c_uv", [P, 2, 2, T])
        og = sb("c_og", [P, 2, KC, T])
        ot = sb("c_ot", [P, 2, 2, 2, C])
        ps_1 = m.psum[:, 0:4, :].rearrange("p (a o) t -> p a o t", a=2)
        ps_2 = m.psum[:, 4:6, :]
        ps_act = m.psum[:, 6, :]
        ps_dve = m.psum[:, 7, :]
        ident = m.const[:, C_IDENT:C_IDENT + P]
        sgn = m.const[:, C_SGN:C_SGN + 1]
        w_loaded = sem("cpl_weights_loaded")
        ready = sem("cpl_constants_ready")
        in_loaded = [sem(f"cpl_inputs_loaded{s}") for s in range(2)]

        def ca(c, a):
            return 2 * c + a

        def program(eng, step):
            def one(q, last=False):
                for s, following in merged:
                    if not following:
                        step(q, s)
                    elif not last:
                        step(q.next(), s)

            for s in pro:
                step(Seq(0, 0), s)
            with eng.Fori(0, R // 2 - 1) as it:
                one(Seq(it, 0))
                one(Seq(it, 1))
            one(Seq(R // 2 - 1, 0))
            one(Seq(R // 2 - 1, 1), last=True)

        with nc.Block() as block:
            @block.sync
            def _(sp):
                for dst, src in ((w1, m.d["c1"]), (w2, m.d["c2"]), (w34, m.d["c3"]), (w4, m.d["c4"]), (g1w, m.d["g1"]),
                                 (g2w, m.d["g2"]), (g3w, m.d["g3"]), (bias, m.d["cb"])):
                    sp.dma_start(dst[:], src).then_inc(w_loaded, 16)

                def step(q, s):
                    if s[0] == "ln":
                        sp.wait_ge(g.o_done.sem, g.o_done.before(q, 4, 2))
                        sp.dma_start(x_in[:, q.s].rearrange("p a i c -> p (a i) c"),
                                     m.x3_d[bass.ds(q.n * 2 * NT, 2 * NT)].rearrange("i p c -> p i c")).then_inc(in_loaded[q.s], 16)
                    if s[0] == "oT":
                        _, a, i = s
                        sp.wait_ge(g.o_done.sem, g.o_done.done(q, 2 * a + i + 1))
                        sp.dma_start(m.out_t[bass.ds(q.n * 2 * NT + a * NT + 2 * i, 2)].rearrange("i p c -> p i c"),
                                     ot[:, a, i]).then_inc(g.store.sem, 16)

                program(sp, step)
                sp.wait_ge(g.store.sem, g.store.done(Seq(R // 2 - 1, 1), g.store.per))

            @block.gpsimd
            def _(pool):
                chain = Chain(pool, g.pool_steps, m.passed)

                def step(q, s):
                    if s[0] == "ag":
                        chain.start(q)
                        pool.wait_ge(g.moments.sem, g.moments.done(q, 2 * NT))
                        pool.wait_ge(g.xn.sem, g.xn.before(q, 2 * NT))
                        settle(pool, m.passed)
                        chain.link(pool.tensor_scalar(vtmp[:], mv[:, :, 1], EPS, None, ALU.add))
                        pool.tensor_tensor(rstd[:], vtmp[:], mhalf[:], ALU.pow).then_inc(g.rstd.sem, 1)
                        chain.end()

                pool.wait_ge(ready, 1)
                program(pool, step)

            @block.vector
            def _(dve):
                chain = Chain(dve, g.steps, m.passed)

                def step(q, s):
                    if s == ("st", 0):
                        dve.wait_ge(in_loaded[q.s], q.it * 16 + 16)
                        dve.wait_ge(g.gate.sem, g.gate.before(q, 4, 2))
                        dve.tensor_copy(cols[:, q.s], m.modT[:, 1, 6:12, bass.ds(q.n * 2, 2)]).then_inc(g.cols.sem, 1)
                    if s[0] == "st":
                        i = s[1]
                        dve.bn_stats(bst[:, i, :], x_in[:, q.s, i // NT, i % NT, :]).then_inc(g.stats.sem, 1)
                    if s[0] == "ag":
                        dve.wait_ge(g.stats.sem, g.stats.done(q, 2 * NT))
                        dve.wait_ge(g.xn.sem, g.xn.before(q, 2 * NT))
                        settle(dve, m.passed)
                        for i in range(2 * NT):
                            dve.bn_aggr(mv[:, i, :], bst[:, i, :]).then_inc(g.moments.sem, 1)
                    if s[0] == "xn":
                        i = s[1]
                        dve.wait_ge(g.rstd.sem, g.rstd.done(q, 1))
                        dve.wait_ge(g.pa_drain.sem, g.pa_drain.before(q, 7))
                        dve.tensor_scalar(xn[:, i, :], x_in[:, q.s, i // NT, i % NT, :], mv[:, i, 0:1], rstd[:, i:i + 1],
                                          ALU.subtract, ALU.mult).then_inc(g.xn.sem, 1)
                    if s[0] == "g3":
                        dve.wait_ge(g.pa_drain.sem, g.pa_drain.done(q, pa_use[s] + 1))
                        dve.tensor_scalar(coef[:, q.s, :], gs3[:], half[:, 3:4], 0.1, ALU.mult, ALU.add).then_inc(g.coef.sem, 1)
                    if s[0] == "up":
                        _, c, a = s
                        n = ca(c, a)
                        if n == 0:
                            chain.start(q)
                            dve.wait_ge(g.coef.sem, g.coef.done(q, 1))
                        chain.go_on(q)
                        dve.wait_ge(g.l4.sem, g.l4.done(q, n + 1))
                        chain.link(dve.tensor_scalar(cc[:, a, :], th[:, a, :], half[:, 2:3], coef[:, q.s, a:a + 1], ALU.mult, ALU.add))
                        st = o[:, q.s, a]
                        dve.scalar_tensor_tensor(out=uv[:, a, 0, :], in0=st[:, 1, :], scalar=sgn, in1=cc[:, a, :],
                                                 op0=ALU.mult, op1=ALU.mult)
                        chain.link(dve.scalar_tensor_tensor(out=uv[:, a, 1, :], in0=st[:, 0, :], scalar=nsgn[:, 0:1], in1=cc[:, a, :],
                                                            op0=ALU.mult, op1=ALU.mult))
                        for k in range(KC):
                            dve.tensor_tensor(st[:, k, :], st[:, k, :], uv[:, a, k, :], ALU.add).then_inc(g.state.sem, 1)
                        dve.wait_ge(g.state.sem, g.state.done(q, 2 * n + 2))
                        if n == 2 * CYCLES - 1:
                            chain.end()
                    if s[0] == "oT":
                        _, a, i = s
                        n = 2 * a + i
                        dve.wait_ge(g.o_fill.sem, g.o_fill.done(q, n + 1))
                        dve.wait_ge(g.store.sem, g.store.before(q, 16 * 4))
                        dve.tensor_tensor(ot[:, a, i].rearrange("p i c -> p (i c)"), ps_dve,
                                          x_in[:, q.s, a, 2 * i:2 * i + 2, :].rearrange("p i c -> p (i c)"),
                                          ALU.add).then_inc(g.o_done.sem, 1)

                dve.wait_ge(w_loaded, 8 * 16)
                dve.tensor_scalar(nsgn[:], sgn, -1.0, None, ALU.mult)
                dve.tensor_scalar(half[:, 0:1], bias[:, 4:5], 0.5, None, ALU.mult)
                dve.tensor_scalar(half[:, 1:2], bias[:, 7:8], 0.5, None, ALU.mult)
                dve.tensor_scalar(half[:, 2:3], bias[:, 8:9], 0.3, None, ALU.mult)
                dve.tensor_scalar(half[:, 3:4], bias[:, 8:9], 0.7, None, ALU.mult)
                dve.memset(mhalf[:], -0.5).then_inc(ready, 1)
                dve.wait_ge(ready, 1)
                program(dve, step)

            @block.scalar
            def _(act):
                def step(q, s):
                    if s[0] == "hT":
                        _, a, k = s
                        act.wait_ge(g.pa_fill.sem, g.pa_fill.done(q, pa_use[s] + 1))
                        act.wait_ge(g.cols.sem, g.cols.done(q, 1))
                        act.activation(o[:, q.s, a, k, :], ps_act, ACT.Identity, bias=cols[:, q.s, k, a:a + 1],
                                       scale=cols[:, q.s, KC + k, a:a + 1], accum_out=sums[:, k, a:a + 1]).then_inc(g.pa_drain.sem, 1)
                    if s[0] == "g1":
                        act.wait_ge(g.pa_fill.sem, g.pa_fill.done(q, pa_use[s] + 1))
                        act.activation(gs1[:], ps_act[:, 0:2], ACT.Gelu, bias=bias[:, 5:6], scale=1.0 / T).then_inc(g.pa_drain.sem, 1)
                    if s[0] == "g2":
                        act.wait_ge(g.pa_fill.sem, g.pa_fill.done(q, pa_use[s] + 1))
                        act.activation(gs2[:], ps_act[0:64, 0:2], ACT.Gelu, bias=bias[0:64, 6:7]).then_inc(g.pa_drain.sem, 1)
                    if s[0] == "g3":
                        act.wait_ge(g.pa_fill.sem, g.pa_fill.done(q, pa_use[s] + 1))
                        act.wait_ge(g.coef.sem, g.coef.before(q, 1))
                        act.activation(gs3[:], ps_act[:, 0:2], ACT.Tanh, bias=half[:, 1:2], scale=0.5).then_inc(g.pa_drain.sem, 1)
                    if s[0] == "L1":
                        _, c, a, u = s
                        n, k = ca(c, a), u // 2
                        if u % 2:
                            act.wait_ge(g.l1_fill.sem, g.l1_fill.done(q, 2 * n + k + 1))
                            act.activation(a1[:, a, k, :], ps_1[:, a, k, :], ACT.Gelu, bias=bias[:, k:k + 1]).then_inc(g.l1.sem, 1)
                    if s[0] == "L2":
                        _, c, a = s
                        act.wait_ge(g.l2_fill.sem, g.l2_fill.done(q, ca(c, a) + 1))
                        act.activation(a2[:, a, :], ps_2[:, a, :], ACT.Gelu, bias=bias[:, 2:3]).then_inc(g.l2.sem, 1)
                    if s[0] == "L3":
                        _, c, a = s
                        act.wait_ge(g.l3_fill.sem, g.l3_fill.done(q, ca(c, a) + 1))
                        act.activation(a3[:, a, :], ps_2[0:64, a, :], ACT.Gelu, bias=bias[0:64, 3:4]).then_inc(g.l3.sem, 1)
                    if s[0] == "L4":
                        _, c, a = s
                        act.wait_ge(g.l4_fill.sem, g.l4_fill.done(q, ca(c, a) + 1))
                        act.activation(th[:, a, :], ps_2[:, a, :], ACT.Tanh, bias=half[:, 0:1], scale=0.5).then_inc(g.l4.sem, 1)
                    if s[0] == "gate":
                        a = s[1]
                        act.wait_ge(g.state.sem, g.state.done(q, 2 * ca(CYCLES - 1, a) + 2))
                        act.wait_ge(g.o_fill.sem, g.o_fill.before(q, 4))
                        for k in range(KC):
                            act.activation(og[:, a, k, :], o[:, q.s, a, k, :], ACT.Copy,
                                           scale=cols[:, q.s, 2 * KC + k, a:a + 1]).then_inc(g.gate.sem, 1)

                act.wait_ge(ready, 1)
                program(act, step)

            @block.tensor
            def _(pe):
                def step(q, s):
                    if s[0] in ("hT", "g1", "g2", "g3"):
                        n = pa_use[s]
                        pe.wait_ge(g.pa_drain.sem, g.pa_drain.done(q, n) if n else g.pa_drain.before(q, 7))
                    if s[0] == "hT":
                        _, a, k = s
                        pe.wait_ge(g.xn.sem, g.xn.done(q, NT * (a + 1)))
                        for i in range(NT):
                            last = pe.transpose(ps_act[:, i * P:(i + 1) * P], xn[:, a * NT + i, k * P:(k + 1) * P], ident)
                        last.then_inc(g.pa_fill.sem, 1)
                    if s[0] == "g1":
                        for k in range(KC):
                            last = pe.matmul(ps_act[:, 0:2], g1w[:, k, :], sums[:, k, :], start=k == 0, stop=k == KC - 1)
                        last.then_inc(g.pa_fill.sem, 1)
                    if s[0] == "g2":
                        pe.matmul(ps_act[0:64, 0:2], g2w[:], gs1[:], start=True, stop=True).then_inc(g.pa_fill.sem, 1)
                    if s[0] == "g3":
                        pe.matmul(ps_act[:, 0:2], g3w[:], gs2[:], start=True, stop=True).then_inc(g.pa_fill.sem, 1)
                    if s[0] == "L1":
                        _, c, a, u = s
                        n, h, k = ca(c, a), u // 2, u % 2
                        if u == 0:
                            if c:
                                pe.wait_ge(g.state.sem, g.state.done(q, 2 * ca(c - 1, a) + 1))
                                pe.wait_ge(g.l1.sem, g.l1.done(q, 2 * ca(c - 1, a) + 2))
                            else:
                                pe.wait_ge(g.pa_drain.sem, g.pa_drain.done(q, pa_use[("hT", a, 1)] + 1))
                                pe.wait_ge(g.l1.sem, g.l1.before(q, 2 * ca(CYCLES - 1, a) + 2))
                        if u == 1 and c:
                            pe.wait_ge(g.state.sem, g.state.done(q, 2 * ca(c - 1, a) + 2))
                        ins = pe.matmul(ps_1[:, a, h, :], w1[:, k, h * P:(h + 1) * P], o[:, q.s, a, k, :],
                                        start=k == 0, stop=k == KC - 1)
                        if k == KC - 1:
                            ins.then_inc(g.l1_fill.sem, 1)
                    if s[0] == "L2":
                        _, c, a = s
                        n = ca(c, a)
                        pe.wait_ge(g.l4.sem, g.l4.done(q, n - 1) if c else g.l4.before(q, ca(CYCLES - 1, a) + 1))
                        for k in range(KC):
                            pe.wait_ge(g.l1.sem, g.l1.done(q, 2 * n + k + 1))
                            last = pe.matmul(ps_2[:, a, :], w2[:, k, :], a1[:, a, k, :], start=k == 0, stop=k == KC - 1)
                        last.then_inc(g.l2_fill.sem, 1)
                    if s[0] == "L3":
                        _, c, a = s
                        pe.wait_ge(g.l2.sem, g.l2.done(q, ca(c, a) + 1))
                        pe.matmul(ps_2[0:64, a, :], w34[:], a2[:, a, :], start=True, stop=True).then_inc(g.l3_fill.sem, 1)
                    if s[0] == "L4":
                        _, c, a = s
                        pe.wait_ge(g.l3.sem, g.l3.done(q, ca(c, a) + 1))
                        pe.matmul(ps_2[:, a, :], w4[:], a3[:, a, :], start=True, stop=True).then_inc(g.l4_fill.sem, 1)
                    if s[0] == "oT":
                        _, a, i = s
                        n = 2 * a + i
                        pe.wait_ge(g.gate.sem, g.gate.done(q, 2 * a + 2))
                        pe.wait_ge(g.o_done.sem, g.o_done.done(q, n) if n else g.o_done.before(q, 4))
                        for t in range(2):
                            for k in range(KC):
                                last = pe.transpose(ps_dve[:, (2 * t + k) * P:(2 * t + k + 1) * P],
                                                    og[:, a, k, (2 * i + t) * P:(2 * i + t + 1) * P], ident)
                        last.then_inc(g.o_fill.sem, 1)

                pe.wait_ge(ready, 1)
                program(pe, step)


INPUTS = {
    "const": (P, C_END), "x": (B * NT, P, C), "cT": (P, 2, KC, B), "wmod": (P, 2, KC, 6 * C),
    "wqkv": (P, KC, C + 2 * HD), "bqkv": (P, C + 2 * HD), "wo": (P, KC, C), "bo": (P, C),
    "wg": (P, KC, E), "bg": (E, 1), "eb": (P, E, 3), "ew": (E, P, 3 * KC * C),
    "lw": (P, KC, 3 * C), "lwo": (P, KC, C), "lbo": (P, C), "lbv": (P, C), "lbqk": (P, 4),
    "c1": (P, KC, C), "c2": (P, KC, P), "c3": (P, 64), "c4": (64, P),
    "g1": (P, KC, P), "g2": (P, 64), "g3": (64, P), "cb": (P, 9),
}


class Shared:
    pass


def build(nc, d, out):
    m = Shared()
    m.d, m.primed = d, []
    with ExitStack() as ctx:
        def new(name, per):
            signal = Signal(ctx.enter_context(nc.semaphore(name)), per)
            m.primed.append(signal)
            return signal

        def sb(name, shape, dt=F32):
            return ctx.enter_context(nc.sbuf_tensor(name, shape, dt))

        def dram(name, shape):
            return nc.dram_tensor(name, shape, F32, kind="Internal").ap()

        m.passed = ctx.enter_context(nc.semaphore("waits_passed"))
        m.att = AttentionSignals(new)
        m.exp = ExpertSignals(new)
        m.lin = LinearSignals(new)
        m.cpl = CouplingSignals(new)
        m.out_t = out.rearrange("b (i p) c -> (b i) p c", p=P)
        m.const = sb("const_sb", [P, C_END])
        m.ident_bf = sb("ident_bf", [P, P], BF16)
        m.negs_bf = sb("negs_bf", [P, P], BF16)
        m.negt_bf = sb("negt_bf", [P, P], BF16)
        m.modT = sb("modT", [P, 2, 12, B])
        m.psum = ctx.enter_context(nc.psum_tensor("psum", [P, 8, 512], F32))
        m.mod_rows = dram("mod_rows", (B, ROWS * C))
        m.x1_d = dram("residual", (B * NT, P, C))
        m.h2_d = dram("router_input", (B * NT, P, C))
        m.lg_d = dram("router_logits", (B, E, T))
        m.x3_d = dram("x3_dram", (B * NT, P, C))
        with ExitStack() as inner:
            m.k6T = inner.enter_context(nc.sbuf_tensor("k6T", [6 * HD + 3, 2, T], BF16))
            m.v32 = inner.enter_context(nc.sbuf_tensor("v32", [P, 2, NT, 32], F32))
            m.mhalf = inner.enter_context(nc.sbuf_tensor("mhalf", [P, NT], F32))
            m.x_in = inner.enter_context(nc.sbuf_tensor("x_in", [P, 2, NT, C], F32))
            m.in_loaded = [inner.enter_context(nc.semaphore(f"att_inputs_loaded{s}")) for s in range(2)]
            m.att_w_loaded = inner.enter_context(nc.semaphore("att_weights_loaded"))
            m.att_weights = [(inner.enter_context(nc.sbuf_tensor(f"{name}_sb", shape, F32)), d[name]) for name, shape in (
                ("wqkv", [P, KC, C + 2 * HD]), ("wo", [P, KC, C]), ("wg", [P, KC, E]),
                ("bqkv", [P, C + 2 * HD]), ("bo", [P, C]), ("bg", [E, 1]))]
            setup_phase(nc, m)
            attention_phase(nc, m)
        with ExitStack() as inner:
            m.idx_e = inner.enter_context(nc.sbuf_tensor("idx_e", [P, E, 4], U32))
            m.par_e = inner.enter_context(nc.sbuf_tensor("par_e", [P, E, 11], F32))
            m.gb_rows = inner.enter_context(nc.sbuf_tensor("gb_rows", [P, 4, C], F32))
            routing_phase(nc, m)
            expert_phase(nc, m)
        linear_phase(nc, m)
        coupling_phase(nc, m)


def halves(w):
    return w.reshape(KC, P, -1).transpose(1, 0, 2)


def pack(i):
    def rows(v, n=P):
        return np.broadcast_to(np.asarray(v).reshape(1, -1), (n, np.asarray(v).size))

    def columns(*vectors):
        c = np.zeros((P, len(vectors)), np.float32)
        for n, v in enumerate(vectors):
            c[:v.size if v.size > 1 else P, n] = v
        return c

    i = {k: np.asarray(v) for k, v in i.items()}
    return {
        "const": shape_constants(),
        "x": i["L0_attn_x"].reshape(B * NT, P, C),
        "cT": np.stack([i[f"L{n}_c"].T.reshape(KC, P, B) for n in range(2)]).transpose(2, 0, 1, 3),
        "wmod": np.stack([halves(i[f"L{n}_wmod"]) for n in range(2)], axis=1),
        "wqkv": halves(np.concatenate([i["L0_attn_Wq"], i["L0_attn_Wk"], i["L0_attn_Wv"]], axis=1)),
        "bqkv": rows(np.concatenate([i["L0_attn_bq"], i["L0_attn_bk"], i["L0_attn_bv"]])),
        "wo": halves(i["L0_attn_Wo"]), "bo": rows(i["L0_attn_bo"]),
        "wg": halves(i["L0_ffn_Wg"]), "bg": i["L0_ffn_bg"].reshape(E, 1),
        "eb": np.broadcast_to(np.stack([i[f"L0_ffn_b{n}"][:, 0] for n in (1, 2, 3)], axis=1)[None], (P, E, 3)),
        "ew": np.stack([i[f"L0_ffn_w{n}"].reshape(E, KC, P, C).transpose(0, 2, 1, 3) for n in (1, 2, 3)],
                       axis=2).reshape(E, P, 3 * KC * C),
        "lw": halves(i["L1_attn_qkv_w"]), "lwo": halves(i["L1_attn_out_w"]), "lbo": rows(i["L1_attn_out_b"]),
        "lbv": rows(i["L1_attn_qkv_b"][2 * C:]), "lbqk": i["L1_attn_qkv_b"][:2 * C].reshape(4, P).T,
        "c1": halves(i["L1_ffn_cn_w1"]), "c2": halves(i["L1_ffn_cn_w2"]), "c3": i["L1_ffn_cn_w3"],
        "c4": np.broadcast_to(i["L1_ffn_cn_w4"], (64, P)),
        "g1": halves(i["L1_ffn_gc_w1"]), "g2": i["L1_ffn_gc_w2"], "g3": np.broadcast_to(i["L1_ffn_gc_w3"], (64, P)),
        "cb": columns(i["L1_ffn_cn_b1"][:P], i["L1_ffn_cn_b1"][P:], i["L1_ffn_cn_b2"], i["L1_ffn_cn_b3"],
                      i["L1_ffn_cn_b4"], i["L1_ffn_gc_b1"], i["L1_ffn_gc_b2"], i["L1_ffn_gc_b3"],
                      i["L1_ffn_adaptive_range"]),
    }


def kernel(**inputs):
    import concourse.bacc as bacc
    from concourse.bass_utils import run_bass_kernel_spmd

    nc = bacc.Bacc("TRN2", target_bir_lowering=False, num_devices=1)
    arrays, d = {}, {}
    for name, a in pack(inputs).items():
        assert a.shape == INPUTS[name], (name, a.shape)
        arrays[f"in_{name}"] = np.ascontiguousarray(a, dtype=np.float32)
        d[name] = nc.dram_tensor(f"in_{name}", a.shape, F32, kind="ExternalInput").ap()
    out = nc.dram_tensor("out_0", (B, T, C), F32, kind="ExternalOutput").ap()
    build(nc, d, out)
    r = run_bass_kernel_spmd(nc, [arrays], core_ids=[0])
    return r.results[0]["out_0"]
```
